# Optimizing a Trainium2 kernel written in Bass

```python
import numpy as np
import jax
import jax.numpy as jnp

def _softmax(x, axis=-1):
    return jax.nn.softmax(x, axis=axis)

def _gelu(x):
    return jax.nn.gelu(x, approximate=True)

def _silu(x):
    return jax.nn.silu(x)

def _sigmoid(x):
    return jax.nn.sigmoid(x)

def _layernorm(x, axis=-1, eps=1e-05):
    m = jnp.mean(x, axis=axis, keepdims=True)
    v = jnp.var(x, axis=axis, keepdims=True)
    return (x - m) / jnp.sqrt(v + eps)

def _scatter_add(tgt, idx, src, axis=0):
    return tgt.at[idx].add(src)

def _segment_sum(src, seg, n):
    return jax.ops.segment_sum(src, seg, n)
kernel_name = 'mk_decoder_postln_d2_seqx_r4_f63abd'

def setup_inputs(seed: int=0):
    np.random.seed(seed)
    _w = jnp.asarray

    def _rec_inputs():
        import jax
        import jax.numpy as jnp
        _rk = jax.random.key(seed)
        x = 7.22e-05 + 1 * jax.random.normal(jax.random.fold_in(_rk, 1), (8, 256, 256), jnp.float32)
        _lenS = 256 - jax.random.randint(jax.random.fold_in(_rk, 7), (8,), 0, max(1, 256 // 4) + 1, jnp.int32)
        _lenS2 = 77 - jax.random.randint(jax.random.fold_in(_rk, 8), (8,), 0, max(1, 77 // 4) + 1, jnp.int32)
        _ctx_1024P = jax.random.normal(jax.random.fold_in(_rk, 11), (8, 16, 256), jnp.float32)
        _ctx_1024c = jax.random.dirichlet(jax.random.fold_in(_rk, 511), 0.3 * jnp.ones((16,), jnp.float32), (8, 77))
        _ctx_1024t = jnp.einsum('bsk,bkd->bsd', _ctx_1024c, _ctx_1024P)
        _ctx_1024t = _ctx_1024t * jax.lax.rsqrt(jnp.mean(jnp.square(_ctx_1024t)) + 1e-12) * 0.953939
        ctx_1024 = 4.13588e-05 + 0.999923 * (_ctx_1024t + 0.3 * jax.random.normal(jax.random.fold_in(_rk, 611), (8, 77, 256), jnp.float32))
        _validS = jnp.arange(256)[None, :] < _lenS[:, None]
        _validS2 = jnp.arange(77)[None, :] < _lenS2[:, None]
        _causal = jnp.tril(jnp.ones((256, 256), dtype=bool))
        mask_BxSxS2_ik0 = jnp.where(jnp.broadcast_to(_validS2[:, None, :], (8, 256, 77)), 0, 1).astype(jnp.int32)
        mask_Bx1xSxS2_ff0 = jnp.where(jnp.ones((8, 1, 256, 77), dtype=bool), 0.0, -1000000000.0).astype(jnp.float32)
        return (x, ctx_1024, mask_BxSxS2_ik0, mask_Bx1xSxS2_ff0)
    x, ctx_1024, mask_BxSxS2_ik0, mask_Bx1xSxS2_ff0 = _rec_inputs()

    def _L0_attn_setup():
        import jax, jax.numpy as jnp
        import numpy as np
        B, T, D_MODEL = (2, 512, 256)
        N_HEADS, HEAD_DIM = (16, 64)
        ROPE_BASE = 10000.0

        def rotate_half(x):
            half = x.shape[-1] // 2
            x1, x2 = (x[..., :half], x[..., half:])
            return jnp.concatenate([-x2, x1], axis=-1)
        key = jax.random.key(seed)
        ks = jax.random.split(key, 5)
        scale = 0.02
        return {'x': jax.random.normal(ks[0], (B, T, D_MODEL), dtype=jnp.float32), 'Wq': jax.random.normal(ks[1], (D_MODEL, N_HEADS * HEAD_DIM), dtype=jnp.float32) * scale, 'Wk': jax.random.normal(ks[2], (D_MODEL, N_HEADS * HEAD_DIM), dtype=jnp.float32) * scale, 'Wv': jax.random.normal(ks[3], (D_MODEL, N_HEADS * HEAD_DIM), dtype=jnp.float32) * scale, 'Wo': jax.random.normal(ks[4], (N_HEADS * HEAD_DIM, D_MODEL), dtype=jnp.float32) * scale}
    _L0_attn_all = _L0_attn_setup()
    _L0_attn_in = {k: v for k, v in _L0_attn_all.items() if k in ('Wq', 'Wk', 'Wv', 'Wo')}
    del _L0_attn_all

    def _L0_xattn_setup():
        import jax, jax.numpy as jnp
        import numpy as np
        D_MODEL = 256
        H = 16
        D_K = D_MODEL // H
        B, S = (4, 512)
        NEG = -1000000000.0
        key = jax.random.key(seed)
        ks = jax.random.split(key, 12)
        scale = 1.0 / np.sqrt(D_MODEL)
        inp = {'query': jax.random.normal(ks[0], (B, S, D_MODEL), jnp.float32), 'key': jax.random.normal(ks[1], (B, S, D_MODEL), jnp.float32), 'value': jax.random.normal(ks[2], (B, S, D_MODEL), jnp.float32), 'mask': jnp.broadcast_to(jnp.tril(jnp.ones((S, S), jnp.int32)), (B, S, S)), 'Wq': jax.random.normal(ks[3], (D_MODEL, D_MODEL), jnp.float32) * scale, 'bq': jnp.zeros((D_MODEL,), jnp.float32), 'Wk': jax.random.normal(ks[4], (D_MODEL, D_MODEL), jnp.float32) * scale, 'bk': jnp.zeros((D_MODEL,), jnp.float32), 'Wv': jax.random.normal(ks[5], (D_MODEL, D_MODEL), jnp.float32) * scale, 'bv': jnp.zeros((D_MODEL,), jnp.float32), 'Wo': jax.random.normal(ks[6], (D_MODEL, D_MODEL), jnp.float32) * scale, 'bo': jnp.zeros((D_MODEL,), jnp.float32)}
        return inp
    _L0_xattn_all = _L0_xattn_setup()
    _L0_xattn_in = {k: v for k, v in _L0_xattn_all.items() if k in ('Wq', 'bq', 'Wk', 'bk', 'Wv', 'bv', 'Wo', 'bo')}
    del _L0_xattn_all

    def _L0_ffn_setup():
        import math
        import jax, jax.numpy as jnp
        import numpy as np
        D_MODEL = 256
        D_FF = 1024
        N_EXPERTS = 8
        CAPACITY_FACTOR = 1.25
        L, B = (128, 8)

        def _route(tokens, router_w):
            T = tokens.shape[0]
            E = router_w.shape[0]
            capacity = int(math.ceil(T / E * CAPACITY_FACTOR))
            logits = tokens @ router_w.T
            probs = jax.nn.softmax(logits, axis=-1)
            top1_idx = jnp.argmax(probs, axis=-1)
            top1_prob = jnp.max(probs, axis=-1)
            order = jnp.lexsort((-top1_prob, top1_idx))
            sorted_e = top1_idx[order]
            counts = jnp.bincount(top1_idx, length=E)
            start = jnp.cumsum(counts) - counts
            pos_in_group = jnp.arange(T) - start[sorted_e]
            keep_sorted = pos_in_group < capacity
            keep = jnp.zeros((T,), bool).at[order].set(keep_sorted)
            return jnp.where(keep, top1_idx, 0).astype(jnp.int32)
        key = jax.random.key(seed)
        ks = jax.random.split(key, 6)
        s_in = 1.0 / math.sqrt(D_MODEL)
        s_ff = 1.0 / math.sqrt(D_FF)
        return {'x': jax.random.normal(ks[0], (L, B, D_MODEL), dtype=jnp.float32), 'router_w': jax.random.uniform(ks[1], (N_EXPERTS, D_MODEL), minval=-s_in, maxval=s_in), 'W1': jax.random.uniform(ks[2], (N_EXPERTS, D_MODEL, D_FF), minval=-s_in, maxval=s_in), 'b1': jax.random.uniform(ks[3], (N_EXPERTS, D_FF), minval=-s_in, maxval=s_in), 'W2': jax.random.uniform(ks[4], (N_EXPERTS, D_FF, D_MODEL), minval=-s_ff, maxval=s_ff), 'b2': jax.random.uniform(ks[5], (N_EXPERTS, D_MODEL), minval=-s_ff, maxval=s_ff)}
    _L0_ffn_all = _L0_ffn_setup()
    _L0_ffn_in = {k: v for k, v in _L0_ffn_all.items() if k in ('router_w', 'W1', 'b1', 'W2', 'b2')}
    del _L0_ffn_all

    def _L1_attn_setup():
        import jax, jax.numpy as jnp
        from jax import lax
        import numpy as np
        DIM = 256
        HID = 512
        K = 4
        B = 4
        T = 512
        ALPHA_LOG_SCALE = -8.0

        def init_forget_gate(size, a=0.001, b=0.1, lo=-9.0, hi=-4.323):
            x = np.log(np.expm1(np.linspace(a, b, size, dtype=np.float64)))
            x = (x - x.min()) / (x.max() - x.min())
            x = x * abs(hi - lo) + lo
            return jnp.asarray(x, dtype=jnp.float32)

        def _scan_combine(c1, c2):
            a1, b1 = c1
            a2, b2 = c2
            return (a1 * a2, a2 * b1 + b2)
        key = jax.random.key(seed)
        ks = jax.random.split(key, 7)
        x = jax.random.normal(ks[0], (B, T, DIM), dtype=jnp.float32)
        W_in = jax.random.normal(ks[1], (2 * HID, DIM), dtype=jnp.float32) * DIM ** (-0.5)
        s = 1.0 / np.sqrt(K)
        conv_w = jax.random.uniform(ks[2], (HID, 1, K), jnp.float32, -s, s)
        conv_b = jax.random.uniform(ks[3], (HID,), jnp.float32, -s, s)
        W_g = jax.random.normal(ks[4], (2 * HID, HID), dtype=jnp.float32) * HID ** (-0.5)
        sg = 1.0 / np.sqrt(HID)
        b_g = jax.random.uniform(ks[5], (2 * HID,), jnp.float32, -sg, sg)
        forget_base = init_forget_gate(HID)
        W_out = jax.random.normal(ks[6], (DIM, HID), dtype=jnp.float32) * HID ** (-0.5)
        return {'x': x, 'W_in': W_in, 'conv_w': conv_w, 'conv_b': conv_b, 'W_g': W_g, 'b_g': b_g, 'forget_base': forget_base, 'W_out': W_out}
    _L1_attn_all = _L1_attn_setup()
    _L1_attn_in = {k: v for k, v in _L1_attn_all.items() if k in ('W_in', 'conv_w', 'conv_b', 'W_g', 'b_g', 'forget_base', 'W_out')}
    del _L1_attn_all

    def _L1_xattn_setup():
        import jax, jax.numpy as jnp
        import numpy as np
        D_MODEL = 256
        NUM_HEADS = 16
        HEAD_DIM = D_MODEL // NUM_HEADS
        B, S = (4, 512)

        def _split(x):
            b, s, _ = x.shape
            return x.reshape(b, s, NUM_HEADS, HEAD_DIM).transpose(0, 2, 1, 3)
        key = jax.random.key(seed)
        ks = jax.random.split(key, 12)
        std = 1.0 / np.sqrt(D_MODEL)
        inp = {'q': jax.random.normal(ks[0], (B, S, D_MODEL), jnp.float32), 'k': jax.random.normal(ks[1], (B, S, D_MODEL), jnp.float32), 'v': jax.random.normal(ks[2], (B, S, D_MODEL), jnp.float32), 'mask': jnp.zeros((B, 1, S, S), jnp.float32), 'w_q': jax.random.normal(ks[3], (D_MODEL, D_MODEL), jnp.float32) * std, 'b_q': jax.random.normal(ks[4], (D_MODEL,), jnp.float32) * std, 'w_k': jax.random.normal(ks[5], (D_MODEL, D_MODEL), jnp.float32) * std, 'b_k': jax.random.normal(ks[6], (D_MODEL,), jnp.float32) * std, 'w_v': jax.random.normal(ks[7], (D_MODEL, D_MODEL), jnp.float32) * std, 'b_v': jax.random.normal(ks[8], (D_MODEL,), jnp.float32) * std, 'w_o': jax.random.normal(ks[9], (D_MODEL, D_MODEL), jnp.float32) * std, 'b_o': jax.random.normal(ks[10], (D_MODEL,), jnp.float32) * std}
        return inp
    _L1_xattn_all = _L1_xattn_setup()
    _L1_xattn_in = {k: v for k, v in _L1_xattn_all.items() if k in ('w_q', 'b_q', 'w_k', 'b_k', 'w_v', 'b_v', 'w_o', 'b_o')}
    del _L1_xattn_all

    def _L1_ffn_setup():
        import jax, jax.numpy as jnp
        import numpy as np

        def _binarize(w):
            alpha = jax.lax.stop_gradient(jnp.mean(jnp.abs(w), axis=1, keepdims=True))
            bw = alpha * jnp.sign(w)
            return w + jax.lax.stop_gradient(bw - w)
        key = jax.random.key(seed)
        k1, k2, k3, k4, k5 = jax.random.split(key, 5)
        D, H = (256, 1024)
        x = jax.random.normal(k1, (64, 196, D), dtype=jnp.float32)
        w1 = jax.random.normal(k2, (H, D), dtype=jnp.float32) * 0.02
        b1 = jax.random.normal(k3, (H,), dtype=jnp.float32) * 0.02
        w2 = jax.random.normal(k4, (D, H), dtype=jnp.float32) * 0.02
        b2 = jax.random.normal(k5, (D,), dtype=jnp.float32) * 0.02
        return {'x': x, 'w1': w1, 'b1': b1, 'w2': w2, 'b2': b2}
    _L1_ffn_all = _L1_ffn_setup()
    _L1_ffn_in = {k: v for k, v in _L1_ffn_all.items() if k in ('w1', 'b1', 'w2', 'b2')}
    del _L1_ffn_all
    return {'x': x, 'ctx_1024': ctx_1024, 'mask_BxSxS2_ik0': mask_BxSxS2_ik0, 'mask_Bx1xSxS2_ff0': mask_Bx1xSxS2_ff0, 'L0_attn_Wq': _L0_attn_in['Wq'], 'L0_attn_Wk': _L0_attn_in['Wk'], 'L0_attn_Wv': _L0_attn_in['Wv'], 'L0_attn_Wo': _L0_attn_in['Wo'], 'L0_xattn_Wq': _L0_xattn_in['Wq'], 'L0_xattn_bq': _L0_xattn_in['bq'], 'L0_xattn_Wk': _L0_xattn_in['Wk'], 'L0_xattn_bk': _L0_xattn_in['bk'], 'L0_xattn_Wv': _L0_xattn_in['Wv'], 'L0_xattn_bv': _L0_xattn_in['bv'], 'L0_xattn_Wo': _L0_xattn_in['Wo'], 'L0_xattn_bo': _L0_xattn_in['bo'], 'L0_ffn_router_w': _L0_ffn_in['router_w'], 'L0_ffn_W1': _L0_ffn_in['W1'], 'L0_ffn_b1': _L0_ffn_in['b1'], 'L0_ffn_W2': _L0_ffn_in['W2'], 'L0_ffn_b2': _L0_ffn_in['b2'], 'L1_attn_W_in': _L1_attn_in['W_in'], 'L1_attn_conv_w': _L1_attn_in['conv_w'], 'L1_attn_conv_b': _L1_attn_in['conv_b'], 'L1_attn_W_g': _L1_attn_in['W_g'], 'L1_attn_b_g': _L1_attn_in['b_g'], 'L1_attn_forget_base': _L1_attn_in['forget_base'], 'L1_attn_W_out': _L1_attn_in['W_out'], 'L1_xattn_w_q': _L1_xattn_in['w_q'], 'L1_xattn_b_q': _L1_xattn_in['b_q'], 'L1_xattn_w_k': _L1_xattn_in['w_k'], 'L1_xattn_b_k': _L1_xattn_in['b_k'], 'L1_xattn_w_v': _L1_xattn_in['w_v'], 'L1_xattn_b_v': _L1_xattn_in['b_v'], 'L1_xattn_w_o': _L1_xattn_in['w_o'], 'L1_xattn_b_o': _L1_xattn_in['b_o'], 'L1_ffn_w1': _L1_ffn_in['w1'], 'L1_ffn_b1': _L1_ffn_in['b1'], 'L1_ffn_w2': _L1_ffn_in['w2'], 'L1_ffn_b2': _L1_ffn_in['b2']}

def reference(x, ctx_1024, mask_BxSxS2_ik0, mask_Bx1xSxS2_ff0, L0_attn_Wq, L0_attn_Wk, L0_attn_Wv, L0_attn_Wo, L0_xattn_Wq, L0_xattn_bq, L0_xattn_Wk, L0_xattn_bk, L0_xattn_Wv, L0_xattn_bv, L0_xattn_Wo, L0_xattn_bo, L0_ffn_router_w, L0_ffn_W1, L0_ffn_b1, L0_ffn_W2, L0_ffn_b2, L1_attn_W_in, L1_attn_conv_w, L1_attn_conv_b, L1_attn_W_g, L1_attn_b_g, L1_attn_forget_base, L1_attn_W_out, L1_xattn_w_q, L1_xattn_b_q, L1_xattn_w_k, L1_xattn_b_k, L1_xattn_w_v, L1_xattn_b_v, L1_xattn_w_o, L1_xattn_b_o, L1_ffn_w1, L1_ffn_b1, L1_ffn_w2, L1_ffn_b2):
    import jax
    import jax.numpy as jnp

    def _L0_attn_ref(x, Wq, Wk, Wv, Wo):
        import jax, jax.numpy as jnp
        import numpy as np
        B, T, D_MODEL = (2, 512, 256)
        N_HEADS, HEAD_DIM = (16, 64)
        ROPE_BASE = 10000.0

        def rotate_half(x):
            half = x.shape[-1] // 2
            x1, x2 = (x[..., :half], x[..., half:])
            return jnp.concatenate([-x2, x1], axis=-1)
        Bx, Tx, C = x.shape
        H, D = (N_HEADS, HEAD_DIM)
        Q = (x @ Wq).reshape(Bx, Tx, H, D).transpose(0, 2, 1, 3)
        K = (x @ Wk).reshape(Bx, Tx, H, D).transpose(0, 2, 1, 3)
        V = (x @ Wv).reshape(Bx, Tx, H, D).transpose(0, 2, 1, 3)
        t = jnp.arange(Tx, dtype=jnp.float32)
        inv_freq = 1.0 / ROPE_BASE ** (jnp.arange(0, D, 2, dtype=jnp.float32) / D)
        f = t[:, None] * inv_freq[None, :]
        freqs = jnp.concatenate([f, f], axis=-1)
        cos, sin = (jnp.cos(freqs), jnp.sin(freqs))
        Q = Q * cos + rotate_half(Q) * sin
        K = K * cos + rotate_half(K) * sin
        scores = jnp.einsum('bhqd,bhkd->bhqk', Q, K) / jnp.sqrt(jnp.float32(D))
        w = Tx // 4
        idx = jnp.arange(Tx)
        allowed = jnp.abs(idx[:, None] - idx[None, :]) <= w
        scores = jnp.where(allowed[None, None], scores, -jnp.inf)
        attn = jax.nn.softmax(scores, axis=-1)
        out = jnp.einsum('bhqk,bhkd->bhqd', attn, V)
        out = out.transpose(0, 2, 1, 3).reshape(Bx, Tx, H * D)
        return out @ Wo

    def _L0_xattn_ref(query, key, value, mask, Wq, bq, Wk, bk, Wv, bv, Wo, bo):
        import jax, jax.numpy as jnp
        import numpy as np
        D_MODEL = 256
        H = 16
        D_K = D_MODEL // H
        B, S = (4, 512)
        NEG = -1000000000.0
        b, s, _ = query.shape

        def proj(x, W, bias):
            return (x @ W.T + bias).reshape(b, -1, H, D_K).transpose(0, 2, 1, 3)
        Q = proj(query, Wq, bq)
        K = proj(key, Wk, bk)
        V = proj(value, Wv, bv)
        scores = jnp.einsum('bhqd,bhkd->bhqk', Q, K) / np.sqrt(D_K)
        m = mask[:, None, :, :]
        scores = jnp.where(m == 0, NEG, scores)
        attn = jax.nn.softmax(scores, axis=-1)
        x = jnp.einsum('bhqk,bhkd->bhqd', attn, V)
        x = x.transpose(0, 2, 1, 3).reshape(b, -1, D_MODEL)
        return x @ Wo.T + bo

    def _L0_ffn_ref(x, router_w, W1, b1, W2, b2):
        import math
        import jax, jax.numpy as jnp
        import numpy as np
        D_MODEL = 256
        D_FF = 1024
        N_EXPERTS = 8
        CAPACITY_FACTOR = 1.25
        L, B = (128, 8)

        def _route(tokens, router_w):
            T = tokens.shape[0]
            E = router_w.shape[0]
            capacity = int(math.ceil(T / E * CAPACITY_FACTOR))
            logits = tokens @ router_w.T
            probs = jax.nn.softmax(logits, axis=-1)
            top1_idx = jnp.argmax(probs, axis=-1)
            top1_prob = jnp.max(probs, axis=-1)
            order = jnp.lexsort((-top1_prob, top1_idx))
            sorted_e = top1_idx[order]
            counts = jnp.bincount(top1_idx, length=E)
            start = jnp.cumsum(counts) - counts
            pos_in_group = jnp.arange(T) - start[sorted_e]
            keep_sorted = pos_in_group < capacity
            keep = jnp.zeros((T,), bool).at[order].set(keep_sorted)
            return jnp.where(keep, top1_idx, 0).astype(jnp.int32)
        Lx, Bx, D = x.shape
        T = Lx * Bx
        E = router_w.shape[0]
        tokens = x.reshape(T, D)
        final_e = _route(tokens, router_w)
        out = jnp.zeros_like(tokens)
        for e in range(E):
            h = jax.nn.relu(tokens @ W1[e] + b1[e])
            y = h @ W2[e] + b2[e]
            out = out + jnp.where((final_e == e)[:, None], y, 0.0)
        return out.reshape(Lx, Bx, D)

    def _L1_attn_ref(x, W_in, conv_w, conv_b, W_g, b_g, forget_base, W_out):
        import jax, jax.numpy as jnp
        from jax import lax
        import numpy as np
        DIM = 256
        HID = 512
        K = 4
        B = 4
        T = 512
        ALPHA_LOG_SCALE = -8.0

        def init_forget_gate(size, a=0.001, b=0.1, lo=-9.0, hi=-4.323):
            x = np.log(np.expm1(np.linspace(a, b, size, dtype=np.float64)))
            x = (x - x.min()) / (x.max() - x.min())
            x = x * abs(hi - lo) + lo
            return jnp.asarray(x, dtype=jnp.float32)

        def _scan_combine(c1, c2):
            a1, b1 = c1
            a2, b2 = c2
            return (a1 * a2, a2 * b1 + b2)
        gi = jnp.einsum('btd,hd->bth', x, W_in)
        gate, xc = jnp.split(gi, 2, axis=-1)
        xt = jnp.transpose(xc, (0, 2, 1))
        xt = jnp.pad(xt, ((0, 0), (0, 0), (K - 1, 0)))
        y = lax.conv_general_dilated(xt, conv_w, window_strides=(1,), padding='VALID', dimension_numbers=('NCH', 'OIH', 'NCH'), feature_group_count=HID)
        y = y + conv_b[None, :, None]
        xc = jnp.transpose(y, (0, 2, 1))
        g = jnp.einsum('bth,gh->btg', xc, W_g) + b_g
        forget, inp = jnp.split(g, 2, axis=-1)
        alpha = jnp.exp(ALPHA_LOG_SCALE * jax.nn.softplus(forget_base) * jax.nn.sigmoid(forget))
        beta = jnp.sqrt(1.0 - alpha ** 2 + 1e-06)
        bterm = beta * jax.nn.sigmoid(inp) * xc
        _, h = lax.associative_scan(_scan_combine, (alpha, bterm), axis=1)
        out = jnp.einsum('bth,dh->btd', jax.nn.gelu(gate, approximate=False) * h, W_out)
        return out

    def _L1_xattn_ref(q, k, v, mask, w_q, b_q, w_k, b_k, w_v, b_v, w_o, b_o):
        import jax, jax.numpy as jnp
        import numpy as np
        D_MODEL = 256
        NUM_HEADS = 16
        HEAD_DIM = D_MODEL // NUM_HEADS
        B, S = (4, 512)

        def _split(x):
            b, s, _ = x.shape
            return x.reshape(b, s, NUM_HEADS, HEAD_DIM).transpose(0, 2, 1, 3)
        qh = _split(q @ w_q.T + b_q)
        kh = _split(k @ w_k.T + b_k)
        vh = _split(v @ w_v.T + b_v)
        scale = 1.0 / jnp.sqrt(jnp.asarray(HEAD_DIM, qh.dtype))
        scores = jnp.einsum('bhtd,bhsd->bhts', qh, kh) * scale + mask
        attn = jax.nn.softmax(scores, axis=-1)
        out = jnp.einsum('bhts,bhsd->bhtd', attn, vh)
        b, h, t, dh = out.shape
        out = out.transpose(0, 2, 1, 3).reshape(b, t, h * dh)
        return out @ w_o.T + b_o

    def _L1_ffn_ref(x, w1, b1, w2, b2):
        import jax, jax.numpy as jnp
        import numpy as np

        def _binarize(w):
            alpha = jax.lax.stop_gradient(jnp.mean(jnp.abs(w), axis=1, keepdims=True))
            bw = alpha * jnp.sign(w)
            return w + jax.lax.stop_gradient(bw - w)
        bw1 = _binarize(w1)
        h = jnp.einsum('bsd,hd->bsh', x, bw1) + b1
        h = jax.nn.gelu(h, approximate=False)
        bw2 = _binarize(w2)
        out = jnp.einsum('bsh,dh->bsd', h, bw2) + b2
        return out
    x = _layernorm(x + _L0_attn_ref(x, L0_attn_Wq, L0_attn_Wk, L0_attn_Wv, L0_attn_Wo), axis=-1)
    x = _layernorm(x + _L0_xattn_ref(x, ctx_1024, ctx_1024, mask_BxSxS2_ik0, L0_xattn_Wq, L0_xattn_bq, L0_xattn_Wk, L0_xattn_bk, L0_xattn_Wv, L0_xattn_bv, L0_xattn_Wo, L0_xattn_bo), axis=-1)
    x = _layernorm(x + _L0_ffn_ref(x, L0_ffn_router_w, L0_ffn_W1, L0_ffn_b1, L0_ffn_W2, L0_ffn_b2), axis=-1)
    x = _layernorm(x + _L1_attn_ref(x, L1_attn_W_in, L1_attn_conv_w, L1_attn_conv_b, L1_attn_W_g, L1_attn_b_g, L1_attn_forget_base, L1_attn_W_out), axis=-1)
    x = _layernorm(x + _L1_xattn_ref(x, ctx_1024, ctx_1024, mask_Bx1xSxS2_ff0, L1_xattn_w_q, L1_xattn_b_q, L1_xattn_w_k, L1_xattn_b_k, L1_xattn_w_v, L1_xattn_b_v, L1_xattn_w_o, L1_xattn_b_o), axis=-1)
    x = _layernorm(x + _L1_ffn_ref(x, L1_ffn_w1, L1_ffn_b1, L1_ffn_w2, L1_ffn_b2), axis=-1)
    return x

_drawn_inputs = setup_inputs


def setup_inputs(seed=0):
    import zlib

    import numpy as np

    out = dict(_drawn_inputs(seed))
    spreads = {'L0_xattn_bq': (0.0, 0.1),
     'L0_xattn_bk': (0.0, 0.8),
     'L0_xattn_bv': (0.0, 0.1),
     'L0_xattn_bo': (0.0, 0.1)}
    factors = {'L0_attn_Wq': 4.462,
     'L0_attn_Wk': 3.637,
     'L0_ffn_b1': 4.024,
     'L0_ffn_b2': 3.093,
     'L1_attn_b_g': 7.698,
     'L1_xattn_b_q': 4.233,
     'L1_xattn_b_k': 8.0,
     'L1_ffn_b1': 8.0,
     'L1_ffn_b2': 2.922}
    for name, (base, spread) in spreads.items():
        noise = np.random.default_rng([zlib.crc32(name.encode()), seed]).standard_normal(out[name].shape)
        drawn = base * np.exp(spread * noise) if base else spread * noise
        out[name] = jnp.asarray(drawn.astype(out[name].dtype))
    for name, factor in factors.items():
        out[name] = (out[name] * factor).astype(out[name].dtype)
    return out
```

```python
from contextlib import ExitStack

import numpy as np

import concourse.bass as bass
from concourse import mybir

F32 = mybir.dt.float32
F16 = mybir.dt.float16
BF16 = mybir.dt.bfloat16
I32 = mybir.dt.int32
ALU = mybir.AluOpType
ACT = mybir.ActivationFunctionType
AX = mybir.AxisListType

P = 128
BATCH, SEQ, DIM = 8, 256, 256
TOKENS = BATCH * SEQ
TILES = TOKENS // P
TPB = SEQ // P
KT_ = DIM // P
EPS = 1e-5
NEG = -1.0e30
SCALE = 1024.0
UNSCALE = 1.0 / (SCALE * SCALE)


class Ring:

    def __init__(self, steps, first, last, ahead):
        self.steps, self.first, self.last, self.ahead = steps, first, last, ahead
        self.per = sum(map(len, steps))
        assert self.per % 2 == 0

    def number(self, n, b=0):
        return n % 2, n // 2 + b * (self.per // 2)

    def slot(self, slot, b):
        static = isinstance(b, int)
        if static and b == 0:
            n, turns = len(self.first), 0
        else:
            n, turns = len(self.first) - len(self.last), b
        out = []
        for s, steps in enumerate(self.steps):
            for kind, i in steps:
                if static and (b == 0 and (kind, i) in self.last or b == BATCH - 1 and kind in self.ahead):
                    continue
                if s == slot:
                    out.append((kind, i, *self.number(n, turns)))
                n += 1
        return out

    def prologue(self):
        return [(kind, i, *self.number(n)) for n, (kind, i) in enumerate(self.first)]

    def epilogue(self):
        n = len(self.first) - len(self.last) + self.per * (BATCH - 1)
        n += sum(kind not in self.ahead for steps in self.steps for kind, _ in steps)
        return [(kind, i, *self.number(n + k)) for k, (kind, i) in enumerate(self.last)]

    def place(self, kind, i, b):
        body = b - 1 if kind in self.ahead else b + 1 if (kind, i) in self.last else b
        if first(b) and kind in self.ahead:
            found = self.prologue()
        elif isinstance(b, int) and body == BATCH:
            found = self.epilogue()
        else:
            found = [x for slot in range(len(self.steps)) for x in self.slot(slot, body)]
        return next((bank, uses) for k, j, bank, uses in found if (k, j) == (kind, i))

    def serves(self, kind, i):
        return 1 if kind in self.ahead else -1 if (kind, i) in self.last else 0

    def wait_read(self, engine, free, steps, b):
        last = {}
        for kind, i in steps:
            bank, uses = self.place(kind, i, b)
            last[bank] = uses
        for bank, uses in last.items():
            engine.wait_ge(free[bank], uses + 1)


def at(ap, index):
    return ap[:, index] if isinstance(index, int) else ap[:, bass.ds(index, 1)].squeeze(1)


def identity(pool, tile, made, done):
    pool.memset(tile[:], 0.0).then_inc(made, 1)
    pool.wait_ge(made, done)
    return pool.affine_select(out=tile[:], in_=tile[:], compare_op=ALU.not_equal, fill=1.0, base=0,
                              pattern=[[-1, P]], channel_multiplier=1)

class Norm:

    def __init__(self, ctx, nc, tag):
        def sb(name, shape):
            return ctx.enter_context(nc.sbuf_tensor(f"{tag}_{name}", shape, F32))

        def sem(name):
            return ctx.enter_context(nc.semaphore(f"{tag}_{name}"))

        self.res = sb("res", [P, TPB, DIM])
        self.stats = sb("stats", [P, TPB, 6])
        self.mv = sb("mv", [P, TPB, 2])
        self.var_eps = sb("var_eps", [P, TPB, 1])
        self.rstd = sb("rstd", [P, TPB, 1])
        self.half = sb("half", [P, 1])
        self.stat = sem("stat")
        self.mean_var = sem("mean_var")
        self.var_ready = sem("var_ready")
        self.rstd_ready = sem("rstd_ready")
        self.ln_done = sem("ln_done")

    def wait_res_free(self, dve, b):
        dve.wait_ge(self.ln_done, b * TPB)

    def statistics(self, dve, b, t):
        dve.bn_stats(self.stats[:, t], self.res[:, t]).then_inc(self.stat, 1)
        dve.wait_ge(self.stat, b * TPB + t + 1)
        dve.memset(self.var_eps[:, t], 0.0)
        dve.bn_aggr(self.mv[:, t], self.stats[:, t]).then_inc(self.mean_var, 1)
        dve.wait_ge(self.mean_var, b * TPB + t + 1)
        dve.tensor_scalar(self.var_eps[:, t], self.mv[:, t, 1:2], EPS, None, ALU.add).then_inc(self.var_ready, 1)

    def root(self, pool, b, t):
        pool.wait_ge(self.var_ready, b * TPB + t + 1)
        pool.tensor_tensor(self.rstd[:, t], self.var_eps[:, t], self.half[:], ALU.pow).then_inc(self.rstd_ready, 1)

    def apply(self, dve, b, t, out):
        dve.wait_ge(self.rstd_ready, b * TPB + t + 1)
        dve.tensor_scalar(out, self.res[:, t], self.mv[:, t, 0:1], self.rstd[:, t],
                          ALU.subtract, ALU.mult).then_inc(self.ln_done, 1)


def first(b):
    return isinstance(b, int) and b == 0


HEADS, HD = 16, 64
WINDOW = SEQ // 4
SPAN = P + WINDOW
QKV = 3 * HEADS * HD
PSCALE = 4096.0
WA = Ring(
    steps=[
        [("project", 0), ("project", 1), ("project", 2)],
        [("project", 3), ("project", 4), ("project", 5)],
        [("heads", 3), ("project", 6), ("turn", 0), ("turn", 1)],
        [("project", 7), ("mix", 0), ("mix", 1), ("turn", 2), ("turn", 3), ("heads", 0)],
        [("project", 8), ("project", 9), ("project", 10)],
        [("heads", 1), ("project", 11), ("turn", 4), ("turn", 5)],
        [("turn", 6), ("turn", 7)],
        [("heads", 2)],
    ],
    first=([("project", n) for n in range(6)] + [("turn", 0), ("turn", 1), ("project", 6), ("turn", 2), ("turn", 3)]
           + [("project", n) for n in range(7, 12)] + [("turn", n) for n in range(4, 8)]),
    last=[("heads", 3), ("mix", 0), ("mix", 1)],
    ahead={"project", "turn"},
)
ROPE_SIN = {0: 0, 1: 1, 3: 2, 4: 3}
ROPE_ADD = {1: 0, 2: 1, 4: 2, 5: 3}


def windows(ap):
    return bass.AP(tensor=ap.tensor, offset=ap.offset, ap=[list(ap.ap[0]), [SEQ + WINDOW, 2], [1, SPAN]])


def window_attention(nc, x_dram, xt_dram, wqkv_dram, wo_dram, rope_dram, X):
    with ExitStack() as ctx:
        def sb(name, shape, dt=F32):
            return ctx.enter_context(nc.sbuf_tensor("wa_" + name, shape, dt))

        def sem(name):
            sems.append(nc.alloc_semaphore("wa_" + name))
            return sems[-1]

        sems = []

        w_stage = sb("w_stage", [P, 2, KT_, 512])
        wh = sb("wh", [P, KT_, QKV], F16)
        wl = sb("wl", [P, KT_, QKV], F16)
        wo = sb("wo", [P, HEADS * HD // P, DIM])
        cos_sin = sb("cos_sin", [P, TPB, 2, HD])
        x_stage = sb("x_stage", [P, 2, KT_, SEQ])
        xh = sb("xh", [P, 2, KT_, SEQ], F16)
        xl = sb("xl", [P, 2, KT_, SEQ], F16)
        raw = sb("raw", [P, 2, HEADS, HD])
        rot = sb("rot", [P, 2, HEADS, HD])
        sine = sb("sine", [P, HEADS, HD])
        qt = [sb(f"qt{k}", [P, HEADS, SEQ]) for k in range(2)]
        kt = [sb(f"kt{k}", [P, HEADS // 2, SEQ]) for k in range(2)]
        vh = [sb(f"vh{k}", [P, TPB, HEADS, HD + 1], F16) for k in range(2)]
        vl = [sb(f"vl{k}", [P, TPB, HEADS, HD + 1], F16) for k in range(2)]
        shifted = [sb(f"shifted{k}", [P, 2, SPAN]) for k in range(4)]
        probs = [sb(f"probs{k}", [P, 2, SEQ]) for k in range(4)]
        top = sb("top", [P, 4, 2])
        pth = [sb(f"pth{k}", [P, 2 * SEQ], F16) for k in range(4)]
        ptl = [sb(f"ptl{k}", [P, 2 * SEQ], F16) for k in range(4)]
        inv = sb("inv", [P, 2, TPB, 2])
        heads_out = sb("heads_out", [P, TPB, HEADS, HD])
        heads_t = sb("heads_t", [P, HEADS // 2, SEQ])
        ident = sb("ident", [P, P])
        ident_bf = sb("ident_bf", [P, P], BF16)
        band = sb("band", [P, TPB, SPAN], BF16)

        shared = [ctx.enter_context(nc.psum_tensor(f"wa_shared{k}", [P, 512], F32)) for k in range(2)]
        s_bank = [ctx.enter_context(nc.psum_tensor(f"wa_scores{k}", [P, 2, SEQ], F32)) for k in range(2)]
        t_bank = [ctx.enter_context(nc.psum_tensor(f"wa_turned{k}", [P, 512], F32)) for k in range(2)]
        o_bank = [ctx.enter_context(nc.psum_tensor(f"wa_out{k}", [P, TPB, 2, P], F32)) for k in range(2)]

        norm = Norm(ctx, nc, "wa")
        w_loaded = [sem("w_loaded0"), sem("w_loaded1")]
        w_high = sem("w_high")
        w_low = sem("w_low")
        x_loaded = [sem("x_loaded0"), sem("x_loaded1")]
        x_high = sem("x_high")
        x_low = sem("x_low")
        tokens_loaded = sem("tokens_loaded")
        wo_loaded = sem("wo_loaded")
        rope_loaded = sem("rope_loaded")
        consts = sem("consts")
        zeroed = sem("zeroed")
        full = [sem("full0"), sem("full1")]
        free = [sem("free0"), sem("free1")]
        cos_done = sem("cos_done")
        sin_done = sem("sin_done")
        rope_done = sem("rope_done")
        v_high = sem("v_high")
        scores = sem("scores")
        maxed = sem("maxed")
        shift = sem("shift")
        exped = sem("exped")
        probs_t = sem("probs_t")
        probs_high = sem("probs_high")
        probs_low = sem("probs_low")
        weighted = sem("weighted")
        inverted = sem("inverted")
        normed = sem("normed")

        def wait_read(engine, steps, b):
            WA.wait_read(engine, free, steps, b)

        def wait_raw(engine, b, r):
            wait_read(engine, [("project", 6 * (r // 2) + 2 * (r % 2) + c) for c in range(2)], b)

        def wait_rot_used(engine, b, r):
            bank, uses = WA.place("turn", 2 * (r - 2) + 1, b) if r >= 2 else WA.place("turn", 2 * (r + 2) + 1, b - 1)
            engine.wait_ge(full[bank], uses + 1)

        block_scope = ExitStack()
        block = block_scope.enter_context(nc.Block())

        @block.sync
        def _(sp):
            def load_x(b, par):
                sp.dma_start(x_stage[:, par], xt_dram[:, :, bass.ds(b * SEQ, SEQ)]).then_inc(x_loaded[par], 16)

            load_x(0, 0)
            for c in range(6):
                if c >= 2:
                    sp.wait_ge(w_low, c - 1)
                sp.dma_start(w_stage[:, c % 2], wqkv_dram[:, :, c * 512:(c + 1) * 512]).then_inc(w_loaded[c % 2], 16)
                if c == 1:
                    load_x(1, 1)
                    sp.dma_start(cos_sin[:], rope_dram).then_inc(rope_loaded, 16)
            sp.dma_start(wo[:], wo_dram).then_inc(wo_loaded, 16)
            sp.dma_start(X[:], x_dram).then_inc(tokens_loaded, 16)
            with sp.Fori(0, BATCH // 2 - 1) as i:
                sp.wait_ge(x_low, 2 * i + 1)
                load_x(2 * i + 2, 0)
                sp.wait_ge(x_low, 2 * i + 2)
                load_x(2 * i + 3, 1)

        @block.gpsimd
        def _(pool):
            identity(pool, ident, consts, 1).then_inc(consts, 1)
            identity(pool, ident_bf, consts, 3).then_inc(consts, 1)
            pool.memset(norm.half[:], -0.5).then_inc(consts, 1)
            pool.memset(band[:], 0.0).then_inc(consts, 1)
            pool.wait_ge(consts, 6)
            for t, base in ((0, 0), (1, P - WINDOW)):
                n = 6 + 2 * t
                pool.affine_select(out=band[:, t], in_=band[:, t], compare_op=ALU.is_ge, fill=NEG,
                                   base=base + WINDOW, pattern=[[-1, SPAN]], channel_multiplier=1).then_inc(consts, 1)
                pool.wait_ge(consts, n + 1)
                pool.affine_select(out=band[:, t], in_=band[:, t], compare_op=ALU.is_ge, fill=NEG,
                                   base=WINDOW - base, pattern=[[1, SPAN]], channel_multiplier=-1).then_inc(consts, 1)

            def cosine(b, r):
                wait_raw(pool, b, r)
                if r == 0 and isinstance(b, int) and b == 0:
                    pool.wait_ge(rope_loaded, 16)
                if not (first(b) and r < 2):
                    wait_rot_used(pool, b, r)
                c = cos_sin[:, r // 2, 0].unsqueeze(1).broadcast_to((P, HEADS, HD))
                pool.tensor_tensor(rot[:, r % 2], raw[:, r % 2], c, ALU.mult).then_inc(cos_done, 1)

            def batch(b, before=True, after=True):
                for slot in range(8):
                    if after and slot in ROPE_SIN:
                        cosine(b + 1, ROPE_SIN[slot])
                    if before and slot == 3:
                        norm.root(pool, b - 1, 0)
                        norm.root(pool, b - 1, 1)

            for r in range(4):
                cosine(0, r)
            batch(0, before=False)
            with pool.Fori(0, BATCH // 2 - 1) as i:
                batch(2 * i + 1)
                batch(2 * i + 2)
            batch(BATCH - 1, after=False)
            norm.root(pool, BATCH - 1, 0)
            norm.root(pool, BATCH - 1, 1)

        @block.scalar
        def _(act):
            def split_w(c):
                act.wait_ge(w_loaded[c % 2], 16 * (c // 2 + 1))
                act.activation(wh[:, :, c * 512:(c + 1) * 512], w_stage[:, c % 2], ACT.Copy, scale=SCALE).then_inc(w_high, 1)

            def split_x(b, par):
                act.wait_ge(x_loaded[par], 8 * (b - par) + 16)
                act.activation(xh[:, par], x_stage[:, par], ACT.Copy, scale=SCALE).then_inc(x_high, 1)

            def step(b, par, kind, i, bank, uses):
                src = shared[bank]
                if kind == "mix":
                    return
                act.wait_ge(full[bank], uses + 1)
                if kind == "project":
                    t, c = divmod(i, 6)
                    if c < 4:
                        unit = 2 * t + c // 2
                        if not (first(b) and unit < 2):
                            act.wait_ge(sin_done, b * 4 + unit - 1)
                            act.wait_ge(cos_done, b * 4 + unit - 1)
                        dst = raw[:, unit % 2, (c % 2) * 8:(c % 2) * 8 + 8]
                        act.activation(dst, src[:].rearrange("p (h d) -> p h d", h=8), ACT.Copy,
                                       scale=UNSCALE).then_inc(free[bank], 1)
                    else:
                        h0 = (c - 4) * 8
                        act.activation(vh[par][:, t, h0:h0 + 8, 0:HD], src[:].rearrange("p (h d) -> p h d", h=8),
                                       ACT.Copy, scale=1.0 / SCALE).then_inc(v_high, 1)
                elif kind == "turn":
                    t, c = divmod(i, 4)
                    cols = slice(t * P, (t + 1) * P)
                    s = src[:].rearrange("p (h q) -> p h q", h=4)
                    if c < 2:
                        act.activation(qt[par][0:HD, 8 * c:8 * c + 8:2, cols], s[0:HD], ACT.Copy)
                        act.activation(qt[par][HD:P, 8 * c + 1:8 * c + 8:2, cols], s[HD:P],
                                       ACT.Copy).then_inc(free[bank], 1)
                    else:
                        act.activation(kt[par][:, 4 * (c - 2):4 * (c - 2) + 4, cols], s,
                                       ACT.Copy).then_inc(free[bank], 1)
                elif kind == "heads":
                    act.activation(heads_t[:, 2 * i:2 * i + 2], src[:].rearrange("p (h q) -> p h q", h=2),
                                   ACT.Copy).then_inc(free[bank], 1)

            def batch(b, par, before=True, after=True):
                for slot in range(8):
                    if after and slot == 0:
                        split_x(b + 1, 1 - par)
                    for t in range(TPB):
                        n = 2 * slot + t
                        k = 2 * (slot % 2) + t
                        act.wait_ge(shift, b * 16 + n + 1)
                        if not (first(b) and slot < 2):
                            act.wait_ge(probs_t, b * 16 + 2 * slot - 2)
                        act.activation(probs[k][:, :, t * WINDOW:t * WINDOW + SPAN], shifted[k][:], ACT.Exp,
                                       scale=HD ** -0.5).then_inc(exped, 1)
                    for kind, i, bank, uses in WA.slot(slot, b):
                        d = WA.serves(kind, i)
                        step(b + d, (par + d) % 2, kind, i, bank, uses)
                    for h in range(2):
                        k = 2 * (slot % 2) + h
                        act.wait_ge(probs_t, b * 16 + 2 * slot + h + 1)
                        if not (first(b) and slot < 2):
                            act.wait_ge(weighted, b * 8 + slot - 1)
                        act.activation(windows(pth[k][:]), windows(t_bank[h][:]), ACT.Copy, scale=PSCALE).then_inc(probs_high, 1)

            split_x(0, 0)
            for c in range(6):
                split_w(c)
            act.wait_ge(zeroed, 1)
            for kind, i, bank, uses in WA.prologue():
                step(0, 0, kind, i, bank, uses)
            batch(0, 0, before=False)
            with act.Fori(0, BATCH // 2 - 1) as i:
                batch(2 * i + 1, 1)
                batch(2 * i + 2, 0)
            batch(BATCH - 1, 1, after=False)
            for kind, i, bank, uses in WA.epilogue():
                step(BATCH - 1, 1, kind, i, bank, uses)

        @block.vector
        def _(dve):
            def split_w(c):
                cols = slice(c * 512, (c + 1) * 512)
                dve.wait_ge(w_high, c + 1)
                dve.scalar_tensor_tensor(out=wl[:, :, cols], in0=w_stage[:, c % 2], scalar=SCALE,
                                         in1=wh[:, :, cols], op0=ALU.mult, op1=ALU.subtract).then_inc(w_low, 1)

            def split_x(b, par):
                dve.wait_ge(x_high, b + 1)
                dve.scalar_tensor_tensor(out=xl[:, par], in0=x_stage[:, par], scalar=SCALE,
                                         in1=xh[:, par], op0=ALU.mult, op1=ALU.subtract).then_inc(x_low, 1)

            def sin_part(b, r):
                wait_raw(dve, b, r)
                if not (first(b) and r == 0):
                    dve.wait_ge(rope_done, b * 4 + r)
                for a, z in ((0, HD // 2), (HD // 2, 0)):
                    s = cos_sin[:, r // 2, 1, a:a + HD // 2].unsqueeze(1).broadcast_to((P, HEADS, HD // 2))
                    ins = dve.tensor_tensor(sine[:, :, a:a + HD // 2], raw[:, r % 2, :, z:z + HD // 2], s, ALU.mult)
                ins.then_inc(sin_done, 1)

            def add_part(b, r):
                dve.wait_ge(sin_done, b * 4 + r + 1)
                dve.wait_ge(cos_done, b * 4 + r + 1)
                dve.tensor_tensor(rot[:, r % 2], rot[:, r % 2], sine[:], ALU.add).then_inc(rope_done, 1)

            def value_low(b, par, i, bank):
                t, c = divmod(i, 6)
                h0 = (c - 4) * 8
                dve.wait_ge(v_high, b * 4 + 2 * t + c - 3)
                dve.scalar_tensor_tensor(out=vl[par][:, t, h0:h0 + 8, 0:HD],
                                         in0=shared[bank][:].rearrange("p (h d) -> p h d", h=8), scalar=1.0 / SCALE,
                                         in1=vh[par][:, t, h0:h0 + 8, 0:HD], op0=ALU.mult,
                                         op1=ALU.subtract).then_inc(free[bank], 1)

            def residual(b, t, bank, uses):
                dve.wait_ge(full[bank], uses + 1)
                norm.wait_res_free(dve, b)
                dve.tensor_tensor(norm.res[:, t], shared[bank][:, 0:DIM], at(X, b * TPB + t), ALU.add).then_inc(free[bank], 1)
                dve.wait_ge(free[bank], uses + 1)
                norm.statistics(dve, b, t)

            def layer_norm(b, t):
                norm.apply(dve, b, t, at(X, b * TPB + t))

            def shift_scores(b, u, par):
                for t in range(TPB):
                    n = 2 * u + t
                    k = 2 * (u % 2) + t
                    dve.wait_ge(scores, b * 16 + n + 1)
                    if not (first(b) and u < 2):
                        dve.wait_ge(exped, b * 16 + n - 3)
                    dve.tensor_reduce(top[:, k], s_bank[t][:, :, 0:SPAN], AX.X, ALU.max).then_inc(maxed, 1)
                    dve.wait_ge(maxed, b * 16 + n + 1)
                    dve.tensor_tensor(shifted[k][:], s_bank[t][:, :, 0:SPAN],
                                      top[:, k].unsqueeze(2).broadcast_to((P, 2, SPAN)), ALU.subtract).then_inc(shift, 1)

            def normalise(b, u):
                dve.wait_ge(weighted, b * 8 + u + 1)
                bank = o_bank[u % 2]
                if not (first(b) and u < 2):
                    dve.wait_ge(normed, b * 8 + u - 1)
                dve.reciprocal(inv[:, u % 2], bank[:, :, :, HD:HD + 1].squeeze(3)).then_inc(inverted, 1)
                dve.wait_ge(inverted, b * 8 + u + 1)
                if not first(b):
                    before, uses = WA.place("heads", u // 2, b - 1)
                    dve.wait_ge(full[before], uses + 1)
                dve.tensor_tensor(heads_out[:, :, 2 * u:2 * u + 2], bank[:, :, :, 0:HD],
                                  inv[:, u % 2].unsqueeze(3).broadcast_to((P, TPB, 2, HD)), ALU.mult).then_inc(normed, 1)

            def probs_rest(b, u):
                for h in range(2):
                    k = 2 * (u % 2) + h
                    dve.wait_ge(probs_high, b * 16 + 2 * u + h + 1)
                    dve.scalar_tensor_tensor(out=windows(ptl[k][:]), in0=windows(t_bank[h][:]), scalar=PSCALE,
                                             in1=windows(pth[k][:]), op0=ALU.mult, op1=ALU.subtract).then_inc(probs_low, 1)

            def batch(b, par, before=True, after=True):
                for slot in range(8):
                    if after and slot == 0:
                        split_x(b + 1, 1 - par)
                    if slot < 7:
                        shift_scores(b, slot + 1, par)
                    elif after:
                        shift_scores(b + 1, 0, 1 - par)
                    for kind, i, bank, uses in WA.slot(slot, b):
                        if kind == "project" and i % 6 > 3:
                            value_low(b + 1, 1 - par, i, bank)
                        if kind == "mix":
                            residual(b - 1, i, bank, uses)
                    if after and slot in ROPE_ADD:
                        add_part(b + 1, ROPE_ADD[slot])
                    if after and slot in ROPE_SIN:
                        sin_part(b + 1, ROPE_SIN[slot])
                    if before and slot == 4:
                        layer_norm(b - 1, 0)
                        layer_norm(b - 1, 1)
                    probs_rest(b, slot)
                    if slot > 0:
                        normalise(b, slot - 1)
                    elif before:
                        normalise(b - 1, 7)

            for k in range(2):
                dve.memset(vh[k][:, :, :, HD:HD + 1], SCALE)
                dve.memset(vl[k][:, :, :, HD:HD + 1], 0.0)
                dve.memset(qt[k][0:HD, 1:HEADS:2], 0.0)
                dve.memset(qt[k][HD:P, 0:HEADS:2], 0.0)
            for k in range(4):
                dve.memset(probs[k][:], 0.0)
                dve.memset(pth[k][:], 0.0)
                ins = dve.memset(ptl[k][:], 0.0)
            ins.then_inc(zeroed, 1)
            split_x(0, 0)
            for c in range(6):
                split_w(c)
            dve.wait_ge(rope_loaded, 16)
            for kind, i, bank, uses in WA.prologue():
                if kind == "project" and i % 6 > 3:
                    value_low(0, 0, i, bank)
                if kind == "project" and i % 6 in (1, 3):
                    r = 2 * (i // 6) + (i % 6) // 2
                    sin_part(0, r)
                    add_part(0, r)
            shift_scores(0, 0, 0)
            dve.wait_ge(tokens_loaded, 16)
            batch(0, 0, before=False)
            with dve.Fori(0, BATCH // 2 - 1) as i:
                batch(2 * i + 1, 1)
                batch(2 * i + 2, 0)
            batch(BATCH - 1, 1, after=False)
            normalise(BATCH - 1, 7)
            for kind, i, bank, uses in WA.epilogue():
                if kind == "mix":
                    residual(BATCH - 1, i, bank, uses)
            layer_norm(BATCH - 1, 0)
            layer_norm(BATCH - 1, 1)

        @block.tensor
        def _(pe):
            def step(b, par, kind, i, bank, uses):
                dst = shared[bank]
                if not (isinstance(uses, int) and uses == 0):
                    pe.wait_ge(free[bank], uses)
                if kind == "project":
                    t, c = divmod(i, 6)
                    if i == 0:
                        pe.wait_ge(x_low, b + 1)
                    if first(b):
                        pe.wait_ge(w_low, c + 1)
                    tok = slice(t * P, (t + 1) * P)
                    cols = slice(c * 512, (c + 1) * 512)
                    for k in range(KT_):
                        for n, (a, w) in enumerate(((xh, wh), (xh, wl), (xl, wh))):
                            ins = pe.matmul(dst[:], a[:, par, k, tok], w[:, k, cols],
                                            start=(k == 0 and n == 0), stop=(k == KT_ - 1 and n == 2))
                elif kind == "turn":
                    t, c = divmod(i, 4)
                    unit = 2 * t + c // 2
                    pe.wait_ge(rope_done, b * 4 + unit + 1)
                    for j in range(4):
                        h = 8 * (c % 2) + 2 * j
                        ins = pe.transpose(dst[:, j * P:(j + 1) * P],
                                           rot[:, unit % 2, h:h + 2].rearrange("p h d -> p (h d)"), ident[:])
                elif kind == "heads":
                    pe.wait_ge(normed, b * 8 + 2 * i + 2)
                    for j in range(2):
                        for t in range(TPB):
                            pair = 2 * i + j
                            ins = pe.transpose(dst[:, (2 * j + t) * P:(2 * j + t + 1) * P],
                                               heads_out[:, t, 2 * pair:2 * pair + 2].rearrange("p h d -> p (h d)"), ident[:])
                else:
                    wait_read(pe, [("heads", j) for j in range(4)], b)
                    for j in range(HEADS // 2):
                        ins = pe.matmul(dst[:, 0:DIM], heads_t[:, j, i * P:(i + 1) * P], wo[:, j],
                                        start=(j == 0), stop=(j == HEADS // 2 - 1))
                ins.then_inc(full[bank], 1)

            def score(b, u, par):
                if u == 0:
                    wait_read(pe, [("turn", i) for i in range(4, 8)], b)
                for t in range(TPB):
                    if not (first(b) and u == 0):
                        pe.wait_ge(shift, b * 16 + 2 * u + t - 1)
                    for h in range(2):
                        dst = s_bank[t][:, h, 0:SPAN]
                        pe.matmul(dst, ident_bf[:], band[:, t], start=True, stop=False)
                        ins = pe.matmul(dst, qt[par][:, 2 * u + h, t * P:(t + 1) * P],
                                        kt[par][:, u, t * WINDOW:t * WINDOW + SPAN], start=False, stop=True)
                    ins.then_inc(scores, 1)

            def turn_probs(b, u):
                pe.wait_ge(exped, b * 16 + 2 * u + 2)
                for h in range(2):
                    if not (first(b) and u == 0):
                        pe.wait_ge(probs_low, b * 16 + 2 * u + h - 1)
                    for j in range(2):
                        for t in range(TPB):
                            ins = pe.transpose(t_bank[h][:, j * SEQ + t * P:j * SEQ + (t + 1) * P],
                                               probs[2 * (u % 2) + t][:, h, j * P:(j + 1) * P], ident[:])
                    ins.then_inc(probs_t, 1)

            def weigh(b, u, par):
                pe.wait_ge(probs_low, b * 16 + 2 * u + 2)
                if u == 0:
                    wait_read(pe, [("project", 10), ("project", 11)], b)
                if not (first(b) and u < 2):
                    pe.wait_ge(normed, b * 8 + u - 1)
                for t in range(TPB):
                    for h in range(2):
                        k = 2 * (u % 2) + h
                        n = 0
                        for j in range(2):
                            q = slice(j * SEQ + t * P, j * SEQ + (t + 1) * P)
                            for a, v in ((pth[k], vh[par]), (pth[k], vl[par]), (ptl[k], vh[par])):
                                ins = pe.matmul(o_bank[u % 2][:, t, h, 0:HD + 1], a[:, q], v[:, j, 2 * u + h],
                                                start=(n == 0), stop=(n == 5))
                                n += 1
                ins.then_inc(weighted, 1)

            def batch(b, par, before=True, after=True):
                for slot in range(8):
                    if slot < 7:
                        score(b, slot + 1, par)
                    elif after:
                        score(b + 1, 0, 1 - par)
                    for kind, i, bank, uses in WA.slot(slot, b):
                        d = WA.serves(kind, i)
                        step(b + d, (par + d) % 2, kind, i, bank, uses)
                    turn_probs(b, slot)
                    if slot > 0:
                        weigh(b, slot - 1, par)
                    elif before:
                        weigh(b - 1, 7, 1 - par)

            pe.wait_ge(consts, 10)
            for kind, i, bank, uses in WA.prologue():
                step(0, 0, kind, i, bank, uses)
            score(0, 0, 0)
            pe.wait_ge(wo_loaded, 16)
            batch(0, 0, before=False)
            with pe.Fori(0, BATCH // 2 - 1) as i:
                batch(2 * i + 1, 1)
                batch(2 * i + 2, 0)
            batch(BATCH - 1, 1, after=False)
            weigh(BATCH - 1, 7, 1)
            for kind, i, bank, uses in WA.epilogue():
                step(BATCH - 1, 1, kind, i, bank, uses)

        block_scope.close()
        nc.clear_and_free_semaphores(sems)
        nc.all_engine_barrier()


CTX = 77
CH, CD = 16, 16
UH = 4
UNITS = TPB * CH // UH
MASKED = -4.0e9
OPEN = 1.0e38
CA = Ring(
    steps=[
        [("key", 0)],
        [("heads", 1), ("value", 0)],
        [("mix", 1)],
        [("tokens", 0)],
        [],
        [("query", 0)],
        [("heads", 0)],
        [("mix", 0)],
    ],
    first=[("key", 0), ("value", 0), ("tokens", 0), ("query", 0)],
    last=[("heads", 1), ("mix", 1)],
    ahead={"key", "value", "tokens", "query"},
)


def cross_attention(nc, tag, w_dram, b_dram, rows_dram, ctx_dram, mask_dram, additive, X):
    with ExitStack() as ctx:
        def sb(name, shape, dt=F32):
            return ctx.enter_context(nc.sbuf_tensor(f"{tag}_{name}", shape, dt))

        def sem(name):
            sems.append(nc.alloc_semaphore(f"{tag}_{name}"))
            return sems[-1]

        sems = []

        w = sb("w", [P, 4, KT_, DIM])
        bias = sb("bias", [P, 2, KT_])
        rows = sb("rows", [P, 2, DIM])
        context = [sb(f"context{k}", [P, KT_, CTX]) for k in range(2)]
        xs = [sb(f"xs{k}", [P, TPB, DIM]) for k in range(2)]
        mask = sb("mask", [P, TILES, CTX], F32 if additive else I32)
        limit = None if additive else sb("limit", [P, TILES, CTX])
        head_of = sb("head_of", [P, CH // KT_])
        ident = sb("ident", [P, P])
        xt = [sb(f"xt{k}", [P, KT_, SEQ]) for k in range(2)]
        q = [sb(f"q{k}", [P, KT_, SEQ]) for k in range(2)]
        kb = sb("kb", [P, KT_, CTX])
        km = [sb(f"km{k}", [P, KT_, CH // KT_, CTX]) for k in range(2)]
        v = sb("v", [P, CH, CD])
        vh = [sb(f"vh{k}", [P, CH, CD + 1], F16) for k in range(2)]
        vl = [sb(f"vl{k}", [P, CH, CD + 1], F16) for k in range(2)]
        z = [sb(f"z{k}", [P, UH, CTX]) for k in range(2)]
        top = sb("top", [P, 2, UH])
        probs = [sb(f"probs{k}", [P, UH, CTX]) for k in range(2)]
        pth = [sb(f"pth{k}", [P, UH * P], F16) for k in range(2)]
        ptl = [sb(f"ptl{k}", [P, UH * P], F16) for k in range(2)]
        inv = sb("inv", [P, TPB, CH])
        o = sb("o", [P, TPB, CH, CD])
        ot = sb("ot", [P, TPB, KT_, P])
        xb = sb("xb", [P, TPB, DIM])

        shared = [ctx.enter_context(nc.psum_tensor(f"{tag}_shared{k}", [P, 512], F32)) for k in range(2)]
        s_bank = [ctx.enter_context(nc.psum_tensor(f"{tag}_scores{k}", [P, 512], F32)) for k in range(2)]
        t_bank = [ctx.enter_context(nc.psum_tensor(f"{tag}_turned{k}", [P, 512], F32)) for k in range(2)]
        o_bank = [ctx.enter_context(nc.psum_tensor(f"{tag}_out{k}", [P, CH, 32], F32)) for k in range(2)]

        norm = Norm(ctx, nc, tag)
        kv_loaded = sem("kv_loaded")
        context_loaded = [sem("context_loaded0"), sem("context_loaded1")]
        staged = [sem("staged0"), sem("staged1")]
        w_loaded = sem("w_loaded")
        mask_loaded = sem("mask_loaded")
        consts = sem("consts")
        limits = sem("limits")
        ones = sem("ones")
        full = [sem("full0"), sem("full1")]
        free = [sem("free0"), sem("free1")]
        key_masked = sem("key_masked")
        v_high = sem("v_high")
        v_low = sem("v_low")
        token_sum = sem("token_sum")
        scores = sem("scores")
        masked = sem("masked")
        maxed = sem("maxed")
        shift = sem("shift")
        exped = sem("exped")
        probs_t = sem("probs_t")
        probs_high = sem("probs_high")
        probs_low = sem("probs_low")
        weighted = sem("weighted")
        inverted = sem("inverted")
        normed = sem("normed")

        def wait_read(engine, steps, b):
            CA.wait_read(engine, free, steps, b)

        def wait_full(engine, kind, i, b):
            bank, uses = CA.place(kind, i, b)
            engine.wait_ge(full[bank], uses + 1)

        def both(batch):
            def run(engine):
                batch(0, 0, before=False)
                with engine.Fori(0, BATCH // 2 - 1) as i:
                    batch(2 * i + 1, 1)
                    batch(2 * i + 2, 0)
                batch(BATCH - 1, 1, after=False)
            return run

        block_scope = ExitStack()
        block = block_scope.enter_context(nc.Block())

        @block.sync
        def _(sp):
            def load_context(b, par):
                sp.dma_start(context[par][:], ctx_dram[:, :, bass.ds(b * CTX, CTX)]).then_inc(context_loaded[par], 16)

            def stage(b, par):
                sp.dma_start(xs[par][:], X[:, bass.ds(b * TPB, TPB)]).then_inc(staged[par], 16)

            for b in (0, 1):
                load_context(b, b)
                stage(b, b)
            sp.dma_start(bias[:], b_dram).then_inc(kv_loaded, 16)
            sp.dma_start(rows[:], rows_dram).then_inc(kv_loaded, 16)
            sp.dma_start(w[:], w_dram).then_inc(w_loaded, 16)
            sp.dma_start(mask[:], mask_dram).then_inc(mask_loaded, 16)

            def replace(b, par):
                wait_full(sp, "value", 0, b)
                load_context(b + 2, par)
                wait_full(sp, "tokens", 0, b)
                sp.wait_ge(token_sum, (b + 1) * TPB)
                stage(b + 2, par)

            replace(0, 0)
            replace(1, 1)
            with sp.Fori(1, BATCH // 2 - 1) as i:
                replace(2 * i, 0)
                replace(2 * i + 1, 1)

        @block.gpsimd
        def _(pool):
            identity(pool, ident, consts, 1).then_inc(consts, 1)
            pool.memset(norm.half[:], -0.5).then_inc(consts, 1)
            pool.memset(head_of[:], 1.0).then_inc(consts, 1)
            pool.wait_ge(consts, 4)
            pool.affine_select(out=head_of[:], in_=head_of[:], compare_op=ALU.is_ge, fill=0.0, base=0,
                               pattern=[[-CD, CH // KT_]], channel_multiplier=1).then_inc(consts, 1)
            pool.wait_ge(consts, 5)
            pool.affine_select(out=head_of[:], in_=head_of[:], compare_op=ALU.is_ge, fill=0.0, base=CD - 1,
                               pattern=[[CD, CH // KT_]], channel_multiplier=-1).then_inc(consts, 1)
            pool.wait_ge(consts, 6)
            pool.wait_ge(kv_loaded, 32)

            def mask_keys(b, par):
                wait_read(pool, [("key", 0)], b)
                for g in range(KT_):
                    ins = pool.tensor_tensor(km[par][:, g], kb[:, g].unsqueeze(1).broadcast_to((P, CH // KT_, CTX)),
                                             head_of[:].unsqueeze(2).broadcast_to((P, CH // KT_, CTX)), ALU.mult)
                ins.then_inc(key_masked, 1)

            def subtract(b, c):
                pool.wait_ge(maxed, b * UNITS + c + 1)
                k = c % 2
                pool.tensor_tensor(z[k][:], z[k][:], top[:, k].unsqueeze(2).broadcast_to((P, UH, CTX)),
                                   ALU.subtract).then_inc(shift, 1)

            def add_bias(b, par):
                if not first(b):
                    wait_read(pool, [("mix", 0), ("mix", 1)], b - 1)
                pool.wait_ge(staged[par], 8 * (b - par) + 16)
                for t in range(TPB):
                    pool.tensor_tensor(xb[:, t], xs[par][:, t], rows[:, 1], ALU.add).then_inc(token_sum, 1)

            def batch(b, par, before=True, after=True):
                for c in range(UNITS):
                    if c < UNITS - 1:
                        subtract(b, c + 1)
                    elif after:
                        subtract(b + 1, 0)
                    if c == 0 and after:
                        mask_keys(b + 1, 1 - par)
                    if c == 2 and before:
                        norm.root(pool, b - 1, 1)
                    if c == 4:
                        add_bias(b, par)
                    if c == 7:
                        norm.root(pool, b, 0)

            mask_keys(0, 0)
            subtract(0, 0)
            both(batch)(pool)
            norm.root(pool, BATCH - 1, 1)

        @block.scalar
        def _(act):
            act.wait_ge(kv_loaded, 32)

            def step(b, par, kind, i, bank, uses):
                src = shared[bank]
                if kind in ("mix", "value"):
                    return
                act.wait_ge(full[bank], uses + 1)
                if kind == "tokens":
                    ins = act.activation(xt[par][:], src[:].rearrange("p (g q) -> p g q", g=KT_), ACT.Copy)
                elif kind == "query":
                    for g in range(KT_):
                        ins = act.activation(q[par][:, g], src[:, g * SEQ:(g + 1) * SEQ], ACT.Identity, bias=bias[:, 0, g:g + 1])
                elif kind == "key":
                    if not first(b):
                        act.wait_ge(key_masked, b)
                    for g in range(KT_):
                        ins = act.activation(kb[:, g], src[:, g * CTX:(g + 1) * CTX], ACT.Identity, bias=bias[:, 1, g:g + 1])
                elif kind == "heads":
                    ins = act.activation(ot[:, i], src[:, 0:DIM].rearrange("p (g q) -> p g q", g=KT_), ACT.Copy)
                ins.then_inc(free[bank], 1)

            def value_high(b, par):
                wait_read(act, [("value", 0)], b)
                act.activation(vh[par][0:CTX, :, 0:CD], v[0:CTX], ACT.Copy, scale=SCALE).then_inc(v_high, 1)

            def batch(b, par, before=True, after=True):
                for c in range(UNITS):
                    k = c % 2
                    act.wait_ge(shift, b * UNITS + c + 1)
                    if not (first(b) and c < 2):
                        act.wait_ge(probs_t, b * UNITS + c - 1)
                    act.activation(probs[k][:], z[k][:], ACT.Exp, scale=1.0 if additive else CD ** -0.5).then_inc(exped, 1)
                    for kind, i, bank, uses in CA.slot(c, b):
                        d = CA.serves(kind, i)
                        step(b + d, (par + d) % 2, kind, i, bank, uses)
                    act.wait_ge(probs_t, b * UNITS + c + 1)
                    if not (first(b) and c < 2):
                        act.wait_ge(weighted, b * UNITS + c - 1)
                    act.activation(pth[k][0:CTX], t_bank[k][0:CTX], ACT.Copy, scale=PSCALE).then_inc(probs_high, 1)
                    if c == 2 and after:
                        value_high(b + 1, 1 - par)

            act.wait_ge(ones, 1)
            for kind, i, bank, uses in CA.prologue():
                step(0, 0, kind, i, bank, uses)
            value_high(0, 0)
            both(batch)(act)
            for kind, i, bank, uses in CA.epilogue():
                step(BATCH - 1, 1, kind, i, bank, uses)

        @block.vector
        def _(dve):
            for k in range(2):
                dve.memset(vh[k][:, :, CD:CD + 1], SCALE)
                ins = dve.memset(vl[k][:, :, CD:CD + 1], 0.0)
            ins.then_inc(ones, 1)
            dve.wait_ge(kv_loaded, 32)

            def value(b, par, bank, uses):
                dve.wait_ge(full[bank], uses + 1)
                if not first(b):
                    dve.wait_ge(v_low, b)
                dve.tensor_tensor(v[0:CTX], shared[bank][0:CTX, 0:DIM].rearrange("p (h d) -> p h d", h=CH),
                                  rows[0:CTX, 0].rearrange("p (h d) -> p h d", h=CH), ALU.add).then_inc(free[bank], 1)

            def value_low(b, par):
                dve.wait_ge(v_high, b + 1)
                dve.scalar_tensor_tensor(out=vl[par][0:CTX, :, 0:CD], in0=v[0:CTX], scalar=SCALE,
                                         in1=vh[par][0:CTX, :, 0:CD], op0=ALU.mult, op1=ALU.subtract).then_inc(v_low, 1)

            def mask_scores(b, c):
                k = c % 2
                dve.wait_ge(scores, b * UNITS + c + 1)
                if not (first(b) and c < 2):
                    dve.wait_ge(exped, b * UNITS + c - 1)
                s = s_bank[k][:, 0:UH * CTX].rearrange("p (h k) -> p h k", h=UH)
                m = at(mask if additive else limit, b * TPB + c // (UNITS // TPB)).unsqueeze(1).broadcast_to((P, UH, CTX))
                if additive:
                    ins = dve.scalar_tensor_tensor(out=z[k][:], in0=s, scalar=CD ** -0.5, in1=m, op0=ALU.mult, op1=ALU.add)
                else:
                    ins = dve.tensor_tensor(z[k][:], s, m, ALU.min)
                ins.then_inc(masked, 1)
                dve.wait_ge(masked, b * UNITS + c + 1)
                dve.tensor_reduce(top[:, k], z[k][:], AX.X, ALU.max).then_inc(maxed, 1)

            def probs_rest(b, c):
                k = c % 2
                dve.wait_ge(probs_high, b * UNITS + c + 1)
                dve.scalar_tensor_tensor(out=ptl[k][0:CTX], in0=t_bank[k][0:CTX], scalar=PSCALE, in1=pth[k][0:CTX],
                                         op0=ALU.mult, op1=ALU.subtract).then_inc(probs_low, 1)

            def normalise(b, t):
                dve.wait_ge(weighted, b * UNITS + (t + 1) * (UNITS // TPB))
                dve.wait_ge(normed, b * TPB + t)
                dve.reciprocal(inv[:, t], o_bank[t][:, :, CD:CD + 1].squeeze(2)).then_inc(inverted, 1)
                dve.wait_ge(inverted, b * TPB + t + 1)
                if not first(b):
                    wait_read(dve, [("heads", t)], b - 1)
                dve.tensor_tensor(o[:, t], o_bank[t][:, :, 0:CD], inv[:, t].unsqueeze(2).broadcast_to((P, CH, CD)),
                                  ALU.mult).then_inc(normed, 1)

            def residual(b, t, bank, uses):
                dve.wait_ge(full[bank], uses + 1)
                dve.wait_ge(token_sum, b * TPB + t + 1)
                norm.wait_res_free(dve, b)
                dve.tensor_tensor(norm.res[:, t], shared[bank][:, 0:DIM], xb[:, t], ALU.add).then_inc(free[bank], 1)
                dve.wait_ge(free[bank], uses + 1)
                norm.statistics(dve, b, t)

            def batch(b, par, before=True, after=True):
                for c in range(UNITS):
                    if c < UNITS - 1:
                        mask_scores(b, c + 1)
                    elif after:
                        mask_scores(b + 1, 0)
                    for kind, i, bank, uses in CA.slot(c, b):
                        if kind == "value":
                            value(b + 1, 1 - par, bank, uses)
                        if kind == "mix":
                            residual(b + CA.serves(kind, i), i, bank, uses)
                    if c == 0 and before:
                        norm.apply(dve, b - 1, 0, at(X, (b - 1) * TPB))
                    if c == 3 and before:
                        norm.apply(dve, b - 1, 1, at(X, (b - 1) * TPB + 1))
                    probs_rest(b, c)
                    if c == 2 and after:
                        value_low(b + 1, 1 - par)
                    if c == 4:
                        normalise(b, 0)
                    if c == 0 and before:
                        normalise(b - 1, 1)

            for kind, i, bank, uses in CA.prologue():
                if kind == "value":
                    value(0, 0, bank, uses)
            value_low(0, 0)
            dve.wait_ge(mask_loaded, 16)
            if not additive:
                dve.tensor_scalar(limit[:], mask[:], 0, -2 * OPEN, ALU.is_equal, ALU.mult).then_inc(limits, 1)
                dve.wait_ge(limits, 1)
                dve.tensor_scalar(limit[:], limit[:], OPEN, MASKED, ALU.add, ALU.max).then_inc(limits, 1)
                dve.wait_ge(limits, 2)
            mask_scores(0, 0)
            both(batch)(dve)
            norm.apply(dve, BATCH - 1, 0, at(X, (BATCH - 1) * TPB))
            normalise(BATCH - 1, 1)
            for kind, i, bank, uses in CA.epilogue():
                if kind == "mix":
                    residual(BATCH - 1, i, bank, uses)
            norm.apply(dve, BATCH - 1, 1, at(X, (BATCH - 1) * TPB + 1))

        @block.tensor
        def _(pe):
            def step(b, par, kind, i, bank, uses):
                dst = shared[bank]
                if not (isinstance(uses, int) and uses == 0):
                    pe.wait_ge(free[bank], uses)
                if kind == "tokens":
                    pe.wait_ge(staged[par], 8 * (b - par) + 16)
                    for g in range(KT_):
                        for t in range(TPB):
                            ins = pe.transpose(dst[:, g * SEQ + t * P:g * SEQ + (t + 1) * P],
                                               xs[par][:, t, g * P:(g + 1) * P], ident[:])
                elif kind == "query":
                    wait_read(pe, [("tokens", 0)], b)
                    for g in range(KT_):
                        for k in range(KT_):
                            ins = pe.matmul(dst[:, g * SEQ:(g + 1) * SEQ], w[:, 0, k, g * P:(g + 1) * P], xt[par][:, k],
                                            start=(k == 0), stop=(k == KT_ - 1))
                elif kind == "key":
                    pe.wait_ge(context_loaded[par], 8 * (b - par) + 16)
                    for g in range(KT_):
                        for k in range(KT_):
                            ins = pe.matmul(dst[:, g * CTX:(g + 1) * CTX], w[:, 1, k, g * P:(g + 1) * P],
                                            context[par][:, k], start=(k == 0), stop=(k == KT_ - 1))
                elif kind == "value":
                    for k in range(KT_):
                        ins = pe.matmul(dst[0:CTX, 0:DIM], context[par][:, k], w[:, 2, k],
                                        start=(k == 0), stop=(k == KT_ - 1))
                elif kind == "heads":
                    pe.wait_ge(normed, b * TPB + i + 1)
                    for g in range(KT_):
                        ins = pe.transpose(dst[:, g * P:(g + 1) * P],
                                           o[:, i, g * 8:(g + 1) * 8].rearrange("p h d -> p (h d)"), ident[:])
                else:
                    wait_read(pe, [("heads", i)], b)
                    for g in range(KT_):
                        ins = pe.matmul(dst[:, 0:DIM], ot[:, i, g], w[:, 3, g], start=(g == 0), stop=(g == KT_ - 1))
                ins.then_inc(full[bank], 1)

            def score(b, c, par):
                t, part = divmod(c, UNITS // TPB)
                g, h = part // 2, UH * (part % 2)
                if c == 0:
                    wait_read(pe, [("query", 0)], b)
                    pe.wait_ge(key_masked, b + 1)
                if not (first(b) and c < 2):
                    pe.wait_ge(masked, b * UNITS + c - 1)
                pe.matmul(s_bank[c % 2][:, 0:UH * CTX], q[par][:, g, t * P:(t + 1) * P],
                          km[par][:, g, h:h + UH].rearrange("p h k -> p (h k)"), start=True, stop=True).then_inc(scores, 1)

            def turn_probs(b, c):
                k = c % 2
                pe.wait_ge(exped, b * UNITS + c + 1)
                if not (first(b) and c < 2):
                    pe.wait_ge(probs_low, b * UNITS + c - 1)
                for h in range(UH):
                    ins = pe.transpose(t_bank[k][0:CTX, h * P:(h + 1) * P], probs[k][:, h], ident[:])
                ins.then_inc(probs_t, 1)

            def weigh(b, c, par):
                k, t = c % 2, c // (UNITS // TPB)
                pe.wait_ge(probs_low, b * UNITS + c + 1)
                if c == 0:
                    pe.wait_ge(v_low, b + 1)
                if c % (UNITS // TPB) == 0 and not first(b):
                    pe.wait_ge(normed, b * TPB + t - 1)
                for h in range(UH):
                    head = UH * (c % (UNITS // TPB)) + h
                    cols = slice(h * P, (h + 1) * P)
                    for n, (a, x) in enumerate(((pth[k], vh[par]), (pth[k], vl[par]), (ptl[k], vh[par]))):
                        ins = pe.matmul(o_bank[t][:, head, 0:CD + 1], a[0:CTX, cols], x[0:CTX, head],
                                        start=(n == 0), stop=(n == 2))
                ins.then_inc(weighted, 1)

            def batch(b, par, before=True, after=True):
                for c in range(UNITS):
                    if c < UNITS - 1:
                        score(b, c + 1, par)
                    elif after:
                        score(b + 1, 0, 1 - par)
                    for kind, i, bank, uses in CA.slot(c, b):
                        d = CA.serves(kind, i)
                        step(b + d, (par + d) % 2, kind, i, bank, uses)
                    turn_probs(b, c)
                    if c > 0:
                        weigh(b, c - 1, par)
                    elif before:
                        weigh(b - 1, UNITS - 1, 1 - par)

            pe.wait_ge(consts, 2)
            pe.wait_ge(kv_loaded, 32)
            pe.wait_ge(w_loaded, 16)
            for kind, i, bank, uses in CA.prologue():
                step(0, 0, kind, i, bank, uses)
            score(0, 0, 0)
            both(batch)(pe)
            weigh(BATCH - 1, UNITS - 1, 1)
            for kind, i, bank, uses in CA.epilogue():
                step(BATCH - 1, 1, kind, i, bank, uses)

        block_scope.close()
        nc.clear_and_free_semaphores(sems)
        nc.all_engine_barrier()


EXPERTS, FF = 8, 1024
CAP = TOKENS * 5 // (4 * EXPERTS)
MOST = -(-TOKENS // CAP)
SIDE = EXPERTS - 1
SLOTS = (SIDE + MOST + 1) * CAP
ROWS = [P] * (CAP // P) + [CAP % P]
FT = FF // P


def route(nc, router_dram, slots, X, slot, chunks):
    with ExitStack() as ctx:
        def sb(name, shape, dt=F32):
            return ctx.enter_context(nc.sbuf_tensor("rt_" + name, shape, dt))

        def sem(name):
            return ctx.enter_context(nc.semaphore("rt_" + name))

        router = sb("router", [P, KT_, EXPERTS])
        ident = sb("ident", [P, P])
        before = sb("before", [P, P])
        before_bf = sb("before_bf", [P, P], BF16)
        ones_bf = sb("ones_bf", [P, P], BF16)
        ones = sb("ones", [P, TILES])
        code = sb("code", [P, EXPERTS])
        starts = sb("starts", [P, MOST])
        zeros = sb("zeros", [96, 10, DIM])
        xt = [sb(f"xt{k}", [P, KT_, P]) for k in range(2)]
        gap = sb("gap", [P, TILES, EXPERTS])
        power = sb("power", [P, TILES, EXPERTS])
        best = sb("best", [P, TILES])
        pick = sb("pick", [P, TILES, EXPERTS])
        chosen = sb("chosen", [P, TILES])
        onehot = sb("onehot", [P, TILES, EXPERTS])
        onehot_bf = sb("onehot_bf", [P, TILES, EXPERTS], BF16)
        key = sb("key", [P, TILES])
        keys = sb("keys", [P, TOKENS])
        same = sb("same", [P, 2, P])
        ahead = sb("ahead", [P, TILES, TOKENS], BF16)
        own = sb("own", [P, TILES, EXPERTS])
        rank = sb("rank", [P, TILES])
        kept = sb("kept", [P, TILES])
        side = sb("side", [P, TILES])
        base = sb("base", [P, TILES])
        base_bf = sb("base_bf", [P, TILES], BF16)
        upto = sb("upto", [P, TILES])
        place = sb("place", [P, TILES])
        place_side = sb("place_side", [P, TILES])
        over = sb("over", [P, MOST])
        many = sb("many", [P, 1])

        x_bank = [ctx.enter_context(nc.psum_tensor(f"rt_x{k}", [P, KT_, 2 * P], F32)) for k in range(2)]
        l_bank = ctx.enter_context(nc.psum_tensor("rt_logit_bank", [P, TILES, 32], F32))
        k_bank = ctx.enter_context(nc.psum_tensor("rt_key_bank", [P, TOKENS], F32))
        r_bank = ctx.enter_context(nc.psum_tensor("rt_rank_bank", [P, 64, EXPERTS], F32))

        router_loaded = sem("router_loaded")
        consts = sem("consts")
        zero_tile = sem("zero_tile")
        zeroed = sem("zeroed")
        x_turned = sem("x_turned")
        x_ready = sem("x_ready")
        logits = sem("logits")
        step = sem("step")
        gap_ready = sem("gap_ready")
        power_ready = sem("power_ready")
        key_ready = sem("key_ready")
        keys_turned = sem("keys_turned")
        keys_ready = sem("keys_ready")
        diagonal = sem("diagonal")
        compared = sem("compared")
        ranks = sem("ranks")
        base_ready = sem("base_ready")
        counted = sem("counted")
        slots_ready = sem("slots_ready")
        scattered = sem("scattered")

        def logit(pe, j):
            pe.wait_ge(x_ready, j + 1)
            for g in range(KT_):
                ins = pe.matmul(l_bank[:, j, 0:EXPERTS], xt[j % 2][:, g], router[:, g], start=(g == 0), stop=(g == KT_ - 1))
            ins.then_inc(logits, 1)

        block = ctx.enter_context(nc.Block())

        @block.sync
        def _(sp):
            sp.dma_start(router[:], router_dram).then_inc(router_loaded, 16)
            sp.wait_ge(zero_tile, 1)
            rows = 96 * 10
            for n in range(SLOTS // rows):
                sp.dma_start(slots[n * rows:(n + 1) * rows].rearrange("(t p) d -> p t d", p=96), zeros[:]).then_inc(zeroed, 16)

        @block.gpsimd
        def _(pool):
            pool.memset(zeros[:], 0.0).then_inc(zero_tile, 1)
            identity(pool, ident, consts, 1).then_inc(consts, 1)
            pool.memset(before[:], 1.0).then_inc(consts, 1)
            pool.memset(before_bf[:], 1.0).then_inc(consts, 1)
            pool.wait_ge(consts, 4)
            for m in (before, before_bf):
                pool.affine_select(out=m[:], in_=m[:], compare_op=ALU.is_gt, fill=0.0, base=0,
                                   pattern=[[1, P]], channel_multiplier=-1).then_inc(consts, 1)
            pool.memset(ones_bf[:], 1.0).then_inc(consts, 1)
            pool.memset(ones[:], 1.0).then_inc(consts, 1)
            pool.iota(code[:], pattern=[[-1, EXPERTS]], base=EXPERTS, channel_multiplier=0,
                      allow_small_or_imprecise_dtypes=True).then_inc(consts, 1)
            pool.iota(starts[:], pattern=[[CAP, MOST]], base=0, channel_multiplier=0,
                      allow_small_or_imprecise_dtypes=True).then_inc(consts, 1)
            pool.wait_ge(zeroed, 16 * (SLOTS // (96 * 10)))
            pool.wait_ge(slots_ready, 1)
            for j in range(TILES):
                pool.indirect_dma_start(out=slots[:, :], out_offset=bass.IndirectOffsetOnAxis(ap=slot[:, j:j + 1], axis=0),
                                        in_=X[:, j], in_offset=None).then_inc(scattered, 16)
            pool.wait_ge(scattered, 16 * TILES)

        @block.scalar
        def _(act):
            for j in range(TILES):
                act.wait_ge(x_turned, j + 1)
                if j >= 2:
                    act.wait_ge(logits, j - 1)
                act.activation(xt[j % 2][:], x_bank[j % 2][:, :, 0:P], ACT.Copy).then_inc(x_ready, 1)
            act.wait_ge(gap_ready, 1)
            act.activation(power[:], gap[:], ACT.Exp).then_inc(power_ready, 1)
            for n in range(4):
                act.wait_ge(keys_turned, n + 1)
                act.activation(keys[:, n * 512:(n + 1) * 512], k_bank[:, n * 512:(n + 1) * 512], ACT.Copy).then_inc(keys_ready, 1)

        @block.vector
        def _(dve):
            done = [0]

            def then(ins):
                done[0] += 1
                ins.then_inc(step, 1)
                dve.wait_ge(step, done[0])

            def wide(v):
                return v.unsqueeze(2).broadcast_to((P, TILES, EXPERTS))

            codes = code[:].unsqueeze(1).broadcast_to((P, TILES, EXPERTS))
            dve.wait_ge(consts, 10)
            dve.wait_ge(logits, TILES)
            l = l_bank[:, :, 0:EXPERTS]
            then(dve.tensor_reduce(best[:], l, AX.X, ALU.max))
            dve.tensor_tensor(gap[:], l, wide(best[:]), ALU.subtract).then_inc(gap_ready, 1)
            dve.wait_ge(gap_ready, 1)
            then(dve.scalar_tensor_tensor(out=pick[:], in0=gap[:], scalar=0.0, in1=codes, op0=ALU.is_equal, op1=ALU.mult))
            then(dve.tensor_reduce(chosen[:], pick[:], AX.X, ALU.max))
            then(dve.tensor_tensor(onehot[:], codes, wide(chosen[:]), ALU.is_equal))
            then(dve.tensor_copy(onehot_bf[:], onehot[:]))
            dve.wait_ge(power_ready, 1)
            dve.tensor_reduce(key[:], power[:], AX.X, ALU.add).then_inc(key_ready, 1)
            dve.wait_ge(keys_ready, 4)
            dve.wait_ge(key_ready, 1)
            for j in range(TILES):
                k, a, z = key[:, j:j + 1], j * P, (j + 1) * P
                if j:
                    dve.tensor_scalar(ahead[:, j, 0:a], keys[:, 0:a], k, None, ALU.is_gt)
                if j < TILES - 1:
                    dve.tensor_scalar(ahead[:, j, z:], keys[:, z:], k, None, ALU.is_ge)
                if j >= 2:
                    dve.wait_ge(compared, j - 1)
                dve.scalar_tensor_tensor(out=same[:, j % 2], in0=keys[:, a:z], scalar=k, in1=before[:],
                                         op0=ALU.is_equal, op1=ALU.mult).then_inc(diagonal, 1)
                dve.wait_ge(diagonal, j + 1)
                dve.scalar_tensor_tensor(out=ahead[:, j, a:z], in0=keys[:, a:z], scalar=k, in1=same[:, j % 2],
                                         op0=ALU.is_gt, op1=ALU.add).then_inc(compared, 1)
            dve.wait_ge(ranks, 1)
            then(dve.tensor_tensor(own[:], r_bank[:, 0:TILES], onehot[:], ALU.mult))
            then(dve.tensor_reduce(rank[:], own[:], AX.X, ALU.add))
            then(dve.tensor_scalar(kept[:], rank[:], float(CAP), None, ALU.is_lt))
            then(dve.tensor_scalar(side[:], onehot[:, :, 0], -1.0, 1.0, ALU.mult, ALU.add))
            then(dve.tensor_tensor(side[:], side[:], kept[:], ALU.mult))
            then(dve.tensor_scalar(base[:], side[:], -1.0, 1.0, ALU.mult, ALU.add))
            dve.tensor_copy(base_bf[:], base[:]).then_inc(base_ready, 1)
            then(dve.tensor_scalar(place_side[:], chosen[:], -float(CAP), float(CAP * SIDE), ALU.mult, ALU.add))
            then(dve.tensor_tensor(place_side[:], place_side[:], rank[:], ALU.add))
            then(dve.tensor_tensor(place_side[:], place_side[:], side[:], ALU.mult))
            dve.wait_ge(counted, 1)
            total = r_bank[:, 32:34].rearrange("p a e -> p (a e)")
            then(dve.tensor_tensor_scan(upto[:], ones[:], total, 0.0, ALU.mult, ALU.add))
            then(dve.tensor_tensor(place[:], r_bank[:, 48:50].rearrange("p a e -> p (a e)"), upto[:], ALU.add))
            then(dve.tensor_tensor(place[:], total, place[:], ALU.subtract))
            then(dve.tensor_scalar(place[:], place[:], -1.0, float(SIDE * CAP), ALU.mult, ALU.add))
            then(dve.tensor_tensor(place[:], place[:], base[:], ALU.mult))
            dve.tensor_tensor(slot[:], place[:], place_side[:], ALU.add).then_inc(slots_ready, 1)
            then(dve.tensor_scalar(over[:], starts[:], upto[:, TILES - 1:TILES], None, ALU.is_lt))
            then(dve.tensor_reduce(many[:], over[:], AX.X, ALU.add))
            then(dve.tensor_scalar(chunks[:], many[:], 1.0, None, ALU.max))

        @block.tensor
        def _(pe):
            pe.wait_ge(consts, 2)
            pe.wait_ge(router_loaded, 16)
            for j in range(TILES):
                if j >= 2:
                    pe.wait_ge(x_ready, j - 1)
                for g in range(KT_):
                    ins = pe.transpose(x_bank[j % 2][:, g, 0:P], X[:, j, g * P:(g + 1) * P], ident[:])
                ins.then_inc(x_turned, 1)
                if j:
                    logit(pe, j - 1)
            logit(pe, TILES - 1)
            pe.wait_ge(key_ready, 1)
            for j in range(TILES):
                ins = pe.transpose(k_bank[:, j * P:(j + 1) * P], key[:, j:j + 1].broadcast_to((P, P)), ident[:])
                if j % 4 == 3:
                    ins.then_inc(keys_turned, 1)
            pe.wait_ge(compared, TILES)
            for i in range(TILES):
                for j in range(TILES):
                    ins = pe.matmul(r_bank[:, i], ahead[:, j, i * P:(i + 1) * P], onehot_bf[:, j],
                                    start=(j == 0), stop=(j == TILES - 1))
            ins.then_inc(ranks, 1)
            pe.wait_ge(consts, 10)
            pe.wait_ge(base_ready, 1)
            pe.matmul(r_bank[:, 32:34].rearrange("p a e -> p (a e)"), ones_bf[:], base_bf[:], start=True, stop=True)
            pe.matmul(r_bank[:, 48:50].rearrange("p a e -> p (a e)"), before_bf[:], base_bf[:], start=True, stop=True).then_inc(counted, 1)


def experts(nc, router_dram, w1_dram, b1_dram, w2_dram, b2_dram, X):
    slots = nc.dram_tensor("slots", (SLOTS, DIM), F32, kind="Internal").ap()
    with ExitStack() as ctx:
        def sb(name, shape, dt=F32):
            return ctx.enter_context(nc.sbuf_tensor("ex_" + name, shape, dt))

        def sem(name):
            return ctx.enter_context(nc.semaphore("ex_" + name))

        slot = sb("slot", [P, TILES], I32)
        chunks = sb("chunks", [P, 1], I32)
        route(nc, router_dram, slots, X, slot, chunks)

        w1 = [sb(f"w1{k}", [P, KT_, FF]) for k in range(2)]
        w2 = [sb(f"w2{k}", [P, FT, DIM]) for k in range(2)]
        b1 = [sb(f"b1{k}", [P, FT]) for k in range(2)]
        b2 = [sb(f"b2{k}", [P, DIM]) for k in range(2)]
        xe = [sb(f"xe{k}", [P, len(ROWS), DIM]) for k in range(2)]
        xt = [sb(f"xt{k}", [P, KT_, CAP]) for k in range(2)]
        h = [sb(f"h{k}", [P, FT, CAP]) for k in range(2)]
        y = [sb(f"y{k}", [P, len(ROWS), DIM]) for k in range(2)]
        yg = sb("yg", [P, TILES, DIM])
        stats = sb("stats", [P, TILES, 6])
        mv = sb("mv", [P, TILES, 2])
        var_eps = sb("var_eps", [P, TILES])
        rstd = sb("rstd", [P, TILES])
        half = sb("half", [P, 1])
        mark = sb("mark", [1, 2], I32)
        ident = sb("ident", [P, P])

        x_bank = ctx.enter_context(nc.psum_tensor("ex_x", [P, 512], F32))
        u_bank = [ctx.enter_context(nc.psum_tensor(f"ex_up{k}", [P, 512], F32)) for k in range(4)]
        d_bank = [ctx.enter_context(nc.psum_tensor(f"ex_down{k}", [P, 512], F32)) for k in range(3)]

        consts = sem("consts")
        w1_loaded = [sem("w1_loaded0"), sem("w1_loaded1")]
        w2_loaded = [sem("w2_loaded0"), sem("w2_loaded1")]
        x_loaded = [sem("x_loaded0"), sem("x_loaded1")]
        stored = [sem("stored0"), sem("stored1")]
        all_stored = sem("all_stored")
        all_loaded = sem("all_loaded")
        x_turned = sem("x_turned")
        x_ready = sem("x_ready")
        up = sem("up")
        hidden = sem("hidden")
        down = sem("down")
        y_ready = sem("y_ready")
        gathered = [sem(f"gathered{n}") for n in range(4)]
        summed = sem("summed")
        stat = sem("stat")
        mean_var = sem("mean_var")
        var_ready = sem("var_ready")
        rstd_ready = sem("rstd_ready")
        normed = sem("normed")
        NR = len(ROWS)

        def side_items(engine, work):
            work(0, 0, "up", 1, 1)
            work(1, 1, "up", 1, 1)
            work(0, 0, "down", 1, 1)
            with engine.Fori(0, SIDE // 2 - 1) as i:
                work(2 * i + 2, 0, "up", i + 2, i + 2)
                work(2 * i + 1, 1, "down", i + 1, i + 1)
                work(2 * i + 3, 1, "up", i + 2, i + 2)
                work(2 * i + 2, 0, "down", i + 2, i + 2)
            work(SIDE - 1, 0, "up", SIDE // 2 + 1, SIDE // 2 + 1)
            work(SIDE - 2, 1, "down", SIDE // 2, SIDE // 2)
            work(SIDE - 1, 0, "down", SIDE // 2 + 1, SIDE // 2 + 1)

        def base_items(engine, work):
            count = engine.value_load(chunks[0:1, 0:1], min_val=1, max_val=MOST)
            with engine.Fori(0, count) as c:
                work(c + SIDE, 1, "up", c + SIDE // 2 + 1, SIDE // 2 + 1)
                work(c + SIDE, 1, "down", c + SIDE // 2 + 1, SIDE // 2 + 1)

        block = ctx.enter_context(nc.Block())

        @block.sync
        def _(sp):
            def one(dram, it):
                return dram[it] if isinstance(it, int) else dram[bass.ds(it, 1)].squeeze(0)

            def load_w1(it, k):
                sp.dma_start(w1[k][:], one(w1_dram, it)).then_inc(w1_loaded[k], 16)
                sp.dma_start(b1[k][:], one(b1_dram, it)).then_inc(w1_loaded[k], 16)

            def load_w2(it, k):
                sp.dma_start(w2[k][:], one(w2_dram, it)).then_inc(w2_loaded[k], 16)
                sp.dma_start(b2[k][:], one(b2_dram, it)).then_inc(w2_loaded[k], 16)

            def load_x(it, k):
                full_tiles = P * (NR - 1)
                sp.dma_start(xe[k][:, 0:NR - 1], slots[bass.ds(it * CAP, full_tiles)].rearrange("(t p) d -> p t d", p=P)).then_inc(x_loaded[k], 16)
                sp.dma_start(xe[k][0:ROWS[-1], NR - 1], slots[bass.ds(it * CAP + full_tiles, ROWS[-1])]).then_inc(x_loaded[k], 16)

            def store(it, k):
                full_tiles = P * (NR - 1)
                sp.wait_ge(y_ready, (it + 1) * NR)
                sp.dma_start(slots[bass.ds(it * CAP, full_tiles)].rearrange("(t p) d -> p t d", p=P), y[k][:, 0:NR - 1]).then_inc(stored[k], 16)
                sp.dma_start(slots[bass.ds(it * CAP + full_tiles, ROWS[-1])], y[k][0:ROWS[-1], NR - 1]).then_inc(stored[k], 16)

            for it in (0, 1):
                load_x(it, it)
                load_w1(it, it)
                load_w2(it, it)

            def side(it, k, stage, more=True):
                if stage == "up" and more:
                    sp.wait_ge(x_turned, (it + 1) * KT_)
                    load_x(it + 2, k)
                    sp.wait_ge(up, (it + 1) * FT)
                    sp.wait_ge(hidden, (it + 1) * FT)
                    load_w1(it + 2, k)
                if stage == "down":
                    store(it, k)
                    if more:
                        sp.wait_ge(down, (it + 1) * NR)
                        load_w2(it + 2, k)

            side(0, 0, "up")
            with sp.Fori(0, SIDE // 2 - 1) as i:
                side(2 * i + 1, 1, "up")
                side(2 * i, 0, "down")
                side(2 * i + 2, 0, "up")
                side(2 * i + 1, 1, "down")
            side(SIDE - 2, 1, "up")
            side(SIDE - 3, 0, "down")
            side(SIDE - 2, 1, "down")
            side(SIDE - 1, 0, "down", more=False)
            count = sp.value_load(chunks[0:1, 0:1], min_val=1, max_val=MOST)
            with sp.Fori(0, count) as c:
                sp.wait_ge(x_turned, (c + SIDE + 1) * KT_)
                load_x(c + SIDE + 1, 1)
                store(c + SIDE, 1)
            sp.wait_ge(stored[1], count * 32 + 32 * (SIDE // 2))
            sp.dma_start(mark[0:1, 0:1], chunks[0:1, 0:1]).then_inc(all_stored, 16)
            sp.wait_ge(x_loaded[1], count * 32 + 32 * (SIDE // 2 + 1))
            sp.dma_start(mark[0:1, 1:2], chunks[0:1, 0:1]).then_inc(all_loaded, 16)
            sp.wait_ge(all_loaded, 16)

        @block.gpsimd
        def _(pool):
            identity(pool, ident, consts, 1).then_inc(consts, 1)
            pool.memset(half[:], -0.5).then_inc(consts, 1)
            pool.wait_ge(consts, 3)
            pool.wait_ge(stored[0], 32 * (SIDE // 2 + 1))
            pool.wait_ge(all_stored, 16)
            for j in range(TILES):
                pool.indirect_dma_start(out=yg[:, j], out_offset=None, in_=slots[:, :],
                                        in_offset=bass.IndirectOffsetOnAxis(ap=slot[:, j:j + 1], axis=0)).then_inc(gathered[j // 4], 16)
            for n in range(4):
                pool.wait_ge(var_ready, n + 1)
                pool.tensor_tensor(rstd[:, 4 * n:4 * n + 4], var_eps[:, 4 * n:4 * n + 4], half[:].broadcast_to((P, 4)), ALU.pow).then_inc(rstd_ready, 1)

        @block.scalar
        def _(act):
            def work(it, k, stage, xs, ws):
                if stage == "down":
                    return
                for g in range(KT_):
                    act.wait_ge(x_turned, it * KT_ + g + 1)
                    act.activation(xt[k][:, g], x_bank[:, 0:CAP], ACT.Copy).then_inc(x_ready, 1)
                for m in range(FT):
                    act.wait_ge(up, it * FT + m + 1)
                    act.activation(h[k][:, m], u_bank[m % 4][:, 0:CAP], ACT.Relu, bias=b1[k][:, m:m + 1]).then_inc(hidden, 1)

            side_items(act, work)
            base_items(act, work)

        @block.vector
        def _(dve):
            def work(it, k, stage, xs, ws):
                if stage == "up":
                    return
                if not first(it):
                    dve.wait_ge(stored[k], xs * 32 - 32)
                for s, rows in enumerate(ROWS):
                    dve.wait_ge(down, it * NR + s + 1)
                    dve.tensor_tensor(y[k][0:rows, s], d_bank[s][0:rows, 0:DIM], b2[k][0:rows], ALU.add).then_inc(y_ready, 1)

            side_items(dve, work)
            base_items(dve, work)
            for n in range(4):
                t = slice(4 * n, 4 * n + 4)
                dve.wait_ge(gathered[n], 64)
                dve.tensor_tensor(yg[:, t], yg[:, t], X[:, t], ALU.add).then_inc(summed, 1)
                dve.wait_ge(summed, n + 1)
                for j in range(4 * n, 4 * n + 4):
                    ins = dve.bn_stats(stats[:, j], yg[:, j])
                ins.then_inc(stat, 1)
                dve.wait_ge(stat, n + 1)
                for j in range(4 * n, 4 * n + 4):
                    ins = dve.bn_aggr(mv[:, j], stats[:, j])
                ins.then_inc(mean_var, 1)
                dve.wait_ge(mean_var, n + 1)
                dve.tensor_scalar(var_eps[:, t], mv[:, t, 1], EPS, None, ALU.add).then_inc(var_ready, 1)
                dve.wait_ge(rstd_ready, n + 1)
                for j in range(4 * n, 4 * n + 4):
                    dve.tensor_scalar(X[:, j], yg[:, j], mv[:, j, 0:1], rstd[:, j:j + 1], ALU.subtract, ALU.mult).then_inc(normed, 1)

        @block.tensor
        def _(pe):
            pe.wait_ge(consts, 2)

            def work(it, k, stage, xs, ws):
                if stage == "up":
                    pe.wait_ge(x_loaded[k], xs * 32)
                    for g in range(KT_):
                        if not (first(it) and g == 0):
                            pe.wait_ge(x_ready, it * KT_ + g)
                        for s, rows in enumerate(ROWS):
                            ins = pe.transpose(x_bank[:, s * P:s * P + rows], xe[k][0:rows, s, g * P:(g + 1) * P], ident[0:rows, 0:rows])
                        ins.then_inc(x_turned, 1)
                    pe.wait_ge(x_ready, it * KT_ + KT_)
                    pe.wait_ge(w1_loaded[k], ws * 32)
                    for m in range(FT):
                        if not (first(it) and m < 4):
                            pe.wait_ge(hidden, it * FT + m - 3)
                        for g in range(KT_):
                            ins = pe.matmul(u_bank[m % 4][:, 0:CAP], w1[k][:, g, m * P:(m + 1) * P], xt[k][:, g],
                                            start=(g == 0), stop=(g == KT_ - 1))
                        ins.then_inc(up, 1)
                else:
                    pe.wait_ge(w2_loaded[k], ws * 32)
                    pe.wait_ge(hidden, it * FT + FT)
                    for s, rows in enumerate(ROWS):
                        if not first(it):
                            pe.wait_ge(y_ready, it * NR + s - NR + 1)
                        for m in range(FT):
                            ins = pe.matmul(d_bank[s][0:rows, 0:DIM], h[k][:, m, s * P:s * P + rows], w2[k][:, m],
                                            start=(m == 0), stop=(m == FT - 1))
                        ins.then_inc(down, 1)

            side_items(pe, work)
            base_items(pe, work)


HID = 512
HT = HID // P
TAPS = 4
SERIES = 9


def recurrence(nc, w_in_dram, w_g_dram, w_out_dram, hid_dram, X):
    with ExitStack() as ctx:
        def sb(name, shape, dt=F32):
            return ctx.enter_context(nc.sbuf_tensor("re_" + name, shape, dt))

        def sem(name):
            return ctx.enter_context(nc.semaphore("re_" + name))

        w_in = sb("w_in", [P, KT_, 2 * HID])
        w_g = sb("w_g", [P, HT, 2 * HID])
        w_out = sb("w_out", [P, HT, DIM])
        hid = sb("hid", [P, TAPS + 4, HT])
        half_bias = sb("half_bias", [P, 2, HT])
        rate = sb("rate", [P, HT])
        low, power = sb("low", [P, HT]), sb("power", [P, HT])
        ratio, square, series = sb("ratio", [P, HT]), sb("square", [P, HT]), sb("series", [P, HT])
        tiny = sb("tiny", [P, 1])
        ident = sb("ident", [P, P])
        xs = [sb(f"xs{k}", [P, TPB, DIM]) for k in range(2)]
        xt = sb("xt", [P, KT_, SEQ])
        padded = sb("padded", [P, HT, TAPS - 1 + SEQ])
        conv = [sb(f"conv{k}", [P, HT, SEQ]) for k in range(2)]
        gate = [sb(f"gate{k}", [P, HT, SEQ]) for k in range(2)]
        tf = sb("tf", [P, 2, SEQ])
        ti = [sb(f"ti{p}", [P, 2, SEQ]) for p in range(2)]
        T = [sb(f"T{p}", [P, 2, SEQ]) for p in range(2)]
        more = [sb(f"more{p}", [P, 2, SEQ]) for p in range(2)]
        recip = [sb(f"recip{p}", [P, 2, SEQ]) for p in range(2)]
        d = [sb(f"d{p}", [P, 2, SEQ]) for p in range(2)]
        nb = [sb(f"nb{p}", [P, 2, SEQ]) for p in range(2)]
        alpha = [sb(f"alpha{p}", [P, 2, SEQ]) for p in range(2)]
        beta = [sb(f"beta{p}", [P, 2, SEQ]) for p in range(2)]
        scaled = [sb(f"scaled{p}", [P, 2, SEQ]) for p in range(2)]
        bterm = [sb(f"bterm{p}", [P, 2, SEQ]) for p in range(2)]
        h = [sb(f"h{p}", [P, 2, SEQ]) for p in range(2)]
        gh = sb("gh", [P, HT, SEQ])

        x_bank = ctx.enter_context(nc.psum_tensor("re_x", [P, KT_, SEQ], F32))
        i_bank = [ctx.enter_context(nc.psum_tensor(f"re_in{k}", [P, 2, SEQ], F32)) for k in range(2)]
        g_bank = [ctx.enter_context(nc.psum_tensor(f"re_g{m}", [P, 2, SEQ], F32)) for m in range(HT)]
        o_bank = ctx.enter_context(nc.psum_tensor("re_out", [P, TPB, DIM], F32))

        norm = Norm(ctx, nc, "re")
        hid_loaded = sem("hid_loaded")
        in_loaded = sem("in_loaded")
        g_loaded = sem("g_loaded")
        out_loaded = sem("out_loaded")
        staged = [sem("staged0"), sem("staged1")]
        consts = sem("consts")
        setup = sem("setup")
        setup_act = sem("setup_act")
        x_turned = sem("x_turned")
        x_ready = sem("x_ready")
        in_done = sem("in_done")
        in_read = sem("in_read")
        conved = sem("conved")
        g_done = sem("g_done")
        tf_done = sem("tf_done")
        ti_done = sem("ti_done")
        T_done = sem("T_done")
        chain = sem("chain")
        beta_ready = sem("beta_ready")
        doubled = sem("doubled")
        scaled_ready = sem("scaled_ready")
        bterm_ready = sem("bterm_ready")
        scanned = sem("scanned")
        gated = sem("gated")
        out_done = sem("out_done")
        summed = sem("summed")

        def both(batch):
            def run(engine):
                batch(0, 0, before=False)
                with engine.Fori(0, BATCH // 2 - 1) as i:
                    batch(2 * i + 1, 1)
                    batch(2 * i + 2, 0)
                batch(BATCH - 1, 1, after=False)
            return run

        block = ctx.enter_context(nc.Block())

        @block.sync
        def _(sp):
            def stage(b, par):
                sp.dma_start(xs[par][:], X[:, bass.ds(b * TPB, TPB)]).then_inc(staged[par], 16)

            stage(0, 0)
            sp.dma_start(hid[:], hid_dram).then_inc(hid_loaded, 16)
            sp.dma_start(w_in[:], w_in_dram).then_inc(in_loaded, 16)
            stage(1, 1)
            sp.dma_start(w_g[:], w_g_dram).then_inc(g_loaded, 16)
            sp.dma_start(w_out[:], w_out_dram).then_inc(out_loaded, 16)
            for b in (0, 1):
                sp.wait_ge(x_turned, b + 1)
                stage(b + 2, b)
            with sp.Fori(1, BATCH // 2 - 1) as i:
                for par in range(2):
                    sp.wait_ge(x_turned, 2 * i + par + 1)
                    stage(2 * i + par + 2, par)

        @block.gpsimd
        def _(pool):
            identity(pool, ident, consts, 1).then_inc(consts, 1)
            pool.memset(tiny[:], 0.25e-6).then_inc(consts, 1)
            pool.memset(norm.half[:], -0.5).then_inc(consts, 1)
            pool.wait_ge(consts, 4)

            def scale_input(b, par, p):
                c = conv[par][:, 2 * p:2 * p + 2]
                pool.wait_ge(ti_done, b * HT + 2 * p + 2)
                if not first(b):
                    pool.wait_ge(bterm_ready, 2 * b + p - 1)
                pool.tensor_tensor(scaled[p][:], ti[p][:], c, ALU.mult).then_inc(doubled, 1)
                pool.wait_ge(doubled, 2 * b + p + 1)
                pool.tensor_tensor(scaled[p][:], scaled[p][:], c, ALU.add).then_inc(scaled_ready, 1)

            def times_beta(b, p):
                pool.wait_ge(scaled_ready, 2 * b + p + 1)
                pool.wait_ge(beta_ready, 2 * b + p + 1)
                if not first(b):
                    pool.wait_ge(scanned, 2 * b + p - 1)
                pool.tensor_tensor(bterm[p][:], scaled[p][:], beta[p][:], ALU.mult).then_inc(bterm_ready, 1)

            def batch(b, par, before=True, after=True):
                if before:
                    times_beta(b - 1, 1)
                    norm.root(pool, b - 1, 0)
                    norm.root(pool, b - 1, 1)
                scale_input(b, par, 0)
                times_beta(b, 0)
                scale_input(b, par, 1)

            both(batch)(pool)
            times_beta(BATCH - 1, 1)
            norm.root(pool, BATCH - 1, 0)
            norm.root(pool, BATCH - 1, 1)

        @block.scalar
        def _(act):
            act.wait_ge(setup, 1)
            act.activation(power[:], low[:], ACT.Exp).then_inc(setup_act, 1)
            act.wait_ge(setup, 2 * SERIES + 9)
            act.wait_ge(consts, 3)

            def tokens(b):
                act.wait_ge(x_turned, b + 1)
                act.activation(xt[:], x_bank[:], ACT.Copy).then_inc(x_ready, 1)

            def conv_input(b):
                if not first(b):
                    act.wait_ge(conved, b * TAPS * HT)
                for p in range(2):
                    act.wait_ge(in_done, 4 * b + p + 1)
                    act.activation(padded[:, 2 * p:2 * p + 2, TAPS - 1:], i_bank[p][:], ACT.Copy).then_inc(in_read, 1)

            def gates(b, par):
                if not (isinstance(b, int) and b < 2):
                    act.wait_ge(gated, 2 * b - 2)
                for p in range(2):
                    act.wait_ge(in_done, 4 * b + 2 + p + 1)
                    act.activation(gate[par][:, 2 * p:2 * p + 2], i_bank[p][:], ACT.Gelu).then_inc(in_read, 1)

            def tile(b, m):
                p, k = divmod(m, 2)
                act.wait_ge(g_done, b * HT + m + 1)
                if not (first(b) and m < 2):
                    act.wait_ge(T_done, b * HT + m - 1)
                act.activation(tf[:, k], g_bank[m][:, 0], ACT.Tanh, scale=0.5, bias=half_bias[:, 0, m:m + 1]).then_inc(tf_done, 1)
                if not first(b):
                    act.wait_ge(scaled_ready, 2 * b + p - 1)
                act.activation(ti[p][:, k], g_bank[m][:, 1], ACT.Tanh, scale=0.5, bias=half_bias[:, 1, m:m + 1]).then_inc(ti_done, 1)
                act.wait_ge(tf_done, b * HT + m + 1)
                if not first(b):
                    act.wait_ge(chain, 10 * b + 5 * p - 7)
                act.activation(T[p][:, k], tf[:, k], ACT.Tanh, scale=rate[:, m:m + 1], bias=rate[:, m:m + 1]).then_inc(T_done, 1)

            def root(b, p):
                act.wait_ge(chain, 10 * b + 5 * p + 4)
                if not first(b):
                    act.wait_ge(bterm_ready, 2 * b + p - 1)
                act.activation(beta[p][:], nb[p][:], ACT.Sqrt, scale=-0.25, bias=tiny[:]).then_inc(beta_ready, 1)

            def batch(b, par, before=True, after=True):
                if after:
                    tokens(b + 1)
                    conv_input(b + 1)
                if before:
                    root(b - 1, 1)
                tile(b, 0)
                if after:
                    gates(b + 1, 1 - par)
                tile(b, 1)
                tile(b, 2)
                root(b, 0)
                tile(b, 3)

            tokens(0)
            conv_input(0)
            gates(0, 0)
            both(batch)(act)
            root(BATCH - 1, 1)

        @block.vector
        def _(dve):
            done = [0]

            def then(ins):
                done[0] += 1
                ins.then_inc(setup, 1)
                dve.wait_ge(setup, done[0])

            base = hid[:, TAPS + 3]
            dve.wait_ge(hid_loaded, 16)
            then(dve.scalar_tensor_tensor(out=low[:], in0=base, scalar=-1.0, in1=base, op0=ALU.mult, op1=ALU.min))
            dve.wait_ge(setup_act, 1)
            then(dve.tensor_scalar(ratio[:], power[:], 2.0, None, ALU.add))
            then(dve.reciprocal(square[:], ratio[:]))
            then(dve.tensor_tensor(ratio[:], power[:], square[:], ALU.mult))
            then(dve.tensor_tensor(square[:], ratio[:], ratio[:], ALU.mult))
            then(dve.memset(series[:], 1.0 / (2 * SERIES + 1)))
            for n in reversed(range(SERIES)):
                then(dve.tensor_tensor(series[:], series[:], square[:], ALU.mult))
                then(dve.tensor_scalar(series[:], series[:], 1.0 / (2 * n + 1), None, ALU.add))
            then(dve.scalar_tensor_tensor(out=series[:], in0=ratio[:], scalar=2.0, in1=series[:], op0=ALU.mult, op1=ALU.mult))
            then(dve.scalar_tensor_tensor(out=rate[:], in0=base, scalar=0.0, in1=series[:], op0=ALU.max, op1=ALU.add))
            dve.tensor_scalar(rate[:], rate[:], 2.0, None, ALU.mult)
            dve.memset(padded[:, :, 0:TAPS - 1], 0.0)
            then(dve.tensor_scalar(half_bias[:], hid[:, TAPS + 1:TAPS + 3], 0.5, None, ALU.mult))

            def convolve(b, par, p):
                dve.wait_ge(in_read, 4 * b + p + 1)
                if not (isinstance(b, int) and b < 2):
                    dve.wait_ge(scaled_ready, 2 * b - 2)
                for tap in range(TAPS):
                    for k in range(2):
                        m = 2 * p + k
                        out, x, w = conv[par][:, m], padded[:, m, tap:tap + SEQ], hid[:, tap, m:m + 1]
                        if tap == 0:
                            ins = dve.tensor_scalar(out, x, w, hid[:, TAPS, m:m + 1], ALU.mult, ALU.add)
                        else:
                            dve.wait_ge(conved, b * TAPS * HT + TAPS * 2 * p + 2 * tap + k - 1)
                            ins = dve.scalar_tensor_tensor(out=out, in0=x, scalar=w, in1=out, op0=ALU.mult, op1=ALU.add)
                        ins.then_inc(conved, 1)

            def decay(b, p):
                n = 10 * b + 5 * p
                dve.wait_ge(T_done, b * HT + 2 * p + 2)
                dve.tensor_scalar(more[p][:], T[p][:], 1.0, None, ALU.add).then_inc(chain, 1)
                dve.wait_ge(chain, n + 1)
                dve.reciprocal(recip[p][:], more[p][:]).then_inc(chain, 1)
                dve.wait_ge(chain, n + 2)
                dve.scalar_tensor_tensor(out=d[p][:], in0=T[p][:], scalar=2.0, in1=recip[p][:], op0=ALU.mult, op1=ALU.mult).then_inc(chain, 1)
                dve.wait_ge(chain, n + 3)
                dve.scalar_tensor_tensor(out=nb[p][:], in0=d[p][:], scalar=-2.0, in1=d[p][:], op0=ALU.add, op1=ALU.mult).then_inc(chain, 1)
                dve.tensor_scalar(alpha[p][:], d[p][:], -1.0, 1.0, ALU.mult, ALU.add).then_inc(chain, 1)

            def scan(b, par, p):
                dve.wait_ge(bterm_ready, 2 * b + p + 1)
                dve.wait_ge(chain, 10 * b + 5 * p + 5)
                if not first(b):
                    dve.wait_ge(gated, 2 * b + p - 1)
                for k in range(2):
                    ins = dve.tensor_tensor_scan(h[p][:, k], alpha[p][:, k], bterm[p][:, k], 0.0, ALU.mult, ALU.add)
                ins.then_inc(scanned, 1)
                dve.wait_ge(scanned, 2 * b + p + 1)
                dve.wait_ge(in_read, 4 * b + 4)
                dve.tensor_tensor(gh[:, 2 * p:2 * p + 2], gate[par][:, 2 * p:2 * p + 2], h[p][:], ALU.mult).then_inc(gated, 1)

            def residual(b):
                dve.wait_ge(out_done, b + 1)
                for t in range(TPB):
                    norm.wait_res_free(dve, b)
                    dve.tensor_tensor(norm.res[:, t], o_bank[:, t], at(X, b * TPB + t), ALU.add).then_inc(summed, 1)
                    dve.wait_ge(summed, b * TPB + t + 1)
                    norm.statistics(dve, b, t)

            def layer_norm(b):
                for t in range(TPB):
                    norm.apply(dve, b, t, at(X, b * TPB + t))

            def batch(b, par, before=True, after=True):
                if after:
                    convolve(b + 1, 1 - par, 0)
                if before:
                    scan(b - 1, 1 - par, 1)
                if after:
                    convolve(b + 1, 1 - par, 1)
                if before:
                    residual(b - 1)
                decay(b, 0)
                if before:
                    layer_norm(b - 1)
                scan(b, par, 0)
                decay(b, 1)

            convolve(0, 0, 0)
            convolve(0, 0, 1)
            both(batch)(dve)
            scan(BATCH - 1, 1, 1)
            residual(BATCH - 1)
            layer_norm(BATCH - 1)

        @block.tensor
        def _(pe):
            def way_in(b, par):
                pe.wait_ge(staged[par], 8 * (b - par) + 16)
                if not first(b):
                    pe.wait_ge(x_ready, b)
                for g in range(KT_):
                    for t in range(TPB):
                        ins = pe.transpose(x_bank[:, g, t * P:(t + 1) * P], xs[par][:, t, g * P:(g + 1) * P], ident[:])
                ins.then_inc(x_turned, 1)
                pe.wait_ge(x_ready, b + 1)
                for s in range(4):
                    if not (first(b) and s < 2):
                        pe.wait_ge(in_read, 4 * b + s - 1)
                    for k in range(2):
                        m = (HT + 2 * s + k) % (2 * HT)
                        for g in range(KT_):
                            ins = pe.matmul(i_bank[s % 2][:, k], w_in[:, g, m * P:(m + 1) * P], xt[:, g],
                                            start=(g == 0), stop=(g == KT_ - 1))
                    ins.then_inc(in_done, 1)

            def tile(b, par, m):
                if m == 0:
                    pe.wait_ge(conved, (b + 1) * TAPS * HT)
                if not first(b):
                    pe.wait_ge(ti_done, b * HT + m - HT + 1)
                for k in range(2):
                    cols = slice(k * HID + m * P, k * HID + (m + 1) * P)
                    for j in range(HT):
                        ins = pe.matmul(g_bank[m][:, k], w_g[:, j, cols], conv[par][:, j], start=(j == 0), stop=(j == HT - 1))
                ins.then_inc(g_done, 1)

            def way_out(b):
                pe.wait_ge(gated, 2 * b + 2)
                if not first(b):
                    pe.wait_ge(summed, b * TPB)
                for t in range(TPB):
                    for j in range(HT):
                        ins = pe.matmul(o_bank[:, t], gh[:, j, t * P:(t + 1) * P], w_out[:, j], start=(j == 0), stop=(j == HT - 1))
                ins.then_inc(out_done, 1)

            def batch(b, par, before=True, after=True):
                if after:
                    way_in(b + 1, 1 - par)
                tile(b, par, 0)
                if before:
                    way_out(b - 1)
                for m in range(1, HT):
                    tile(b, par, m)

            pe.wait_ge(consts, 2)
            pe.wait_ge(in_loaded, 16)
            way_in(0, 0)
            pe.wait_ge(g_loaded, 16)
            pe.wait_ge(out_loaded, 16)
            both(batch)(pe)
            way_out(BATCH - 1)


HSCALE = 16.0


def binary_ffn(nc, w1_dram, w2_dram, b1_dram, b2_dram, X, out):
    with ExitStack() as ctx:
        def sb(name, shape, dt=F32):
            return ctx.enter_context(nc.sbuf_tensor("bf_" + name, shape, dt))

        def sem(name):
            return ctx.enter_context(nc.semaphore("bf_" + name))

        w1 = sb("w1", [P, KT_, FF])
        w2 = sb("w2", [P, FT, DIM])
        size1, size2 = sb("size1", [P, KT_, FF]), sb("size2", [P, FT, DIM])
        below1, below2 = sb("below1", [P, KT_, FF], F16), sb("below2", [P, FT, DIM], F16)
        sign1, sign2 = sb("sign1", [P, KT_, FF], F16), sb("sign2", [P, FT, DIM], F16)
        alpha1 = sb("alpha1", [P, FT])
        alpha2 = sb("alpha2", [P, DIM])
        b1 = sb("b1", [P, FT])
        b2 = sb("b2", [P, DIM])
        ones = sb("ones", [P, P])
        ident = sb("ident", [P, P])
        xs = [sb(f"xs{k}", [P, TPB, DIM]) for k in range(2)]
        xb = [sb(f"xb{k}", [P, TPB, DIM]) for k in range(2)]
        xh = [sb(f"xh{k}", [P, KT_, SEQ], F16) for k in range(2)]
        xl = [sb(f"xl{k}", [P, KT_, SEQ], F16) for k in range(2)]
        h = sb("h", [P, FT, SEQ])
        hh = [sb(f"hh{k}", [P, FT, SEQ], F16) for k in range(2)]
        hl = [sb(f"hl{k}", [P, FT, SEQ], F16) for k in range(2)]
        scaled = sb("scaled", [P, TPB, DIM])
        y = [sb(f"y{k}", [P, TPB, DIM]) for k in range(2)]

        x_bank = ctx.enter_context(nc.psum_tensor("bf_x", [P, KT_, SEQ], F32))
        u_bank = [ctx.enter_context(nc.psum_tensor(f"bf_up{k}", [P, 2, SEQ], F32)) for k in range(4)]
        o_bank = [ctx.enter_context(nc.psum_tensor(f"bf_out{k}", [P, 512], F32)) for k in range(TPB)]
        a_bank = ctx.enter_context(nc.psum_tensor("bf_alpha", [P, 512], F32))

        norm = Norm(ctx, nc, "bf")
        w1_loaded = sem("w1_loaded")
        w2_loaded = sem("w2_loaded")
        biases_loaded = sem("biases_loaded")
        staged = [sem("staged0"), sem("staged1")]
        stored = [sem("stored0"), sem("stored1")]
        consts = sem("consts")
        sized = sem("sized")
        below = sem("below")
        signed = sem("signed")
        totals = sem("totals")
        alphas = sem("alphas")
        xb_ready = sem("xb_ready")
        x_turned = sem("x_turned")
        x_high = sem("x_high")
        x_low = sem("x_low")
        up = sem("up")
        h_ready = sem("h_ready")
        h_high = sem("h_high")
        h_low = sem("h_low")
        down = sem("down")
        times_alpha = sem("times_alpha")
        summed = sem("summed")

        def all_batches(batch):
            def run(engine):
                with engine.Fori(0, BATCH // 2 - 1) as i:
                    batch(2 * i, 0)
                    batch(2 * i + 1, 1)
                batch(BATCH - 2, 0, ahead=1)
                batch(BATCH - 1, 1, ahead=0)
            return run

        block = ctx.enter_context(nc.Block())

        @block.sync
        def _(sp):
            def stage(b, par):
                sp.dma_start(xs[par][:], X[:, bass.ds(b * TPB, TPB)]).then_inc(staged[par], 16)

            def restage(b, par):
                sp.wait_ge(x_turned, b + 1)
                sp.wait_ge(xb_ready, b + 1)
                stage(b + 2, par)

            def store(b, par):
                sp.wait_ge(norm.ln_done, (b + 1) * TPB)
                where = out[b] if isinstance(b, int) else out[bass.ds(b, 1)].squeeze(0)
                sp.dma_start(where.rearrange("(t p) d -> p t d", p=P), y[par][:]).then_inc(stored[par], 16)

            sp.dma_start(w1[:], w1_dram).then_inc(w1_loaded, 16)
            stage(0, 0)
            stage(1, 1)
            sp.dma_start(w2[:], w2_dram).then_inc(w2_loaded, 16)
            sp.dma_start(b1[:], b1_dram).then_inc(biases_loaded, 16)
            sp.dma_start(b2[:], b2_dram).then_inc(biases_loaded, 16)
            restage(0, 0)
            restage(1, 1)
            with sp.Fori(0, BATCH // 2 - 2) as i:
                for par in range(2):
                    restage(2 * i + par + 2, par)
                    store(2 * i + par, par)
            for b in range(BATCH - 4, BATCH):
                store(b, b % 2)
            for par in range(2):
                sp.wait_ge(stored[par], 16 * (BATCH // 2))

        @block.gpsimd
        def _(pool):
            identity(pool, ident, consts, 1).then_inc(consts, 1)
            pool.memset(ones[:], 1.0).then_inc(consts, 1)
            pool.memset(norm.half[:], -0.5).then_inc(consts, 1)
            pool.wait_ge(consts, 4)
            pool.wait_ge(biases_loaded, 32)

            def add_bias(b, par):
                pool.wait_ge(staged[par], 8 * (b - par) + 16)
                if not (isinstance(b, int) and b < 2):
                    pool.wait_ge(summed, (b - 1) * TPB)
                for t in range(TPB):
                    ins = pool.tensor_tensor(xb[par][:, t], xs[par][:, t], b2[:], ALU.add)
                ins.then_inc(xb_ready, 1)

            def batch(b, par, ahead=2):
                norm.root(pool, b, 0)
                norm.root(pool, b, 1)
                if ahead == 2:
                    add_bias(b + 2, par)

            add_bias(0, 0)
            add_bias(1, 1)
            all_batches(batch)(pool)

        @block.scalar
        def _(act):
            def tokens(b, par):
                act.wait_ge(x_turned, b + 1)
                if not (isinstance(b, int) and b < 2):
                    act.wait_ge(up, (b - 1) * 4)
                act.activation(xh[par][:], x_bank[:], ACT.Copy, scale=SCALE).then_inc(x_high, 1)

            def hidden(b, s):
                act.wait_ge(up, 4 * b + s + 1)
                if not first(b):
                    act.wait_ge(h_low, 4 * b + s - 3)
                for k in range(2):
                    m = 2 * s + k
                    ins = act.activation(h[:, m], u_bank[s][:, k], ACT.Gelu, scale=alpha1[:, m:m + 1], bias=b1[:, m:m + 1])
                ins.then_inc(h_ready, 1)

            def high(b, par, s):
                act.wait_ge(h_ready, 4 * b + s + 1)
                if not (isinstance(b, int) and b < 2):
                    act.wait_ge(down, (b - 1) * TPB)
                act.activation(hh[par][:, 2 * s:2 * s + 2], h[:, 2 * s:2 * s + 2], ACT.Copy, scale=HSCALE).then_inc(h_high, 1)

            def all_hidden(b, par):
                hidden(b, 0)
                for s in range(1, 4):
                    hidden(b, s)
                    high(b, par, s - 1)
                high(b, par, 3)

            def batch(b, par, ahead=2):
                if ahead == 2:
                    tokens(b + 2, par)
                if ahead:
                    all_hidden(b + 1, 1 - par)

            act.wait_ge(biases_loaded, 32)
            tokens(0, 0)
            tokens(1, 1)
            act.wait_ge(alphas, 2)
            all_hidden(0, 0)
            all_batches(batch)(act)

        @block.vector
        def _(dve):
            def tokens_low(b, par):
                dve.wait_ge(x_high, b + 1)
                dve.scalar_tensor_tensor(out=xl[par][:], in0=x_bank[:], scalar=SCALE, in1=xh[par][:],
                                         op0=ALU.mult, op1=ALU.subtract).then_inc(x_low, 1)

            def low(b, par, s):
                dve.wait_ge(h_high, 4 * b + s + 1)
                t = slice(2 * s, 2 * s + 2)
                dve.scalar_tensor_tensor(out=hl[par][:, t], in0=h[:, t], scalar=HSCALE, in1=hh[par][:, t],
                                         op0=ALU.mult, op1=ALU.subtract).then_inc(h_low, 1)

            def residual(b, par, t):
                dve.wait_ge(down, b * TPB + t + 1)
                dve.wait_ge(summed, b * TPB + t)
                dve.tensor_tensor(scaled[:, t], o_bank[t][:, 0:DIM], alpha2[:], ALU.mult).then_inc(times_alpha, 1)
                dve.wait_ge(times_alpha, b * TPB + t + 1)
                dve.wait_ge(xb_ready, b + 1)
                norm.wait_res_free(dve, b)
                dve.tensor_tensor(norm.res[:, t], scaled[:, t], xb[par][:, t], ALU.add).then_inc(summed, 1)
                dve.wait_ge(summed, b * TPB + t + 1)
                norm.statistics(dve, b, t)

            def batch(b, par, ahead=2):
                if ahead == 2:
                    tokens_low(b + 2, par)
                if ahead:
                    low(b + 1, 1 - par, 0)
                    low(b + 1, 1 - par, 1)
                residual(b, par, 0)
                residual(b, par, 1)
                if ahead:
                    low(b + 1, 1 - par, 2)
                    low(b + 1, 1 - par, 3)
                dve.wait_ge(stored[par], 8 * (b - par))
                for t in range(TPB):
                    norm.apply(dve, b, t, y[par][:, t])

            def split_weight(w, size, negative, sign, n):
                dve.scalar_tensor_tensor(out=size[:], in0=w[:], scalar=-1.0, in1=w[:], op0=ALU.mult, op1=ALU.max).then_inc(sized, 1)
                dve.tensor_scalar(negative[:], w[:], 0.0, None, ALU.is_lt).then_inc(below, 1)
                dve.wait_ge(below, n)
                dve.scalar_tensor_tensor(out=sign[:], in0=w[:], scalar=0.0, in1=negative[:],
                                         op0=ALU.is_gt, op1=ALU.subtract).then_inc(signed, 1)

            dve.wait_ge(w1_loaded, 16)
            split_weight(w1, size1, below1, sign1, 1)
            tokens_low(0, 0)
            tokens_low(1, 1)
            dve.wait_ge(totals, 1)
            dve.tensor_scalar(alpha1[:], a_bank[:, 0:FT], 1.0 / (DIM * SCALE), None, ALU.mult).then_inc(alphas, 1)
            dve.wait_ge(w2_loaded, 16)
            split_weight(w2, size2, below2, sign2, 2)
            dve.wait_ge(totals, 2)
            dve.tensor_scalar(alpha2[:], a_bank[:, 0:DIM], 1.0 / (FF * HSCALE), None, ALU.mult).then_inc(alphas, 1)
            dve.wait_ge(alphas, 2)
            for s in range(4):
                low(0, 0, s)
            all_batches(batch)(dve)

        @block.tensor
        def _(pe):
            def turn(b, par):
                pe.wait_ge(staged[par], 8 * (b - par) + 16)
                if not first(b):
                    pe.wait_ge(x_low, b)
                for g in range(KT_):
                    for t in range(TPB):
                        ins = pe.transpose(x_bank[:, g, t * P:(t + 1) * P], xs[par][:, t, g * P:(g + 1) * P], ident[:])
                ins.then_inc(x_turned, 1)

            def way_up(b, par):
                pe.wait_ge(x_low, b + 1)
                for s in range(4):
                    if not first(b):
                        pe.wait_ge(h_ready, 4 * b + s - 3)
                    for k in range(2):
                        m = 2 * s + k
                        n = 0
                        for x in (xh[par], xl[par]):
                            for g in range(KT_):
                                ins = pe.matmul(u_bank[s][:, k], sign1[:, g, m * P:(m + 1) * P], x[:, g],
                                                start=(n == 0), stop=(n == 2 * KT_ - 1))
                                n += 1
                    ins.then_inc(up, 1)

            def way_down(b, par):
                pe.wait_ge(h_low, 4 * b + 4)
                pe.wait_ge(times_alpha, b * TPB)
                for t in range(TPB):
                    n = 0
                    for x in (hh[par], hl[par]):
                        for m in range(FT):
                            ins = pe.matmul(o_bank[t][:, 0:DIM], x[:, m, t * P:(t + 1) * P], sign2[:, m],
                                            start=(n == 0), stop=(n == 2 * FT - 1))
                            n += 1
                    ins.then_inc(down, 1)

            def batch(b, par, ahead=2):
                if ahead == 2:
                    turn(b + 2, par)
                if ahead:
                    way_up(b + 1, 1 - par)
                way_down(b, par)

            pe.wait_ge(consts, 3)
            turn(0, 0)
            turn(1, 1)
            pe.wait_ge(sized, 1)
            for m in range(FT):
                for g in range(KT_):
                    ins = pe.matmul(a_bank[:, m:m + 1], size1[:, g, m * P:(m + 1) * P], ones[:, 0:1],
                                    start=(g == 0), stop=(g == KT_ - 1))
            ins.then_inc(totals, 1)
            pe.wait_ge(signed, 1)
            way_up(0, 0)
            pe.wait_ge(sized, 2)
            pe.wait_ge(alphas, 1)
            for m in range(FT):
                ins = pe.matmul(a_bank[:, 0:DIM], ones[:], size2[:, m], start=(m == 0), stop=(m == FT - 1))
            ins.then_inc(totals, 1)
            pe.wait_ge(signed, 2)
            all_batches(batch)(pe)


def build(nc, ins, out):
    with ExitStack() as ctx:
        X = ctx.enter_context(nc.sbuf_tensor("tokens", [P, TILES, DIM], F32))
        window_attention(nc, ins["x"], ins["xt"], ins["wqkv"], ins["wo0"], ins["rope"], X)
        cross_attention(nc, "ca0", ins["xw0"], ins["xb0"], ins["xr0"], ins["context"], ins["mask0"], False, X)
        experts(nc, ins["router"], ins["ew1"], ins["eb1"], ins["ew2"], ins["eb2"], X)
        recurrence(nc, ins["w_in"], ins["w_g"], ins["w_out"], ins["hid"], X)
        cross_attention(nc, "ca1", ins["xw1"], ins["xb1"], ins["xr1"], ins["context"], ins["mask1"], True, X)
        binary_ffn(nc, ins["w1t"], ins["w2t"], ins["b1"], ins["b2"], X, out)


def kernel(**inputs):
    import concourse.bacc as bacc
    from concourse.bass_utils import run_bass_kernel_spmd

    a = {k: np.asarray(v) for k, v in inputs.items()}

    def halves(w):
        return np.ascontiguousarray(w.reshape(-1, P, w.shape[-1]).transpose(1, 0, 2))

    def by_partition(v):
        return np.ascontiguousarray(v.reshape(-1, P).T)

    def on_all(v):
        return np.ascontiguousarray(np.broadcast_to(v, (P,) + v.shape))

    pos = np.arange(SEQ, dtype=np.float32)
    freq = np.float32(1.0) / np.float32(10000.0) ** (np.arange(0, HD, 2, dtype=np.float32) / np.float32(HD))
    angle = pos[:, None] * freq[None, :]
    cos, sin = np.cos(angle), np.sin(angle)
    rope = np.stack([np.concatenate([cos, cos], 1), np.concatenate([-sin, sin], 1)], 1).astype(np.float32)
    flat = a["x"].reshape(TOKENS, DIM)
    arrays = {
        "x": np.ascontiguousarray(flat.reshape(TILES, P, DIM).transpose(1, 0, 2)),
        "xt": halves(flat.T),
        "wqkv": halves(np.concatenate([a["L0_attn_Wq"], a["L0_attn_Wk"], a["L0_attn_Wv"]], 1)),
        "wo0": halves(a["L0_attn_Wo"]),
        "rope": np.ascontiguousarray(rope.reshape(TPB, P, 2, HD).transpose(1, 0, 2, 3)),
        "context": halves(a["ctx_1024"].reshape(BATCH * CTX, DIM).T),
        "mask0": np.ascontiguousarray(a["mask_BxSxS2_ik0"].reshape(TILES, P, CTX).transpose(1, 0, 2)),
        "mask1": np.ascontiguousarray(a["mask_Bx1xSxS2_ff0"].reshape(TILES, P, CTX).transpose(1, 0, 2)),
    }
    for n, names in (("0", ["L0_xattn_Wq", "L0_xattn_Wk", "L0_xattn_Wv", "L0_xattn_Wo"]),
                     ("1", ["L1_xattn_w_q", "L1_xattn_w_k", "L1_xattn_w_v", "L1_xattn_w_o"])):
        bq, bk, bv, bo = (a[x.replace("W", "b").replace("w_", "b_")] for x in names)
        arrays["xw" + n] = np.ascontiguousarray(np.stack([halves(a[x].T) for x in names], 1))
        arrays["xb" + n] = np.ascontiguousarray(np.stack([by_partition(bq), by_partition(bk)], 1))
        arrays["xr" + n] = np.ascontiguousarray(np.stack([on_all(bv), on_all(bo)], 1))
    router = a["L0_ffn_router_w"]
    others_first = [*range(1, EXPERTS), 0]
    arrays["router"] = halves(router.T)
    arrays["ew1"] = np.stack([halves(a["L0_ffn_W1"][e]) for e in others_first])
    arrays["eb1"] = np.stack([by_partition(a["L0_ffn_b1"][e]) for e in others_first])
    arrays["ew2"] = np.stack([halves(a["L0_ffn_W2"][e]) for e in others_first])
    arrays["eb2"] = np.stack([on_all(a["L0_ffn_b2"][e]) for e in others_first])
    for name in ("W_in", "W_g", "W_out"):
        arrays[name.lower()] = halves(a["L1_attn_" + name].T)
    arrays["hid"] = np.stack([*(by_partition(a["L1_attn_conv_w"][:, 0, t]) for t in range(4)), by_partition(a["L1_attn_conv_b"]),
                              *by_partition(a["L1_attn_b_g"]).reshape(P, 2, -1).transpose(1, 0, 2),
                              by_partition(a["L1_attn_forget_base"])], 1)
    arrays["w1t"] = halves(a["L1_ffn_w1"].T)
    arrays["w2t"] = halves(a["L1_ffn_w2"].T)
    arrays["b1"] = by_partition(a["L1_ffn_b1"])
    arrays["b2"] = on_all(a["L1_ffn_b2"])
    nc = bacc.Bacc("TRN2", target_bir_lowering=False, num_devices=1)
    ins = {k: nc.dram_tensor("in_" + k, v.shape, mybir.dt.from_np(v.dtype), kind="ExternalInput").ap()
           for k, v in arrays.items()}
    out = nc.dram_tensor("out", (BATCH, SEQ, DIM), F32, kind="ExternalOutput").ap()
    build(nc, ins, out)
    r = run_bass_kernel_spmd(nc, [{"in_" + k: v for k, v in arrays.items()}], core_ids=[0])
    return r.results[0]["out"]
```

```python
from contextlib import ExitStack

import numpy as np

import concourse.bass as bass
from concourse import mybir

F32 = mybir.dt.float32
F16 = mybir.dt.float16
BF16 = mybir.dt.bfloat16
I32 = mybir.dt.int32
ALU = mybir.AluOpType
ACT = mybir.ActivationFunctionType
AX = mybir.AxisListType

P = 128
BATCH, SEQ, DIM = 8, 256, 256
TOKENS = BATCH * SEQ
TILES = TOKENS // P
TPB = SEQ // P
KT_ = DIM // P
EPS = 1e-5
NEG = -1.0e30
SCALE = 1024.0
UNSCALE = 1.0 / (SCALE * SCALE)


class Ring:

    def __init__(self, steps, first, last, ahead):
        self.steps, self.first, self.last, self.ahead = steps, first, last, ahead
        self.per = sum(map(len, steps))
        assert self.per % 2 == 0

    def number(self, n, b=0):
        return n % 2, n // 2 + b * (self.per // 2)

    def slot(self, slot, b):
        static = isinstance(b, int)
        if static and b == 0:
            n, turns = len(self.first), 0
        else:
            n, turns = len(self.first) - len(self.last), b
        out = []
        for s, steps in enumerate(self.steps):
            for kind, i in steps:
                if static and (b == 0 and (kind, i) in self.last or b == BATCH - 1 and kind in self.ahead):
                    continue
                if s == slot:
                    out.append((kind, i, *self.number(n, turns)))
                n += 1
        return out

    def prologue(self):
        return [(kind, i, *self.number(n)) for n, (kind, i) in enumerate(self.first)]

    def epilogue(self):
        n = len(self.first) - len(self.last) + self.per * (BATCH - 1)
        n += sum(kind not in self.ahead for steps in self.steps for kind, _ in steps)
        return [(kind, i, *self.number(n + k)) for k, (kind, i) in enumerate(self.last)]

    def place(self, kind, i, b):
        body = b - 1 if kind in self.ahead else b + 1 if (kind, i) in self.last else b
        if first(b) and kind in self.ahead:
            found = self.prologue()
        elif isinstance(b, int) and body == BATCH:
            found = self.epilogue()
        else:
            found = [x for slot in range(len(self.steps)) for x in self.slot(slot, body)]
        return next((bank, uses) for k, j, bank, uses in found if (k, j) == (kind, i))

    def serves(self, kind, i):
        return 1 if kind in self.ahead else -1 if (kind, i) in self.last else 0

    def wait_read(self, engine, free, steps, b):
        last = {}
        for kind, i in steps:
            bank, uses = self.place(kind, i, b)
            last[bank] = uses
        for bank, uses in last.items():
            engine.wait_ge(free[bank], uses + 1)


def at(ap, index):
    return ap[:, index] if isinstance(index, int) else ap[:, bass.ds(index, 1)].squeeze(1)


def identity(pool, tile, made, done):
    pool.memset(tile[:], 0.0).then_inc(made, 1)
    pool.wait_ge(made, done)
    return pool.affine_select(out=tile[:], in_=tile[:], compare_op=ALU.not_equal, fill=1.0, base=0,
                              pattern=[[-1, P]], channel_multiplier=1)

class Norm:

    def __init__(self, ctx, nc, tag):
        def sb(name, shape):
            return ctx.enter_context(nc.sbuf_tensor(f"{tag}_{name}", shape, F32))

        def sem(name):
            return ctx.enter_context(nc.semaphore(f"{tag}_{name}"))

        self.res = sb("res", [P, TPB, DIM])
        self.stats = sb("stats", [P, TPB, 6])
        self.mv = sb("mv", [P, TPB, 2])
        self.var_eps = sb("var_eps", [P, TPB, 1])
        self.rstd = sb("rstd", [P, TPB, 1])
        self.half = sb("half", [P, 1])
        self.stat = sem("stat")
        self.mean_var = sem("mean_var")
        self.var_ready = sem("var_ready")
        self.rstd_ready = sem("rstd_ready")
        self.ln_done = sem("ln_done")

    def statistics(self, dve, b, t):
        dve.bn_stats(self.stats[:, t], self.res[:, t]).then_inc(self.stat, 1)
        dve.wait_ge(self.stat, b * TPB + t + 1)
        dve.memset(self.var_eps[:, t], 0.0)
        dve.bn_aggr(self.mv[:, t], self.stats[:, t]).then_inc(self.mean_var, 1)
        dve.wait_ge(self.mean_var, b * TPB + t + 1)
        dve.tensor_scalar(self.var_eps[:, t], self.mv[:, t, 1:2], EPS, None, ALU.add).then_inc(self.var_ready, 1)

    def root(self, pool, b, t):
        pool.wait_ge(self.var_ready, b * TPB + t + 1)
        pool.tensor_tensor(self.rstd[:, t], self.var_eps[:, t], self.half[:], ALU.pow).then_inc(self.rstd_ready, 1)

    def apply(self, dve, b, t, out):
        dve.wait_ge(self.rstd_ready, b * TPB + t + 1)
        dve.tensor_scalar(out, self.res[:, t], self.mv[:, t, 0:1], self.rstd[:, t],
                          ALU.subtract, ALU.mult).then_inc(self.ln_done, 1)


def first(b):
    return isinstance(b, int) and b == 0


HEADS, HD = 16, 64
WINDOW = SEQ // 4
SPAN = P + WINDOW
QKV = 3 * HEADS * HD
PSCALE = 4096.0
WA = Ring(
    steps=[
        [("project", 0), ("project", 1), ("project", 2)],
        [("project", 3), ("project", 4), ("project", 5)],
        [("heads", 3), ("project", 6), ("turn", 0), ("turn", 1)],
        [("project", 7), ("mix", 0), ("mix", 1), ("turn", 2), ("turn", 3), ("heads", 0)],
        [("project", 8), ("project", 9), ("project", 10)],
        [("heads", 1), ("project", 11), ("turn", 4), ("turn", 5)],
        [("turn", 6), ("turn", 7)],
        [("heads", 2)],
    ],
    first=([("project", n) for n in range(6)] + [("turn", 0), ("turn", 1), ("project", 6), ("turn", 2), ("turn", 3)]
           + [("project", n) for n in range(7, 12)] + [("turn", n) for n in range(4, 8)]),
    last=[("heads", 3), ("mix", 0), ("mix", 1)],
    ahead={"project", "turn"},
)
ROPE_SIN = {0: 0, 1: 1, 3: 2, 4: 3}
ROPE_ADD = {1: 0, 2: 1, 4: 2, 5: 3}


def windows(ap):
    return bass.AP(tensor=ap.tensor, offset=ap.offset, ap=[list(ap.ap[0]), [SEQ + WINDOW, 2], [1, SPAN]])


def window_attention(nc, x_dram, xt_dram, wqkv_dram, wo_dram, rope_dram, X):
    with ExitStack() as ctx:
        def sb(name, shape, dt=F32):
            return ctx.enter_context(nc.sbuf_tensor("wa_" + name, shape, dt))

        def sem(name):
            sems.append(nc.alloc_semaphore("wa_" + name))
            return sems[-1]

        sems = []

        w_stage = sb("w_stage", [P, 2, KT_, 512])
        wh = sb("wh", [P, KT_, QKV], F16)
        wl = sb("wl", [P, KT_, QKV], F16)
        wo = sb("wo", [P, HEADS * HD // P, DIM])
        cos_sin = sb("cos_sin", [P, TPB, 2, HD])
        x_stage = sb("x_stage", [P, 2, KT_, SEQ])
        xh = sb("xh", [P, 2, KT_, SEQ], F16)
        xl = sb("xl", [P, 2, KT_, SEQ], F16)
        raw = sb("raw", [P, 2, HEADS, HD])
        rot = sb("rot", [P, 2, HEADS, HD])
        sine = sb("sine", [P, HEADS, HD])
        qt = [sb(f"qt{k}", [P, HEADS, SEQ]) for k in range(2)]
        kt = [sb(f"kt{k}", [P, HEADS // 2, SEQ]) for k in range(2)]
        vh = [sb(f"vh{k}", [P, TPB, HEADS, HD + 1], F16) for k in range(2)]
        vl = [sb(f"vl{k}", [P, TPB, HEADS, HD + 1], F16) for k in range(2)]
        shifted = [sb(f"shifted{k}", [P, 2, SPAN]) for k in range(4)]
        probs = [sb(f"probs{k}", [P, 2, SEQ]) for k in range(4)]
        top = sb("top", [P, 4, 2])
        pth = [sb(f"pth{k}", [P, 2 * SEQ], F16) for k in range(4)]
        ptl = [sb(f"ptl{k}", [P, 2 * SEQ], F16) for k in range(4)]
        inv = sb("inv", [P, 2, TPB, 2])
        heads_out = sb("heads_out", [P, TPB, HEADS, HD])
        heads_t = sb("heads_t", [P, HEADS // 2, SEQ])
        ident = sb("ident", [P, P])
        ident_bf = sb("ident_bf", [P, P], BF16)
        band = sb("band", [P, TPB, SPAN], BF16)

        shared = [ctx.enter_context(nc.psum_tensor(f"wa_shared{k}", [P, 512], F32)) for k in range(2)]
        s_bank = [ctx.enter_context(nc.psum_tensor(f"wa_scores{k}", [P, 2, SEQ], F32)) for k in range(2)]
        t_bank = [ctx.enter_context(nc.psum_tensor(f"wa_turned{k}", [P, 512], F32)) for k in range(2)]
        o_bank = [ctx.enter_context(nc.psum_tensor(f"wa_out{k}", [P, TPB, 2, P], F32)) for k in range(2)]

        norm = Norm(ctx, nc, "wa")
        w_loaded = [sem("w_loaded0"), sem("w_loaded1")]
        w_high = sem("w_high")
        w_low = sem("w_low")
        x_loaded = [sem("x_loaded0"), sem("x_loaded1")]
        x_high = sem("x_high")
        x_low = sem("x_low")
        tokens_loaded = sem("tokens_loaded")
        wo_loaded = sem("wo_loaded")
        rope_loaded = sem("rope_loaded")
        consts = sem("consts")
        zeroed = sem("zeroed")
        full = [sem("full0"), sem("full1")]
        free = [sem("free0"), sem("free1")]
        cos_done = sem("cos_done")
        sin_done = sem("sin_done")
        rope_done = sem("rope_done")
        v_high = sem("v_high")
        scores = sem("scores")
        maxed = sem("maxed")
        shift = sem("shift")
        exped = sem("exped")
        probs_t = sem("probs_t")
        probs_high = sem("probs_high")
        probs_low = sem("probs_low")
        weighted = sem("weighted")
        inverted = sem("inverted")
        normed = sem("normed")

        def wait_read(engine, steps, b):
            WA.wait_read(engine, free, steps, b)

        def wait_raw(engine, b, r):
            wait_read(engine, [("project", 6 * (r // 2) + 2 * (r % 2) + c) for c in range(2)], b)

        def wait_rot_used(engine, b, r):
            bank, uses = WA.place("turn", 2 * (r - 2) + 1, b) if r >= 2 else WA.place("turn", 2 * (r + 2) + 1, b - 1)
            engine.wait_ge(full[bank], uses + 1)

        block_scope = ExitStack()
        block = block_scope.enter_context(nc.Block())

        @block.sync
        def _(sp):
            def load_x(b, par):
                sp.dma_start(x_stage[:, par], xt_dram[:, :, bass.ds(b * SEQ, SEQ)]).then_inc(x_loaded[par], 16)

            load_x(0, 0)
            for c in range(6):
                if c >= 2:
                    sp.wait_ge(w_low, c - 1)
                sp.dma_start(w_stage[:, c % 2], wqkv_dram[:, :, c * 512:(c + 1) * 512]).then_inc(w_loaded[c % 2], 16)
                if c == 1:
                    load_x(1, 1)
                    sp.dma_start(cos_sin[:], rope_dram).then_inc(rope_loaded, 16)
            sp.dma_start(wo[:], wo_dram).then_inc(wo_loaded, 16)
            sp.dma_start(X[:], x_dram).then_inc(tokens_loaded, 16)
            with sp.Fori(0, BATCH // 2 - 1) as i:
                sp.wait_ge(x_low, 2 * i + 1)
                load_x(2 * i + 2, 0)
                sp.wait_ge(x_low, 2 * i + 2)
                load_x(2 * i + 3, 1)

        @block.gpsimd
        def _(pool):
            identity(pool, ident, consts, 1).then_inc(consts, 1)
            identity(pool, ident_bf, consts, 3).then_inc(consts, 1)
            pool.memset(norm.half[:], -0.5).then_inc(consts, 1)
            pool.memset(band[:], 0.0).then_inc(consts, 1)
            pool.wait_ge(consts, 6)
            for t, base in ((0, 0), (1, P - WINDOW)):
                n = 6 + 2 * t
                pool.affine_select(out=band[:, t], in_=band[:, t], compare_op=ALU.is_ge, fill=NEG,
                                   base=base + WINDOW, pattern=[[-1, SPAN]], channel_multiplier=1).then_inc(consts, 1)
                pool.wait_ge(consts, n + 1)
                pool.affine_select(out=band[:, t], in_=band[:, t], compare_op=ALU.is_ge, fill=NEG,
                                   base=WINDOW - base, pattern=[[1, SPAN]], channel_multiplier=-1).then_inc(consts, 1)

            def cosine(b, r):
                wait_raw(pool, b, r)
                if r == 0 and isinstance(b, int) and b == 0:
                    pool.wait_ge(rope_loaded, 16)
                if not (first(b) and r < 2):
                    wait_rot_used(pool, b, r)
                c = cos_sin[:, r // 2, 0].unsqueeze(1).broadcast_to((P, HEADS, HD))
                pool.tensor_tensor(rot[:, r % 2], raw[:, r % 2], c, ALU.mult).then_inc(cos_done, 1)

            def batch(b, before=True, after=True):
                for slot in range(8):
                    if after and slot in ROPE_SIN:
                        cosine(b + 1, ROPE_SIN[slot])
                    if before and slot == 3:
                        norm.root(pool, b - 1, 0)
                        norm.root(pool, b - 1, 1)

            for r in range(4):
                cosine(0, r)
            batch(0, before=False)
            with pool.Fori(0, BATCH // 2 - 1) as i:
                batch(2 * i + 1)
                batch(2 * i + 2)
            batch(BATCH - 1, after=False)
            norm.root(pool, BATCH - 1, 0)
            norm.root(pool, BATCH - 1, 1)

        @block.scalar
        def _(act):
            def split_w(c):
                act.wait_ge(w_loaded[c % 2], 16 * (c // 2 + 1))
                act.activation(wh[:, :, c * 512:(c + 1) * 512], w_stage[:, c % 2], ACT.Copy, scale=SCALE).then_inc(w_high, 1)

            def split_x(b, par):
                act.wait_ge(x_loaded[par], 8 * (b - par) + 16)
                act.activation(xh[:, par], x_stage[:, par], ACT.Copy, scale=SCALE).then_inc(x_high, 1)

            def step(b, par, kind, i, bank, uses):
                src = shared[bank]
                if kind == "mix":
                    return
                act.wait_ge(full[bank], uses + 1)
                if kind == "project":
                    t, c = divmod(i, 6)
                    if c < 4:
                        unit = 2 * t + c // 2
                        if not (first(b) and unit < 2):
                            act.wait_ge(sin_done, b * 4 + unit - 1)
                            act.wait_ge(cos_done, b * 4 + unit - 1)
                        dst = raw[:, unit % 2, (c % 2) * 8:(c % 2) * 8 + 8]
                        act.activation(dst, src[:].rearrange("p (h d) -> p h d", h=8), ACT.Copy,
                                       scale=UNSCALE).then_inc(free[bank], 1)
                    else:
                        h0 = (c - 4) * 8
                        act.activation(vh[par][:, t, h0:h0 + 8, 0:HD], src[:].rearrange("p (h d) -> p h d", h=8),
                                       ACT.Copy, scale=1.0 / SCALE).then_inc(v_high, 1)
                elif kind == "turn":
                    t, c = divmod(i, 4)
                    cols = slice(t * P, (t + 1) * P)
                    s = src[:].rearrange("p (h q) -> p h q", h=4)
                    if c < 2:
                        act.activation(qt[par][0:HD, 8 * c:8 * c + 8:2, cols], s[0:HD], ACT.Copy)
                        act.activation(qt[par][HD:P, 8 * c + 1:8 * c + 8:2, cols], s[HD:P],
                                       ACT.Copy).then_inc(free[bank], 1)
                    else:
                        act.activation(kt[par][:, 4 * (c - 2):4 * (c - 2) + 4, cols], s,
                                       ACT.Copy).then_inc(free[bank], 1)
                elif kind == "heads":
                    act.activation(heads_t[:, 2 * i:2 * i + 2], src[:].rearrange("p (h q) -> p h q", h=2),
                                   ACT.Copy).then_inc(free[bank], 1)

            def batch(b, par, before=True, after=True):
                for slot in range(8):
                    if after and slot == 0:
                        split_x(b + 1, 1 - par)
                    for t in range(TPB):
                        n = 2 * slot + t
                        k = 2 * (slot % 2) + t
                        act.wait_ge(shift, b * 16 + n + 1)
                        if not (first(b) and slot < 2):
                            act.wait_ge(probs_t, b * 16 + 2 * slot - 2)
                        act.activation(probs[k][:, :, t * WINDOW:t * WINDOW + SPAN], shifted[k][:], ACT.Exp,
                                       scale=HD ** -0.5).then_inc(exped, 1)
                    for kind, i, bank, uses in WA.slot(slot, b):
                        d = WA.serves(kind, i)
                        step(b + d, (par + d) % 2, kind, i, bank, uses)
                    for h in range(2):
                        k = 2 * (slot % 2) + h
                        act.wait_ge(probs_t, b * 16 + 2 * slot + h + 1)
                        if not (first(b) and slot < 2):
                            act.wait_ge(weighted, b * 8 + slot - 1)
                        act.activation(windows(pth[k][:]), windows(t_bank[h][:]), ACT.Copy, scale=PSCALE).then_inc(probs_high, 1)

            split_x(0, 0)
            for c in range(6):
                split_w(c)
            act.wait_ge(zeroed, 1)
            for kind, i, bank, uses in WA.prologue():
                step(0, 0, kind, i, bank, uses)
            batch(0, 0, before=False)
            with act.Fori(0, BATCH // 2 - 1) as i:
                batch(2 * i + 1, 1)
                batch(2 * i + 2, 0)
            batch(BATCH - 1, 1, after=False)
            for kind, i, bank, uses in WA.epilogue():
                step(BATCH - 1, 1, kind, i, bank, uses)

        @block.vector
        def _(dve):
            def split_w(c):
                cols = slice(c * 512, (c + 1) * 512)
                dve.wait_ge(w_high, c + 1)
                dve.scalar_tensor_tensor(out=wl[:, :, cols], in0=w_stage[:, c % 2], scalar=SCALE,
                                         in1=wh[:, :, cols], op0=ALU.mult, op1=ALU.subtract).then_inc(w_low, 1)

            def split_x(b, par):
                dve.wait_ge(x_high, b + 1)
                dve.scalar_tensor_tensor(out=xl[:, par], in0=x_stage[:, par], scalar=SCALE,
                                         in1=xh[:, par], op0=ALU.mult, op1=ALU.subtract).then_inc(x_low, 1)

            def sin_part(b, r):
                wait_raw(dve, b, r)
                if not (first(b) and r == 0):
                    dve.wait_ge(rope_done, b * 4 + r)
                for a, z in ((0, HD // 2), (HD // 2, 0)):
                    s = cos_sin[:, r // 2, 1, a:a + HD // 2].unsqueeze(1).broadcast_to((P, HEADS, HD // 2))
                    ins = dve.tensor_tensor(sine[:, :, a:a + HD // 2], raw[:, r % 2, :, z:z + HD // 2], s, ALU.mult)
                ins.then_inc(sin_done, 1)

            def add_part(b, r):
                dve.wait_ge(sin_done, b * 4 + r + 1)
                dve.wait_ge(cos_done, b * 4 + r + 1)
                dve.tensor_tensor(rot[:, r % 2], rot[:, r % 2], sine[:], ALU.add).then_inc(rope_done, 1)

            def value_low(b, par, i, bank):
                t, c = divmod(i, 6)
                h0 = (c - 4) * 8
                dve.wait_ge(v_high, b * 4 + 2 * t + c - 3)
                dve.scalar_tensor_tensor(out=vl[par][:, t, h0:h0 + 8, 0:HD],
                                         in0=shared[bank][:].rearrange("p (h d) -> p h d", h=8), scalar=1.0 / SCALE,
                                         in1=vh[par][:, t, h0:h0 + 8, 0:HD], op0=ALU.mult,
                                         op1=ALU.subtract).then_inc(free[bank], 1)

            def residual(b, t, bank, uses):
                dve.wait_ge(full[bank], uses + 1)
                dve.tensor_tensor(norm.res[:, t], shared[bank][:, 0:DIM], at(X, b * TPB + t), ALU.add).then_inc(free[bank], 1)
                dve.wait_ge(free[bank], uses + 1)
                norm.statistics(dve, b, t)

            def layer_norm(b, t):
                norm.apply(dve, b, t, at(X, b * TPB + t))

            def shift_scores(b, u, par):
                for t in range(TPB):
                    n = 2 * u + t
                    k = 2 * (u % 2) + t
                    dve.wait_ge(scores, b * 16 + n + 1)
                    if not (first(b) and u < 2):
                        dve.wait_ge(exped, b * 16 + n - 3)
                    dve.tensor_reduce(top[:, k], s_bank[t][:, :, 0:SPAN], AX.X, ALU.max).then_inc(maxed, 1)
                    dve.wait_ge(maxed, b * 16 + n + 1)
                    dve.tensor_tensor(shifted[k][:], s_bank[t][:, :, 0:SPAN],
                                      top[:, k].unsqueeze(2).broadcast_to((P, 2, SPAN)), ALU.subtract).then_inc(shift, 1)

            def normalise(b, u):
                dve.wait_ge(weighted, b * 8 + u + 1)
                bank = o_bank[u % 2]
                if not (first(b) and u < 2):
                    dve.wait_ge(normed, b * 8 + u - 1)
                dve.reciprocal(inv[:, u % 2], bank[:, :, :, HD:HD + 1].squeeze(3)).then_inc(inverted, 1)
                dve.wait_ge(inverted, b * 8 + u + 1)
                if not first(b):
                    before, uses = WA.place("heads", u // 2, b - 1)
                    dve.wait_ge(full[before], uses + 1)
                dve.tensor_tensor(heads_out[:, :, 2 * u:2 * u + 2], bank[:, :, :, 0:HD],
                                  inv[:, u % 2].unsqueeze(3).broadcast_to((P, TPB, 2, HD)), ALU.mult).then_inc(normed, 1)

            def probs_rest(b, u):
                for h in range(2):
                    k = 2 * (u % 2) + h
                    dve.wait_ge(probs_high, b * 16 + 2 * u + h + 1)
                    dve.scalar_tensor_tensor(out=windows(ptl[k][:]), in0=windows(t_bank[h][:]), scalar=PSCALE,
                                             in1=windows(pth[k][:]), op0=ALU.mult, op1=ALU.subtract).then_inc(probs_low, 1)

            def batch(b, par, before=True, after=True):
                for slot in range(8):
                    if after and slot == 0:
                        split_x(b + 1, 1 - par)
                    if slot < 7:
                        shift_scores(b, slot + 1, par)
                    elif after:
                        shift_scores(b + 1, 0, 1 - par)
                    for kind, i, bank, uses in WA.slot(slot, b):
                        if kind == "project" and i % 6 > 3:
                            value_low(b + 1, 1 - par, i, bank)
                        if kind == "mix":
                            residual(b - 1, i, bank, uses)
                    if after and slot in ROPE_ADD:
                        add_part(b + 1, ROPE_ADD[slot])
                    if after and slot in ROPE_SIN:
                        sin_part(b + 1, ROPE_SIN[slot])
                    if before and slot == 4:
                        layer_norm(b - 1, 0)
                        layer_norm(b - 1, 1)
                    probs_rest(b, slot)
                    if slot > 0:
                        normalise(b, slot - 1)
                    elif before:
                        normalise(b - 1, 7)

            for k in range(2):
                dve.memset(vh[k][:, :, :, HD:HD + 1], SCALE)
                dve.memset(vl[k][:, :, :, HD:HD + 1], 0.0)
                dve.memset(qt[k][0:HD, 1:HEADS:2], 0.0)
                dve.memset(qt[k][HD:P, 0:HEADS:2], 0.0)
            for k in range(4):
                dve.memset(probs[k][:], 0.0)
                dve.memset(pth[k][:], 0.0)
                ins = dve.memset(ptl[k][:], 0.0)
            ins.then_inc(zeroed, 1)
            split_x(0, 0)
            for c in range(6):
                split_w(c)
            dve.wait_ge(rope_loaded, 16)
            for kind, i, bank, uses in WA.prologue():
                if kind == "project" and i % 6 > 3:
                    value_low(0, 0, i, bank)
                if kind == "project" and i % 6 in (1, 3):
                    r = 2 * (i // 6) + (i % 6) // 2
                    sin_part(0, r)
                    add_part(0, r)
            shift_scores(0, 0, 0)
            dve.wait_ge(tokens_loaded, 16)
            batch(0, 0, before=False)
            with dve.Fori(0, BATCH // 2 - 1) as i:
                batch(2 * i + 1, 1)
                batch(2 * i + 2, 0)
            batch(BATCH - 1, 1, after=False)
            normalise(BATCH - 1, 7)
            for kind, i, bank, uses in WA.epilogue():
                if kind == "mix":
                    residual(BATCH - 1, i, bank, uses)
            layer_norm(BATCH - 1, 0)
            layer_norm(BATCH - 1, 1)

        @block.tensor
        def _(pe):
            def step(b, par, kind, i, bank, uses):
                dst = shared[bank]
                if not (isinstance(uses, int) and uses == 0):
                    pe.wait_ge(free[bank], uses)
                if kind == "project":
                    t, c = divmod(i, 6)
                    if i == 0:
                        pe.wait_ge(x_low, b + 1)
                    if first(b):
                        pe.wait_ge(w_low, c + 1)
                    tok = slice(t * P, (t + 1) * P)
                    cols = slice(c * 512, (c + 1) * 512)
                    for k in range(KT_):
                        for n, (a, w) in enumerate(((xh, wh), (xh, wl), (xl, wh))):
                            ins = pe.matmul(dst[:], a[:, par, k, tok], w[:, k, cols],
                                            start=(k == 0 and n == 0), stop=(k == KT_ - 1 and n == 2))
                elif kind == "turn":
                    t, c = divmod(i, 4)
                    unit = 2 * t + c // 2
                    pe.wait_ge(rope_done, b * 4 + unit + 1)
                    for j in range(4):
                        h = 8 * (c % 2) + 2 * j
                        ins = pe.transpose(dst[:, j * P:(j + 1) * P],
                                           rot[:, unit % 2, h:h + 2].rearrange("p h d -> p (h d)"), ident[:])
                elif kind == "heads":
                    pe.wait_ge(normed, b * 8 + 2 * i + 2)
                    for j in range(2):
                        for t in range(TPB):
                            pair = 2 * i + j
                            ins = pe.transpose(dst[:, (2 * j + t) * P:(2 * j + t + 1) * P],
                                               heads_out[:, t, 2 * pair:2 * pair + 2].rearrange("p h d -> p (h d)"), ident[:])
                else:
                    wait_read(pe, [("heads", j) for j in range(4)], b)
                    for j in range(HEADS // 2):
                        ins = pe.matmul(dst[:, 0:DIM], heads_t[:, j, i * P:(i + 1) * P], wo[:, j],
                                        start=(j == 0), stop=(j == HEADS // 2 - 1))
                ins.then_inc(full[bank], 1)

            def score(b, u, par):
                if u == 0:
                    wait_read(pe, [("turn", i) for i in range(4, 8)], b)
                for t in range(TPB):
                    if not (first(b) and u == 0):
                        pe.wait_ge(shift, b * 16 + 2 * u + t - 1)
                    for h in range(2):
                        dst = s_bank[t][:, h, 0:SPAN]
                        pe.matmul(dst, ident_bf[:], band[:, t], start=True, stop=False)
                        ins = pe.matmul(dst, qt[par][:, 2 * u + h, t * P:(t + 1) * P],
                                        kt[par][:, u, t * WINDOW:t * WINDOW + SPAN], start=False, stop=True)
                    ins.then_inc(scores, 1)

            def turn_probs(b, u):
                pe.wait_ge(exped, b * 16 + 2 * u + 2)
                for h in range(2):
                    if not (first(b) and u == 0):
                        pe.wait_ge(probs_low, b * 16 + 2 * u + h - 1)
                    for j in range(2):
                        for t in range(TPB):
                            ins = pe.transpose(t_bank[h][:, j * SEQ + t * P:j * SEQ + (t + 1) * P],
                                               probs[2 * (u % 2) + t][:, h, j * P:(j + 1) * P], ident[:])
                    ins.then_inc(probs_t, 1)

            def weigh(b, u, par):
                pe.wait_ge(probs_low, b * 16 + 2 * u + 2)
                if u == 0:
                    wait_read(pe, [("project", 10), ("project", 11)], b)
                if not (first(b) and u < 2):
                    pe.wait_ge(normed, b * 8 + u - 1)
                for t in range(TPB):
                    for h in range(2):
                        k = 2 * (u % 2) + h
                        n = 0
                        for j in range(2):
                            q = slice(j * SEQ + t * P, j * SEQ + (t + 1) * P)
                            for a, v in ((pth[k], vh[par]), (pth[k], vl[par]), (ptl[k], vh[par])):
                                ins = pe.matmul(o_bank[u % 2][:, t, h, 0:HD + 1], a[:, q], v[:, j, 2 * u + h],
                                                start=(n == 0), stop=(n == 5))
                                n += 1
                ins.then_inc(weighted, 1)

            def batch(b, par, before=True, after=True):
                for slot in range(8):
                    if slot < 7:
                        score(b, slot + 1, par)
                    elif after:
                        score(b + 1, 0, 1 - par)
                    for kind, i, bank, uses in WA.slot(slot, b):
                        d = WA.serves(kind, i)
                        step(b + d, (par + d) % 2, kind, i, bank, uses)
                    turn_probs(b, slot)
                    if slot > 0:
                        weigh(b, slot - 1, par)
                    elif before:
                        weigh(b - 1, 7, 1 - par)

            pe.wait_ge(consts, 10)
            for kind, i, bank, uses in WA.prologue():
                step(0, 0, kind, i, bank, uses)
            score(0, 0, 0)
            pe.wait_ge(wo_loaded, 16)
            batch(0, 0, before=False)
            with pe.Fori(0, BATCH // 2 - 1) as i:
                batch(2 * i + 1, 1)
                batch(2 * i + 2, 0)
            batch(BATCH - 1, 1, after=False)
            weigh(BATCH - 1, 7, 1)
            for kind, i, bank, uses in WA.epilogue():
                step(BATCH - 1, 1, kind, i, bank, uses)

        block_scope.close()
        nc.clear_and_free_semaphores(sems)
        nc.all_engine_barrier()


CTX = 77
CH, CD = 16, 16
UH = 4
UNITS = TPB * CH // UH
MASKED = -4.0e9
OPEN = 1.0e38
CA = Ring(
    steps=[
        [("key", 0)],
        [("value", 0)],
        [("heads", 1)],
        [("mix", 1)],
        [("tokens", 0)],
        [("query", 0)],
        [("heads", 0)],
        [("mix", 0)],
    ],
    first=[("key", 0), ("value", 0), ("tokens", 0), ("query", 0)],
    last=[("heads", 1), ("mix", 1)],
    ahead={"key", "value", "tokens", "query"},
)


def cross_attention(nc, tag, w_dram, b_dram, rows_dram, ctx_dram, mask_dram, additive, X):
    with ExitStack() as ctx:
        def sb(name, shape, dt=F32):
            return ctx.enter_context(nc.sbuf_tensor(f"{tag}_{name}", shape, dt))

        def sem(name):
            sems.append(nc.alloc_semaphore(f"{tag}_{name}"))
            return sems[-1]

        sems = []

        w = sb("w", [P, 4, KT_, DIM])
        bias = sb("bias", [P, 2, KT_])
        rows = sb("rows", [P, 2, DIM])
        context = [sb(f"context{k}", [P, KT_, CTX]) for k in range(2)]
        xs = [sb(f"xs{k}", [P, TPB, DIM]) for k in range(2)]
        mask = sb("mask", [P, TILES, CTX], F32 if additive else I32)
        limit = None if additive else sb("limit", [P, TILES, CTX])
        head_of = sb("head_of", [P, CH // KT_])
        ident = sb("ident", [P, P])
        xt = [sb(f"xt{k}", [P, KT_, SEQ]) for k in range(2)]
        q = [sb(f"q{k}", [P, KT_, SEQ]) for k in range(2)]
        kb = sb("kb", [P, KT_, CTX])
        km = [sb(f"km{k}", [P, KT_, CH // KT_, CTX]) for k in range(2)]
        v = sb("v", [P, CH, CD])
        vh = [sb(f"vh{k}", [P, CH, CD + 1], F16) for k in range(2)]
        vl = [sb(f"vl{k}", [P, CH, CD + 1], F16) for k in range(2)]
        z = [sb(f"z{k}", [P, UH, CTX]) for k in range(2)]
        top = sb("top", [P, 2, UH])
        probs = [sb(f"probs{k}", [P, UH, CTX]) for k in range(2)]
        pth = [sb(f"pth{k}", [P, UH * P], F16) for k in range(2)]
        ptl = [sb(f"ptl{k}", [P, UH * P], F16) for k in range(2)]
        inv = sb("inv", [P, TPB, CH])
        o = sb("o", [P, TPB, CH, CD])
        ot = sb("ot", [P, TPB, KT_, P])
        xb = sb("xb", [P, TPB, DIM])

        shared = [ctx.enter_context(nc.psum_tensor(f"{tag}_shared{k}", [P, 512], F32)) for k in range(2)]
        s_bank = [ctx.enter_context(nc.psum_tensor(f"{tag}_scores{k}", [P, 512], F32)) for k in range(2)]
        t_bank = [ctx.enter_context(nc.psum_tensor(f"{tag}_turned{k}", [P, 512], F32)) for k in range(2)]
        o_bank = [ctx.enter_context(nc.psum_tensor(f"{tag}_out{k}", [P, CH, 32], F32)) for k in range(2)]

        norm = Norm(ctx, nc, tag)
        kv_loaded = sem("kv_loaded")
        context_loaded = [sem("context_loaded0"), sem("context_loaded1")]
        staged = [sem("staged0"), sem("staged1")]
        w_loaded = sem("w_loaded")
        mask_loaded = sem("mask_loaded")
        consts = sem("consts")
        limits = sem("limits")
        ones = sem("ones")
        full = [sem("full0"), sem("full1")]
        free = [sem("free0"), sem("free1")]
        key_masked = sem("key_masked")
        v_high = sem("v_high")
        v_low = sem("v_low")
        token_sum = sem("token_sum")
        scores = sem("scores")
        masked = sem("masked")
        maxed = sem("maxed")
        shift = sem("shift")
        exped = sem("exped")
        probs_t = sem("probs_t")
        probs_high = sem("probs_high")
        probs_low = sem("probs_low")
        weighted = sem("weighted")
        inverted = sem("inverted")
        normed = sem("normed")

        def wait_read(engine, steps, b):
            CA.wait_read(engine, free, steps, b)

        def wait_full(engine, kind, i, b):
            bank, uses = CA.place(kind, i, b)
            engine.wait_ge(full[bank], uses + 1)

        def both(batch):
            def run(engine):
                batch(0, 0, before=False)
                with engine.Fori(0, BATCH // 2 - 1) as i:
                    batch(2 * i + 1, 1)
                    batch(2 * i + 2, 0)
                batch(BATCH - 1, 1, after=False)
            return run

        block_scope = ExitStack()
        block = block_scope.enter_context(nc.Block())

        @block.sync
        def _(sp):
            def load_context(b, par):
                sp.dma_start(context[par][:], ctx_dram[:, :, bass.ds(b * CTX, CTX)]).then_inc(context_loaded[par], 16)

            def stage(b, par):
                sp.dma_start(xs[par][:], X[:, bass.ds(b * TPB, TPB)]).then_inc(staged[par], 16)

            for b in (0, 1):
                load_context(b, b)
                stage(b, b)
            sp.dma_start(bias[:], b_dram).then_inc(kv_loaded, 16)
            sp.dma_start(rows[:], rows_dram).then_inc(kv_loaded, 16)
            sp.dma_start(w[:], w_dram).then_inc(w_loaded, 16)
            sp.dma_start(mask[:], mask_dram).then_inc(mask_loaded, 16)

            def replace(b, par):
                wait_full(sp, "value", 0, b)
                load_context(b + 2, par)
                wait_full(sp, "tokens", 0, b)
                sp.wait_ge(token_sum, (b + 1) * TPB)
                stage(b + 2, par)

            replace(0, 0)
            replace(1, 1)
            with sp.Fori(1, BATCH // 2 - 1) as i:
                replace(2 * i, 0)
                replace(2 * i + 1, 1)

        @block.gpsimd
        def _(pool):
            identity(pool, ident, consts, 1).then_inc(consts, 1)
            pool.memset(norm.half[:], -0.5).then_inc(consts, 1)
            pool.memset(head_of[:], 1.0).then_inc(consts, 1)
            pool.wait_ge(consts, 4)
            pool.affine_select(out=head_of[:], in_=head_of[:], compare_op=ALU.is_ge, fill=0.0, base=0,
                               pattern=[[-CD, CH // KT_]], channel_multiplier=1).then_inc(consts, 1)
            pool.wait_ge(consts, 5)
            pool.affine_select(out=head_of[:], in_=head_of[:], compare_op=ALU.is_ge, fill=0.0, base=CD - 1,
                               pattern=[[CD, CH // KT_]], channel_multiplier=-1).then_inc(consts, 1)
            pool.wait_ge(consts, 6)
            pool.wait_ge(kv_loaded, 32)

            def mask_keys(b, par, g):
                wait_read(pool, [("key", 0)], b)
                pool.tensor_tensor(km[par][:, g], kb[:, g].unsqueeze(1).broadcast_to((P, CH // KT_, CTX)),
                                   head_of[:].unsqueeze(2).broadcast_to((P, CH // KT_, CTX)), ALU.mult).then_inc(key_masked, 1)

            def subtract(b, c):
                pool.wait_ge(maxed, b * UNITS + c + 1)
                k = c % 2
                pool.tensor_tensor(z[k][:], z[k][:], top[:, k].unsqueeze(2).broadcast_to((P, UH, CTX)),
                                   ALU.subtract).then_inc(shift, 1)

            def add_bias(b, par, t):
                if not first(b):
                    wait_read(pool, [("mix", 0), ("mix", 1)], b - 1)
                pool.wait_ge(staged[par], 8 * (b - par) + 16)
                pool.tensor_tensor(xb[:, t], xs[par][:, t], rows[:, 1], ALU.add).then_inc(token_sum, 1)

            def batch(b, par, before=True, after=True):
                for c in range(UNITS):
                    if c < UNITS - 2:
                        subtract(b, c + 2)
                    elif after:
                        subtract(b + 1, c + 2 - UNITS)
                    if c in (1, 3) and after:
                        mask_keys(b + 1, 1 - par, c // 2)
                    if c == 4 and before:
                        norm.root(pool, b - 1, 1)
                    if c in (5, 6):
                        add_bias(b, par, c - 5)
                    if c == 7:
                        norm.root(pool, b, 0)

            mask_keys(0, 0, 0)
            mask_keys(0, 0, 1)
            subtract(0, 0)
            subtract(0, 1)
            both(batch)(pool)
            norm.root(pool, BATCH - 1, 1)

        @block.scalar
        def _(act):
            act.wait_ge(kv_loaded, 32)

            def step(b, par, kind, i, bank, uses):
                src = shared[bank]
                if kind in ("mix", "value"):
                    return
                act.wait_ge(full[bank], uses + 1)
                if kind == "tokens":
                    ins = act.activation(xt[par][:], src[:].rearrange("p (g q) -> p g q", g=KT_), ACT.Copy)
                elif kind == "query":
                    for g in range(KT_):
                        ins = act.activation(q[par][:, g], src[:, g * SEQ:(g + 1) * SEQ], ACT.Identity, bias=bias[:, 0, g:g + 1])
                elif kind == "key":
                    if not first(b):
                        act.wait_ge(key_masked, b * KT_)
                    for g in range(KT_):
                        ins = act.activation(kb[:, g], src[:, g * CTX:(g + 1) * CTX], ACT.Identity, bias=bias[:, 1, g:g + 1])
                elif kind == "heads":
                    ins = act.activation(ot[:, i], src[:, 0:DIM].rearrange("p (g q) -> p g q", g=KT_), ACT.Copy)
                ins.then_inc(free[bank], 1)

            def value_high(b, par):
                wait_read(act, [("value", 0)], b)
                act.activation(vh[par][0:CTX, :, 0:CD], v[0:CTX], ACT.Copy, scale=SCALE).then_inc(v_high, 1)

            def power(b, c):
                k = c % 2
                act.wait_ge(shift, b * UNITS + c + 1)
                if not (first(b) and c < 2):
                    act.wait_ge(probs_t, b * UNITS + c - 1)
                act.activation(probs[k][:], z[k][:], ACT.Exp, scale=1.0 if additive else CD ** -0.5).then_inc(exped, 1)

            def batch(b, par, before=True, after=True):
                for c in range(UNITS):
                    k = c % 2
                    act.wait_ge(probs_t, b * UNITS + c + 1)
                    if not (first(b) and c < 2):
                        act.wait_ge(weighted, b * UNITS + c - 1)
                    act.activation(pth[k][0:CTX], t_bank[k][0:CTX], ACT.Copy, scale=PSCALE).then_inc(probs_high, 1)
                    if c < UNITS - 1:
                        power(b, c + 1)
                    elif after:
                        power(b + 1, 0)
                    for kind, i, bank, uses in CA.slot(c, b):
                        d = CA.serves(kind, i)
                        step(b + d, (par + d) % 2, kind, i, bank, uses)
                    if c == 2 and after:
                        value_high(b + 1, 1 - par)

            act.wait_ge(ones, 1)
            for kind, i, bank, uses in CA.prologue():
                step(0, 0, kind, i, bank, uses)
            value_high(0, 0)
            power(0, 0)
            both(batch)(act)
            for kind, i, bank, uses in CA.epilogue():
                step(BATCH - 1, 1, kind, i, bank, uses)

        @block.vector
        def _(dve):
            for k in range(2):
                dve.memset(vh[k][:, :, CD:CD + 1], SCALE)
                ins = dve.memset(vl[k][:, :, CD:CD + 1], 0.0)
            ins.then_inc(ones, 1)
            dve.wait_ge(kv_loaded, 32)

            def value(b, par, bank, uses):
                dve.wait_ge(full[bank], uses + 1)
                if not first(b):
                    dve.wait_ge(v_low, b)
                dve.tensor_tensor(v[0:CTX], shared[bank][0:CTX, 0:DIM].rearrange("p (h d) -> p h d", h=CH),
                                  rows[0:CTX, 0].rearrange("p (h d) -> p h d", h=CH), ALU.add).then_inc(free[bank], 1)

            def value_low(b, par):
                dve.wait_ge(v_high, b + 1)
                dve.scalar_tensor_tensor(out=vl[par][0:CTX, :, 0:CD], in0=v[0:CTX], scalar=SCALE,
                                         in1=vh[par][0:CTX, :, 0:CD], op0=ALU.mult, op1=ALU.subtract).then_inc(v_low, 1)

            def mask_scores(b, c):
                k = c % 2
                dve.wait_ge(scores, b * UNITS + c + 1)
                if not (first(b) and c < 2):
                    dve.wait_ge(exped, b * UNITS + c - 1)
                s = s_bank[k][:, 0:UH * CTX].rearrange("p (h k) -> p h k", h=UH)
                m = at(mask if additive else limit, b * TPB + c // (UNITS // TPB)).unsqueeze(1).broadcast_to((P, UH, CTX))
                if additive:
                    ins = dve.scalar_tensor_tensor(out=z[k][:], in0=s, scalar=CD ** -0.5, in1=m, op0=ALU.mult, op1=ALU.add)
                else:
                    ins = dve.tensor_tensor(z[k][:], s, m, ALU.min)
                ins.then_inc(masked, 1)
                dve.wait_ge(masked, b * UNITS + c + 1)
                dve.tensor_reduce(top[:, k], z[k][:], AX.X, ALU.max).then_inc(maxed, 1)

            def probs_rest(b, c):
                k = c % 2
                dve.wait_ge(probs_high, b * UNITS + c + 1)
                dve.scalar_tensor_tensor(out=ptl[k][0:CTX], in0=t_bank[k][0:CTX], scalar=PSCALE, in1=pth[k][0:CTX],
                                         op0=ALU.mult, op1=ALU.subtract).then_inc(probs_low, 1)

            def normalise(b, t):
                dve.wait_ge(weighted, b * UNITS + (t + 1) * (UNITS // TPB))
                dve.wait_ge(normed, b * TPB + t)
                dve.reciprocal(inv[:, t], o_bank[t][:, :, CD:CD + 1].squeeze(2)).then_inc(inverted, 1)
                dve.wait_ge(inverted, b * TPB + t + 1)
                if not first(b):
                    wait_read(dve, [("heads", t)], b - 1)
                dve.tensor_tensor(o[:, t], o_bank[t][:, :, 0:CD], inv[:, t].unsqueeze(2).broadcast_to((P, CH, CD)),
                                  ALU.mult).then_inc(normed, 1)

            def residual(b, t, bank, uses):
                dve.wait_ge(full[bank], uses + 1)
                dve.wait_ge(token_sum, b * TPB + t + 1)
                dve.tensor_tensor(norm.res[:, t], shared[bank][:, 0:DIM], xb[:, t], ALU.add).then_inc(free[bank], 1)
                dve.wait_ge(free[bank], uses + 1)
                norm.statistics(dve, b, t)

            def batch(b, par, before=True, after=True):
                for c in range(UNITS):
                    probs_rest(b, c)
                    if c < UNITS - 2:
                        mask_scores(b, c + 2)
                    elif after:
                        mask_scores(b + 1, c + 2 - UNITS)
                    for kind, i, bank, uses in CA.slot(c, b):
                        if kind == "value":
                            value(b + 1, 1 - par, bank, uses)
                        if kind == "mix":
                            residual(b + CA.serves(kind, i), i, bank, uses)
                    if c == 0 and before:
                        norm.apply(dve, b - 1, 0, at(X, (b - 1) * TPB))
                    if c == 5 and before:
                        norm.apply(dve, b - 1, 1, at(X, (b - 1) * TPB + 1))
                    if c == 2 and after:
                        value_low(b + 1, 1 - par)
                    if c == 5:
                        normalise(b, 0)
                    if c == 1 and before:
                        normalise(b - 1, 1)

            for kind, i, bank, uses in CA.prologue():
                if kind == "value":
                    value(0, 0, bank, uses)
            value_low(0, 0)
            dve.wait_ge(mask_loaded, 16)
            if not additive:
                dve.tensor_scalar(limit[:], mask[:], 0, -2 * OPEN, ALU.is_equal, ALU.mult).then_inc(limits, 1)
                dve.wait_ge(limits, 1)
                dve.tensor_scalar(limit[:], limit[:], OPEN, MASKED, ALU.add, ALU.max).then_inc(limits, 1)
                dve.wait_ge(limits, 2)
            mask_scores(0, 0)
            mask_scores(0, 1)
            both(batch)(dve)
            norm.apply(dve, BATCH - 1, 0, at(X, (BATCH - 1) * TPB))
            normalise(BATCH - 1, 1)
            for kind, i, bank, uses in CA.epilogue():
                if kind == "mix":
                    residual(BATCH - 1, i, bank, uses)
            norm.apply(dve, BATCH - 1, 1, at(X, (BATCH - 1) * TPB + 1))

        @block.tensor
        def _(pe):
            def step(b, par, kind, i, bank, uses):
                dst = shared[bank]
                if not (isinstance(uses, int) and uses == 0):
                    pe.wait_ge(free[bank], uses)
                if kind == "tokens":
                    pe.wait_ge(staged[par], 8 * (b - par) + 16)
                    for g in range(KT_):
                        for t in range(TPB):
                            ins = pe.transpose(dst[:, g * SEQ + t * P:g * SEQ + (t + 1) * P],
                                               xs[par][:, t, g * P:(g + 1) * P], ident[:])
                elif kind == "query":
                    wait_read(pe, [("tokens", 0)], b)
                    for g in range(KT_):
                        for k in range(KT_):
                            ins = pe.matmul(dst[:, g * SEQ:(g + 1) * SEQ], w[:, 0, k, g * P:(g + 1) * P], xt[par][:, k],
                                            start=(k == 0), stop=(k == KT_ - 1))
                elif kind == "key":
                    pe.wait_ge(context_loaded[par], 8 * (b - par) + 16)
                    for g in range(KT_):
                        for k in range(KT_):
                            ins = pe.matmul(dst[:, g * CTX:(g + 1) * CTX], w[:, 1, k, g * P:(g + 1) * P],
                                            context[par][:, k], start=(k == 0), stop=(k == KT_ - 1))
                elif kind == "value":
                    for k in range(KT_):
                        ins = pe.matmul(dst[0:CTX, 0:DIM], context[par][:, k], w[:, 2, k],
                                        start=(k == 0), stop=(k == KT_ - 1))
                elif kind == "heads":
                    pe.wait_ge(normed, b * TPB + i + 1)
                    for g in range(KT_):
                        ins = pe.transpose(dst[:, g * P:(g + 1) * P],
                                           o[:, i, g * 8:(g + 1) * 8].rearrange("p h d -> p (h d)"), ident[:])
                else:
                    wait_read(pe, [("heads", i)], b)
                    for g in range(KT_):
                        ins = pe.matmul(dst[:, 0:DIM], ot[:, i, g], w[:, 3, g], start=(g == 0), stop=(g == KT_ - 1))
                ins.then_inc(full[bank], 1)

            def score(b, c, par):
                t, part = divmod(c, UNITS // TPB)
                g, h = part // 2, UH * (part % 2)
                if c == 0:
                    wait_read(pe, [("query", 0)], b)
                    pe.wait_ge(key_masked, (b + 1) * KT_)
                if not (first(b) and c < 2):
                    pe.wait_ge(masked, b * UNITS + c - 1)
                pe.matmul(s_bank[c % 2][:, 0:UH * CTX], q[par][:, g, t * P:(t + 1) * P],
                          km[par][:, g, h:h + UH].rearrange("p h k -> p (h k)"), start=True, stop=True).then_inc(scores, 1)

            def turn_probs(b, c):
                k = c % 2
                pe.wait_ge(exped, b * UNITS + c + 1)
                if not (first(b) and c < 2):
                    pe.wait_ge(probs_low, b * UNITS + c - 1)
                for h in range(UH):
                    ins = pe.transpose(t_bank[k][0:CTX, h * P:(h + 1) * P], probs[k][:, h], ident[:])
                ins.then_inc(probs_t, 1)

            def weigh(b, c, par):
                k, t = c % 2, c // (UNITS // TPB)
                pe.wait_ge(probs_low, b * UNITS + c + 1)
                if c == 0:
                    pe.wait_ge(v_low, b + 1)
                if c % (UNITS // TPB) == 0 and not first(b):
                    pe.wait_ge(normed, b * TPB + t - 1)
                for h in range(UH):
                    head = UH * (c % (UNITS // TPB)) + h
                    cols = slice(h * P, (h + 1) * P)
                    for n, (a, x) in enumerate(((pth[k], vh[par]), (pth[k], vl[par]), (ptl[k], vh[par]))):
                        ins = pe.matmul(o_bank[t][:, head, 0:CD + 1], a[0:CTX, cols], x[0:CTX, head],
                                        start=(n == 0), stop=(n == 2))
                ins.then_inc(weighted, 1)

            def batch(b, par, before=True, after=True):
                for c in range(UNITS):
                    turn_probs(b, c)
                    if c < UNITS - 2:
                        score(b, c + 2, par)
                    elif after:
                        score(b + 1, c + 2 - UNITS, 1 - par)
                    for kind, i, bank, uses in CA.slot(c, b):
                        d = CA.serves(kind, i)
                        step(b + d, (par + d) % 2, kind, i, bank, uses)
                    if c > 0:
                        weigh(b, c - 1, par)
                    elif before:
                        weigh(b - 1, UNITS - 1, 1 - par)

            pe.wait_ge(consts, 2)
            pe.wait_ge(kv_loaded, 32)
            pe.wait_ge(w_loaded, 16)
            for kind, i, bank, uses in CA.prologue():
                step(0, 0, kind, i, bank, uses)
            score(0, 0, 0)
            score(0, 1, 0)
            both(batch)(pe)
            weigh(BATCH - 1, UNITS - 1, 1)
            for kind, i, bank, uses in CA.epilogue():
                step(BATCH - 1, 1, kind, i, bank, uses)

        block_scope.close()
        nc.clear_and_free_semaphores(sems)
        nc.all_engine_barrier()


EXPERTS, FF = 8, 1024
FT = FF // P
CAP = TOKENS * 5 // (4 * EXPERTS)
UNIT = CAP // 2
ROWS = UNIT // 2
SIDE = EXPERTS - 1
MOST = -(-TOKENS // UNIT)
END = 1 + (TOKENS + EXPERTS * UNIT) // UNIT
SLOTS = (END + 2) * UNIT
ZERO_ROWS = SLOTS // 32
HSCALE = 16.0


def route(nc, router_dram, slots, X, slot, starts, ahead_of_experts):
    with ExitStack() as ctx:
        def sb(name, shape, dt=F32):
            return ctx.enter_context(nc.sbuf_tensor("rt_" + name, shape, dt))

        def sem(name):
            return ctx.enter_context(nc.semaphore("rt_" + name))

        router = sb("router", [P, KT_, EXPERTS])
        ident = sb("ident", [P, P])
        before = sb("before", [P, P])
        before_bf = sb("before_bf", [P, P], BF16)
        ones_bf = sb("ones_bf", [P, P], BF16)
        ones = sb("ones", [P, TILES])
        code = sb("code", [P, EXPERTS])
        steps = sb("steps", [P, MOST])
        zeros = sb("zeros", [ZERO_ROWS, 8, DIM])
        xt = [sb(f"xt{k}", [P, KT_, 2 * P]) for k in range(2)]
        gap = sb("gap", [P, TILES, EXPERTS])
        power = sb("power", [P, TILES, EXPERTS])
        best = sb("best", [P, TILES])
        pick = sb("pick", [P, TILES, EXPERTS])
        chosen = sb("chosen", [P, TILES])
        onehot = sb("onehot", [P, TILES, EXPERTS])
        onehot_bf = sb("onehot_bf", [P, TILES, EXPERTS], BF16)
        key = sb("key", [P, TILES])
        keys = sb("keys", [P, TOKENS])
        same = sb("same", [P, 2, P])
        ahead = sb("ahead", [P, TILES, TOKENS], BF16)
        own = sb("own", [P, TILES, EXPERTS])
        rank = sb("rank", [P, TILES])
        kept = sb("kept", [P, TILES])
        side = sb("side", [P, TILES])
        base = sb("base", [P, TILES])
        base_bf = sb("base_bf", [P, TILES], BF16)
        upto = sb("upto", [P, TILES])
        place = sb("place", [P, TILES])
        place_side = sb("place_side", [P, TILES])
        over = sb("over", [P, MOST])
        many = sb("many", [P, 1])
        counts = sb("counts", [P, EXPERTS])
        units = sb("units", [P, EXPERTS])
        first_unit = sb("first_unit", [P, EXPERTS + 1])
        first_slot = sb("first_slot", [P, SIDE])
        theirs = sb("theirs", [P, TILES, SIDE])
        base_slot = sb("base_slot", [P, 1])
        start_slot = sb("start_slot", [P, TILES])

        x_bank = [ctx.enter_context(nc.psum_tensor(f"rt_x{k}", [P, KT_, 2 * P], F32)) for k in range(2)]
        l_bank = ctx.enter_context(nc.psum_tensor("rt_logit_bank", [P, TILES, 32], F32))
        k_bank = ctx.enter_context(nc.psum_tensor("rt_key_bank", [P, TOKENS], F32))
        r_bank = ctx.enter_context(nc.psum_tensor("rt_rank_bank", [P, 64, EXPERTS], F32))

        router_loaded = sem("router_loaded")
        consts = sem("consts")
        zero_tile = sem("zero_tile")
        zeroed = sem("zeroed")
        x_turned = sem("x_turned")
        x_ready = sem("x_ready")
        logits = sem("logits")
        onehot_ready = sem("onehot_ready")
        tallied = sem("tallied")
        step = sem("step")
        gap_ready = sem("gap_ready")
        power_ready = sem("power_ready")
        key_ready = sem("key_ready")
        keys_turned = sem("keys_turned")
        keys_ready = sem("keys_ready")
        diagonal = sem("diagonal")
        compared = sem("compared")
        ranks = sem("ranks")
        base_ready = sem("base_ready")
        counted = sem("counted")
        slots_ready = sem("slots_ready")
        scattered = sem("scattered")

        def logit(pe, j):
            pe.wait_ge(x_ready, j + 1)
            for t in range(2):
                for g in range(KT_):
                    ins = pe.matmul(l_bank[:, 2 * j + t, 0:EXPERTS], xt[j % 2][:, g, t * P:(t + 1) * P], router[:, g],
                                    start=(g == 0), stop=(g == KT_ - 1))
            ins.then_inc(logits, 1)

        block = ctx.enter_context(nc.Block())

        @block.sync
        def _(sp):
            sp.dma_start(router[:], router_dram).then_inc(router_loaded, 16)
            ahead_of_experts["sync"](sp)
            sp.wait_ge(zero_tile, 1)
            rows = ZERO_ROWS * 8
            for n in range(4):
                sp.dma_start(slots[n * rows:(n + 1) * rows].rearrange("(t p) d -> p t d", p=ZERO_ROWS), zeros[:]).then_inc(zeroed, 16)
            ahead_of_experts["sync late"](sp)

        @block.gpsimd
        def _(pool):
            pool.memset(zeros[:], 0.0).then_inc(zero_tile, 1)
            identity(pool, ident, consts, 1).then_inc(consts, 1)
            pool.memset(before[:], 1.0).then_inc(consts, 1)
            pool.memset(before_bf[:], 1.0).then_inc(consts, 1)
            pool.wait_ge(consts, 4)
            for m in (before, before_bf):
                pool.affine_select(out=m[:], in_=m[:], compare_op=ALU.is_gt, fill=0.0, base=0,
                                   pattern=[[1, P]], channel_multiplier=-1).then_inc(consts, 1)
            pool.memset(ones_bf[:], 1.0).then_inc(consts, 1)
            pool.memset(ones[:], 1.0).then_inc(consts, 1)
            pool.iota(code[:], pattern=[[-1, EXPERTS]], base=EXPERTS, channel_multiplier=0,
                      allow_small_or_imprecise_dtypes=True).then_inc(consts, 1)
            pool.iota(steps[:], pattern=[[UNIT, MOST]], base=0, channel_multiplier=0,
                      allow_small_or_imprecise_dtypes=True).then_inc(consts, 1)
            ahead_of_experts["gpsimd"](pool)
            pool.wait_ge(zeroed, 16 * 4)
            pool.wait_ge(slots_ready, 1)
            for j in range(TILES):
                pool.indirect_dma_start(out=slots[:, :], out_offset=bass.IndirectOffsetOnAxis(ap=slot[:, j:j + 1], axis=0),
                                        in_=X[:, j], in_offset=None).then_inc(scattered, 16)
            pool.wait_ge(scattered, 16 * TILES)

        @block.scalar
        def _(act):
            for j in range(TILES // 2):
                act.wait_ge(x_turned, j + 1)
                if j >= 2:
                    act.wait_ge(logits, j - 1)
                act.activation(xt[j % 2][:], x_bank[j % 2][:], ACT.Copy).then_inc(x_ready, 1)
            act.wait_ge(gap_ready, 1)
            act.activation(power[:], gap[:], ACT.Exp).then_inc(power_ready, 1)
            for n in range(4):
                act.wait_ge(keys_turned, n + 1)
                act.activation(keys[:, n * 512:(n + 1) * 512], k_bank[:, n * 512:(n + 1) * 512], ACT.Copy).then_inc(keys_ready, 1)
            ahead_of_experts["scalar"](act)

        @block.vector
        def _(dve):
            done = [0]

            def then(ins):
                done[0] += 1
                ins.then_inc(step, 1)
                dve.wait_ge(step, done[0])

            def wide(v):
                return v.unsqueeze(2).broadcast_to((P, TILES, EXPERTS))

            tally = l_bank[:, 0:4].rearrange("p a e -> p (a e)").rearrange("p (t e) -> p t e", e=EXPERTS)
            codes = code[:].unsqueeze(1).broadcast_to((P, TILES, EXPERTS))
            dve.wait_ge(consts, 10)
            dve.wait_ge(logits, TILES // 2)
            l = l_bank[:, :, 0:EXPERTS]
            then(dve.tensor_reduce(best[:], l, AX.X, ALU.max))
            dve.tensor_tensor(gap[:], l, wide(best[:]), ALU.subtract).then_inc(gap_ready, 1)
            dve.wait_ge(gap_ready, 1)
            then(dve.scalar_tensor_tensor(out=pick[:], in0=gap[:], scalar=0.0, in1=codes, op0=ALU.is_equal, op1=ALU.mult))
            then(dve.tensor_reduce(chosen[:], pick[:], AX.X, ALU.max))
            then(dve.tensor_tensor(onehot[:], codes, wide(chosen[:]), ALU.is_equal))
            dve.tensor_copy(onehot_bf[:], onehot[:]).then_inc(onehot_ready, 1)
            dve.wait_ge(power_ready, 1)
            dve.tensor_reduce(key[:], power[:], AX.X, ALU.add).then_inc(key_ready, 1)
            ahead_of_experts["vector"](dve)
            dve.wait_ge(tallied, 1)
            then(dve.tensor_reduce(counts[:], tally.rearrange("p t e -> p e t"), AX.X, ALU.add))
            then(dve.tensor_scalar(units[:], counts[:], float(UNIT), 1.0, ALU.is_gt, ALU.add))
            then(dve.memset(first_unit[:, 0:1], 1.0))
            then(dve.tensor_tensor_scan(first_unit[:, 1:EXPERTS], ones[:, 0:SIDE], units[:, 1:], 1.0, ALU.mult, ALU.add))
            then(dve.tensor_scalar(first_slot[:], first_unit[:, 0:SIDE], float(UNIT), None, ALU.mult))
            then(dve.tensor_tensor(theirs[:], onehot[:, :, 1:], first_slot[:].unsqueeze(1).broadcast_to((P, TILES, SIDE)), ALU.mult))
            then(dve.tensor_reduce(start_slot[:], theirs[:], AX.X, ALU.add))
            then(dve.tensor_scalar(base_slot[:], first_unit[:, SIDE:EXPERTS], float(UNIT), None, ALU.mult))
            dve.wait_ge(keys_ready, 4)
            dve.wait_ge(key_ready, 1)
            for j in range(TILES):
                k, a, z = key[:, j:j + 1], j * P, (j + 1) * P
                if j:
                    dve.tensor_scalar(ahead[:, j, 0:a], keys[:, 0:a], k, None, ALU.is_gt)
                if j < TILES - 1:
                    dve.tensor_scalar(ahead[:, j, z:], keys[:, z:], k, None, ALU.is_ge)
                if j >= 2:
                    dve.wait_ge(compared, j - 1)
                dve.scalar_tensor_tensor(out=same[:, j % 2], in0=keys[:, a:z], scalar=k, in1=before[:],
                                         op0=ALU.is_equal, op1=ALU.mult).then_inc(diagonal, 1)
                dve.wait_ge(diagonal, j + 1)
                dve.scalar_tensor_tensor(out=ahead[:, j, a:z], in0=keys[:, a:z], scalar=k, in1=same[:, j % 2],
                                         op0=ALU.is_gt, op1=ALU.add).then_inc(compared, 1)
            dve.wait_ge(ranks, 1)
            then(dve.tensor_tensor(own[:], r_bank[:, 0:TILES], onehot[:], ALU.mult))
            then(dve.tensor_reduce(rank[:], own[:], AX.X, ALU.add))
            then(dve.tensor_scalar(kept[:], rank[:], float(CAP), None, ALU.is_lt))
            then(dve.tensor_scalar(side[:], onehot[:, :, 0], -1.0, 1.0, ALU.mult, ALU.add))
            then(dve.tensor_tensor(side[:], side[:], kept[:], ALU.mult))
            then(dve.tensor_scalar(base[:], side[:], -1.0, 1.0, ALU.mult, ALU.add))
            dve.tensor_copy(base_bf[:], base[:]).then_inc(base_ready, 1)
            then(dve.tensor_tensor(place_side[:], start_slot[:], rank[:], ALU.add))
            then(dve.tensor_tensor(place_side[:], place_side[:], side[:], ALU.mult))
            dve.wait_ge(counted, 1)
            total = r_bank[:, 32:34].rearrange("p a e -> p (a e)")
            then(dve.tensor_tensor_scan(upto[:], ones[:], total, 0.0, ALU.mult, ALU.add))
            then(dve.tensor_tensor(place[:], r_bank[:, 48:50].rearrange("p a e -> p (a e)"), upto[:], ALU.add))
            then(dve.tensor_tensor(place[:], total, place[:], ALU.subtract))
            then(dve.tensor_scalar(place[:], place[:], -1.0, base_slot[:], ALU.mult, ALU.add))
            then(dve.tensor_tensor(place[:], place[:], base[:], ALU.mult))
            dve.tensor_tensor(slot[:], place[:], place_side[:], ALU.add).then_inc(slots_ready, 1)
            then(dve.tensor_scalar(over[:], steps[:], upto[:, TILES - 1:TILES], None, ALU.is_lt))
            then(dve.tensor_reduce(many[:], over[:], AX.X, ALU.add))
            then(dve.tensor_scalar(many[:], many[:], 1.0, None, ALU.max))
            then(dve.tensor_tensor(first_unit[:, EXPERTS:], first_unit[:, SIDE:EXPERTS], many[:], ALU.add))
            then(dve.tensor_scalar(starts[:], first_unit[:], -1.0, None, ALU.add))

        @block.tensor
        def _(pe):
            pe.wait_ge(consts, 2)
            pe.wait_ge(router_loaded, 16)
            for j in range(TILES // 2):
                if j >= 2:
                    pe.wait_ge(x_ready, j - 1)
                for t in range(2):
                    for g in range(KT_):
                        ins = pe.transpose(x_bank[j % 2][:, g, t * P:(t + 1) * P], X[:, 2 * j + t, g * P:(g + 1) * P], ident[:])
                ins.then_inc(x_turned, 1)
                if j:
                    logit(pe, j - 1)
            logit(pe, TILES // 2 - 1)
            pe.wait_ge(consts, 10)
            pe.wait_ge(onehot_ready, 1)
            pe.matmul(l_bank[:, 0:4].rearrange("p a e -> p (a e)"), ones_bf[:], onehot_bf[:].rearrange("p t e -> p (t e)"),
                      start=True, stop=True).then_inc(tallied, 1)
            pe.wait_ge(key_ready, 1)
            for j in range(TILES):
                ins = pe.transpose(k_bank[:, j * P:(j + 1) * P], key[:, j:j + 1].broadcast_to((P, P)), ident[:])
                if j % 4 == 3:
                    ins.then_inc(keys_turned, 1)
            pe.wait_ge(compared, TILES)
            for i in range(TILES):
                for j in range(TILES):
                    ins = pe.matmul(r_bank[:, i], ahead[:, j, i * P:(i + 1) * P], onehot_bf[:, j],
                                    start=(j == 0), stop=(j == TILES - 1))
            ins.then_inc(ranks, 1)
            pe.wait_ge(base_ready, 1)
            pe.matmul(r_bank[:, 32:34].rearrange("p a e -> p (a e)"), ones_bf[:], base_bf[:], start=True, stop=True)
            pe.matmul(r_bank[:, 48:50].rearrange("p a e -> p (a e)"), before_bf[:], base_bf[:], start=True, stop=True).then_inc(counted, 1)


def experts(nc, router_dram, w1_dram, w2_dram, bias_dram, X):
    slots = nc.dram_tensor("slots", (SLOTS, DIM), F32, kind="Internal").ap()
    with ExitStack() as ctx:
        def sb(name, shape, dt=F32):
            return ctx.enter_context(nc.sbuf_tensor("ex_" + name, shape, dt))

        def sem(name):
            return ctx.enter_context(nc.semaphore("ex_" + name))

        slot = sb("slot", [P, TILES], I32)
        starts = sb("starts", [P, EXPERTS + 1], I32)
        stage1 = [sb(f"stage1{k}", [P, KT_, FF]) for k in range(2)]
        stage2 = [sb(f"stage2{k}", [P, FT, DIM]) for k in range(2)]
        w1h = [sb(f"w1h{k}", [P, KT_, FF], F16) for k in range(2)]
        w1l = [sb(f"w1l{k}", [P, KT_, FF], F16) for k in range(2)]
        w2h = [sb(f"w2h{k}", [P, FT, DIM], F16) for k in range(2)]
        w2l = [sb(f"w2l{k}", [P, FT, DIM], F16) for k in range(2)]
        biases = sb("biases", [P, EXPERTS, FT + KT_])
        bias = [sb(f"bias{k}", [P, FT + KT_]) for k in range(2)]

        biases_loaded = sem("biases_loaded")
        w_loaded = [sem("w_loaded0"), sem("w_loaded1")]
        w1_high = sem("w1_high")
        w2_high = sem("w2_high")
        bias_ready = sem("bias_ready")
        w1_low = sem("w1_low")
        w2_scaled = sem("w2_scaled")
        w2_low = sem("w2_low")

        def load_weights(sp, n, k):
            one = (lambda dram: dram[n]) if isinstance(n, int) else (lambda dram: dram[bass.ds(n, 1)].squeeze(0))
            sp.dma_start(stage1[k][:], one(w1_dram)).then_inc(w_loaded[k], 16)
            sp.dma_start(stage2[k][:], one(w2_dram)).then_inc(w_loaded[k], 16)

        def split1(dve, n, k):
            dve.wait_ge(w_loaded[k], 16 * (n - k) + 32)
            dve.tensor_scalar(w1h[k][:], stage1[k][:], SCALE, None, ALU.mult).then_inc(w1_high, 1)
            dve.wait_ge(w1_high, n + 1)
            dve.scalar_tensor_tensor(out=w1l[k][:], in0=stage1[k][:], scalar=SCALE, in1=w1h[k][:],
                                     op0=ALU.mult, op1=ALU.subtract).then_inc(w1_low, 1)

        def high2(act, n, k):
            act.wait_ge(w_loaded[k], 16 * (n - k) + 32)
            act.activation(w2h[k][:], stage2[k][:], ACT.Copy, scale=SCALE).then_inc(w2_high, 1)
            act.activation(bias[k][:], at(biases, n), ACT.Copy).then_inc(bias_ready, 1)

        def low2(pool, n):
            stage = stage2[n % 2]
            pool.wait_ge(w2_high, n + 1)
            pool.tensor_scalar(stage[:], stage[:], SCALE, 0.0, ALU.mult, ALU.add).then_inc(w2_scaled, 1)
            pool.wait_ge(w2_scaled, n + 1)
            pool.tensor_tensor(w2l[n % 2][:], stage[:], w2h[n % 2][:], ALU.subtract).then_inc(w2_low, 1)

        def first_loads(sp):
            load_weights(sp, 0, 0)
            load_weights(sp, 1, 1)
            sp.dma_start(biases[:], bias_dram).then_inc(biases_loaded, 16)

        def second_loads(sp):
            sp.wait_ge(w1_low, 1)
            sp.wait_ge(w2_low, 1)
            load_weights(sp, 2, 0)

        def first_lows(pool):
            for n in (0, 1):
                low2(pool, n)

        def first_split1(dve):
            for n in (0, 1):
                split1(dve, n, n)

        def first_high2(act):
            act.wait_ge(biases_loaded, 16)
            for n in (0, 1):
                high2(act, n, n)

        route(nc, router_dram, slots, X, slot, starts,
              {"sync": first_loads, "sync late": second_loads, "gpsimd": first_lows, "vector": first_split1, "scalar": first_high2})

        xe = sb("xe", [ROWS, 2, DIM])
        xh = sb("xh", [P, KT_, UNIT], F16)
        xl = sb("xl", [P, KT_, UNIT], F16)
        h = [sb(f"h{s}", [P, 2, UNIT]) for s in range(4)]
        hh = [sb(f"hh{s}", [P, 2, UNIT], F16) for s in range(4)]
        hl = [sb(f"hl{s}", [P, 2, UNIT], F16) for s in range(4)]
        yt = sb("yt", [P, KT_, UNIT])
        y = sb("y", [ROWS, 2, DIM])
        yg = sb("yg", [P, TILES, DIM])
        stats = sb("stats", [P, TILES, 6])
        mv = sb("mv", [P, TILES, 2])
        var_eps = sb("var_eps", [P, TILES])
        rstd = sb("rstd", [P, TILES])
        half = sb("half", [P, 1])
        mark = sb("mark", [1, 2], I32)
        ident = sb("ident", [P, P])

        x_bank = ctx.enter_context(nc.psum_tensor("ex_x_bank", [P, KT_, 256], F32))
        u_bank = [ctx.enter_context(nc.psum_tensor(f"ex_up{s}", [P, 2, 256], F32)) for s in range(4)]
        d_bank = [ctx.enter_context(nc.psum_tensor(f"ex_down{g}", [P, 512], F32)) for g in range(KT_)]
        y_bank = ctx.enter_context(nc.psum_tensor("ex_y_bank", [P, 2, DIM], F32))

        consts = sem("consts")
        x_loaded = sem("x_loaded")
        x_turned = sem("x_turned")
        x_high = sem("x_high")
        x_low = sem("x_low")
        up = sem("up")
        h_ready = sem("h_ready")
        h_high = sem("h_high")
        h_low = sem("h_low")
        down = sem("down")
        yt_ready = sem("yt_ready")
        y_turned = sem("y_turned")
        y_ready = sem("y_ready")
        stored = sem("stored")
        all_stored = sem("all_stored")
        all_loaded = sem("all_loaded")
        gathered = [sem(f"gathered{n}") for n in range(4)]
        summed = sem("summed")
        stat = sem("stat")
        mean_var = sem("mean_var")
        var_ready = sem("var_ready")
        rstd_ready = sem("rstd_ready")
        normed = sem("normed")

        def layer_norm(dve, n):
            dve.wait_ge(rstd_ready, n + 1)
            for j in range(4 * n, 4 * n + 4):
                dve.tensor_scalar(X[:, j], yg[:, j], mv[:, j, 0:1], rstd[:, j:j + 1], ALU.subtract, ALU.mult).then_inc(normed, 1)

        def start_of(engine, n):
            where = starts[0:1, n:n + 1] if isinstance(n, int) else starts[0:1, bass.ds(n, 1)]
            return engine.value_load(where, min_val=0, max_val=END - 1)

        def units_of(engine, n, k, unit, begin=None, prepare=None):
            a, z = start_of(engine, n), start_of(engine, n + 1)
            if begin:
                begin(n, k)
            if prepare:
                prepare(n + 1, 1 - k, a)
            with engine.Fori(a, z) as u:
                unit(u + 1, k, n)

        def all_units(engine, unit, begin=None, prepare=None):
            units_of(engine, 0, 0, unit, begin)
            with engine.Fori(0, SIDE // 2) as i:
                units_of(engine, 2 * i + 1, 1, unit, begin, prepare)
                units_of(engine, 2 * i + 2, 0, unit, begin, prepare)
            units_of(engine, SIDE, 1, unit, begin)

        block = ctx.enter_context(nc.Block())

        @block.sync
        def _(sp):
            def rows(u):
                return slots[bass.ds(u * UNIT, UNIT)].rearrange("(t p) d -> p t d", p=ROWS)

            def load(u):
                sp.dma_start(xe[:], rows(u)).then_inc(x_loaded, 16)

            def store(u):
                sp.wait_ge(y_ready, u + 1)
                sp.dma_start(rows(u), y[:]).then_inc(stored, 16)

            sp.dma_start(mark[0:1, 0:1], starts[0:1, 0:1]).then_inc(stored, 16)
            load(1)
            sp.wait_ge(x_turned, 1)
            load(2)

            def unit(u, k, n):
                sp.wait_ge(x_turned, u + 1)
                load(u + 2)
                store(u - 1)

            def more_weights(n, k):
                sp.wait_ge(w1_low, n + 1)
                sp.wait_ge(w2_low, n + 1)
                load_weights(sp, n + 2, k)

            units_of(sp, 0, 0, unit)
            with sp.Fori(0, SIDE // 2 - 1) as i:
                units_of(sp, 2 * i + 1, 1, unit, more_weights)
                units_of(sp, 2 * i + 2, 0, unit, more_weights)
            units_of(sp, SIDE - 2, 1, unit, more_weights)
            units_of(sp, SIDE - 1, 0, unit)
            units_of(sp, SIDE, 1, unit)
            last = start_of(sp, EXPERTS)
            store(last)
            sp.wait_ge(stored, last * 16 + 32)
            sp.dma_start(mark[0:1, 0:1], starts[0:1, 0:1]).then_inc(all_stored, 16)
            sp.wait_ge(x_loaded, last * 16 + 32)
            sp.dma_start(mark[0:1, 1:2], starts[0:1, 0:1]).then_inc(all_loaded, 16)
            sp.wait_ge(all_loaded, 16)

        @block.gpsimd
        def _(pool):
            identity(pool, ident, consts, 1).then_inc(consts, 1)
            pool.memset(yt[:], 0.0).then_inc(yt_ready, 1)
            pool.memset(half[:], -0.5).then_inc(consts, 1)
            pool.wait_ge(consts, 3)
            for n in range(2, EXPERTS):
                low2(pool, n)
            pool.wait_ge(all_stored, 16)
            for j in range(TILES):
                pool.indirect_dma_start(out=yg[:, j], out_offset=None, in_=slots[:, :],
                                        in_offset=bass.IndirectOffsetOnAxis(ap=slot[:, j:j + 1], axis=0)).then_inc(gathered[j // 4], 16)
            for n in range(4):
                pool.wait_ge(var_ready, n + 1)
                pool.tensor_tensor(rstd[:, 4 * n:4 * n + 4], var_eps[:, 4 * n:4 * n + 4], half[:].broadcast_to((P, 4)), ALU.pow).then_inc(rstd_ready, 1)

        @block.scalar
        def _(act):
            def split_x(u):
                act.wait_ge(x_turned, u)
                act.activation(xh[:], x_bank[:, :, 0:UNIT], ACT.Copy, scale=SCALE).then_inc(x_high, 1)

            def unit(u, k, n):
                for s in range(4):
                    act.wait_ge(up, u * 4 + s - 3)
                    for j in range(2):
                        m = 2 * s + j
                        ins = act.activation(h[s][:, j], u_bank[s][:, j, 0:UNIT], ACT.Relu, scale=UNSCALE, bias=bias[k][:, m:m + 1])
                    ins.then_inc(h_ready, 1)
                split_x(u + 1)
                for g in range(KT_):
                    act.wait_ge(down, u * KT_ + g - 1)
                    act.activation(yt[:, g], d_bank[g][:, 0:UNIT], ACT.Identity, scale=1.0 / (SCALE * HSCALE),
                                   bias=bias[k][:, FT + g:FT + g + 1]).then_inc(yt_ready, 1)

            def prepare(n, k, a):
                act.wait_ge(yt_ready, a * KT_ + 1)
                high2(act, n, k)

            act.wait_ge(bias_ready, 2)
            split_x(1)
            all_units(act, unit, prepare=prepare)

        @block.vector
        def _(dve):
            def split_x(u):
                dve.wait_ge(x_high, u)
                dve.scalar_tensor_tensor(out=xl[:], in0=x_bank[:, :, 0:UNIT], scalar=SCALE, in1=xh[:],
                                         op0=ALU.mult, op1=ALU.subtract).then_inc(x_low, 1)

            def take_y(u):
                dve.wait_ge(y_turned, u + 1)
                dve.wait_ge(stored, u * 16 + 16)
                dve.tensor_copy(y[:], y_bank[0:ROWS]).then_inc(y_ready, 1)

            def unit(u, k, n):
                for s in range(4):
                    dve.wait_ge(h_ready, u * 4 + s - 3)
                    dve.tensor_scalar(hh[s][:], h[s][:], HSCALE, None, ALU.mult).then_inc(h_high, 1)
                    dve.wait_ge(h_high, u * 4 + s - 3)
                    dve.scalar_tensor_tensor(out=hl[s][:], in0=h[s][:], scalar=HSCALE, in1=hh[s][:],
                                             op0=ALU.mult, op1=ALU.subtract).then_inc(h_low, 1)
                    if s == 1:
                        take_y(u - 1)
                split_x(u + 1)

            def prepare(n, k, a):
                dve.wait_ge(yt_ready, a * KT_ + 1)
                split1(dve, n, k)

            split_x(1)
            all_units(dve, unit, prepare=prepare)
            take_y(start_of(dve, EXPERTS))
            for n in range(4):
                t = slice(4 * n, 4 * n + 4)
                dve.wait_ge(gathered[n], 64)
                dve.tensor_tensor(yg[:, t], yg[:, t], X[:, t], ALU.add).then_inc(summed, 1)
                dve.wait_ge(summed, n + 1)
                for j in range(4 * n, 4 * n + 4):
                    ins = dve.bn_stats(stats[:, j], yg[:, j])
                ins.then_inc(stat, 1)
                dve.wait_ge(stat, n + 1)
                for j in range(4 * n, 4 * n + 4):
                    ins = dve.bn_aggr(mv[:, j], stats[:, j])
                ins.then_inc(mean_var, 1)
                dve.wait_ge(mean_var, n + 1)
                dve.tensor_scalar(var_eps[:, t], mv[:, t, 1], EPS, None, ALU.add).then_inc(var_ready, 1)
                if n:
                    layer_norm(dve, n - 1)
            layer_norm(dve, 3)

        @block.tensor
        def _(pe):
            def turn_x(u):
                pe.wait_ge(x_loaded, u * 16)
                for g in range(KT_):
                    for t in range(2):
                        ins = pe.transpose(x_bank[:, g, t * ROWS:(t + 1) * ROWS], xe[:, t, g * P:(g + 1) * P], ident[0:ROWS, 0:ROWS])
                ins.then_inc(x_turned, 1)

            def turn_y(u):
                pe.wait_ge(yt_ready, u * KT_ + 1)
                for g in range(KT_):
                    for t in range(2):
                        ins = pe.transpose(y_bank[0:ROWS, t, g * P:(g + 1) * P], yt[:, g, t * ROWS:(t + 1) * ROWS], ident[:])
                ins.then_inc(y_turned, 1)

            def way_up(u, k, s):
                for j in range(2):
                    m, n = 2 * s + j, 0
                    for g in range(KT_):
                        for w, x in ((w1h[k], xh), (w1h[k], xl), (w1l[k], xh)):
                            ins = pe.matmul(u_bank[s][:, j, 0:UNIT], w[:, g, m * P:(m + 1) * P], x[:, g],
                                            start=(n == 0), stop=(n == 3 * KT_ - 1))
                            n += 1
                ins.then_inc(up, 1)

            def way_down(u, k, s):
                pe.wait_ge(h_low, u * 4 + s - 3)
                for g in range(KT_):
                    for j in range(2):
                        m = 2 * s + j
                        for n, (w, x) in enumerate(((w2h[k], hh[s]), (w2h[k], hl[s]), (w2l[k], hh[s]))):
                            ins = pe.matmul(d_bank[g][:, 0:UNIT], w[:, m, g * P:(g + 1) * P], x[:, j],
                                            start=(m == 0 and n == 0), stop=(m == FT - 1 and n == 2))
                    if s == 3:
                        ins.then_inc(down, 1)

            def unit(u, k, n):
                pe.wait_ge(w1_low, n + 1)
                pe.wait_ge(w2_low, n + 1)
                pe.wait_ge(x_low, u)
                way_up(u, k, 0)
                turn_y(u - 1)
                way_up(u, k, 1)
                way_up(u, k, 2)
                way_down(u, k, 0)
                way_up(u, k, 3)
                way_down(u, k, 1)
                way_down(u, k, 2)
                turn_x(u + 1)
                way_down(u, k, 3)

            pe.wait_ge(consts, 2)
            turn_x(1)
            all_units(pe, unit)
            turn_y(start_of(pe, EXPERTS))


HID = 512
HT = HID // P
TAPS = 4
SERIES = 9


def recurrence(nc, w_in_dram, w_g_dram, w_out_dram, hid_dram, X):
    with ExitStack() as ctx:
        def sb(name, shape, dt=F32):
            return ctx.enter_context(nc.sbuf_tensor("re_" + name, shape, dt))

        def sem(name):
            return ctx.enter_context(nc.semaphore("re_" + name))

        w_in = sb("w_in", [P, KT_, 2 * HID])
        w_g = sb("w_g", [P, HT, 2 * HID])
        w_out = sb("w_out", [P, HT, DIM])
        hid = sb("hid", [P, TAPS + 4, HT])
        half_bias = sb("half_bias", [P, 2, HT])
        rate = sb("rate", [P, HT])
        low, power = sb("low", [P, HT]), sb("power", [P, HT])
        ratio, square, series = sb("ratio", [P, HT]), sb("square", [P, HT]), sb("series", [P, HT])
        tiny = sb("tiny", [P, 1])
        ident = sb("ident", [P, P])
        xs = [sb(f"xs{k}", [P, TPB, DIM]) for k in range(2)]
        xt = sb("xt", [P, KT_, SEQ])
        padded = sb("padded", [P, HT, TAPS - 1 + SEQ])
        conv = [sb(f"conv{k}", [P, HT, SEQ]) for k in range(2)]
        gate = [sb(f"gate{k}", [P, HT, SEQ]) for k in range(2)]
        tf = sb("tf", [P, 2, SEQ])
        ti = [sb(f"ti{p}", [P, 2, SEQ]) for p in range(2)]
        T = [sb(f"T{p}", [P, 2, SEQ]) for p in range(2)]
        more = [sb(f"more{p}", [P, 2, SEQ]) for p in range(2)]
        recip = [sb(f"recip{p}", [P, 2, SEQ]) for p in range(2)]
        d = [sb(f"d{p}", [P, 2, SEQ]) for p in range(2)]
        nb = [sb(f"nb{p}", [P, 2, SEQ]) for p in range(2)]
        alpha = [sb(f"alpha{p}", [P, 2, SEQ]) for p in range(2)]
        beta = [sb(f"beta{p}", [P, 2, SEQ]) for p in range(2)]
        scaled = [sb(f"scaled{p}", [P, 2, SEQ]) for p in range(2)]
        bterm = [sb(f"bterm{p}", [P, 2, SEQ]) for p in range(2)]
        h = [sb(f"h{p}", [P, 2, SEQ]) for p in range(2)]
        gh = sb("gh", [P, HT, SEQ])

        x_bank = ctx.enter_context(nc.psum_tensor("re_x", [P, KT_, SEQ], F32))
        i_bank = [ctx.enter_context(nc.psum_tensor(f"re_in{k}", [P, 2, SEQ], F32)) for k in range(2)]
        g_bank = [ctx.enter_context(nc.psum_tensor(f"re_g{m}", [P, 2, SEQ], F32)) for m in range(HT)]
        o_bank = ctx.enter_context(nc.psum_tensor("re_out", [P, TPB, DIM], F32))

        norm = Norm(ctx, nc, "re")
        hid_loaded = sem("hid_loaded")
        in_loaded = sem("in_loaded")
        g_loaded = sem("g_loaded")
        out_loaded = sem("out_loaded")
        staged = [sem("staged0"), sem("staged1")]
        consts = sem("consts")
        setup = sem("setup")
        setup_act = sem("setup_act")
        x_turned = sem("x_turned")
        x_ready = sem("x_ready")
        in_done = sem("in_done")
        in_read = sem("in_read")
        conved = sem("conved")
        g_done = sem("g_done")
        tf_done = sem("tf_done")
        ti_done = sem("ti_done")
        T_done = sem("T_done")
        chain = sem("chain")
        beta_ready = sem("beta_ready")
        doubled = sem("doubled")
        scaled_ready = sem("scaled_ready")
        bterm_ready = sem("bterm_ready")
        scanned = sem("scanned")
        gated = sem("gated")
        out_done = sem("out_done")
        summed = sem("summed")

        def both(batch):
            def run(engine):
                batch(0, 0, before=False)
                with engine.Fori(0, BATCH // 2 - 1) as i:
                    batch(2 * i + 1, 1)
                    batch(2 * i + 2, 0)
                batch(BATCH - 1, 1, after=False)
            return run

        block = ctx.enter_context(nc.Block())

        @block.sync
        def _(sp):
            def stage(b, par):
                sp.dma_start(xs[par][:], X[:, bass.ds(b * TPB, TPB)]).then_inc(staged[par], 16)

            stage(0, 0)
            sp.dma_start(hid[:], hid_dram).then_inc(hid_loaded, 16)
            sp.dma_start(w_in[:], w_in_dram).then_inc(in_loaded, 16)
            stage(1, 1)
            sp.dma_start(w_g[:], w_g_dram).then_inc(g_loaded, 16)
            sp.dma_start(w_out[:], w_out_dram).then_inc(out_loaded, 16)
            for b in (0, 1):
                sp.wait_ge(x_turned, b + 1)
                stage(b + 2, b)
            with sp.Fori(1, BATCH // 2 - 1) as i:
                for par in range(2):
                    sp.wait_ge(x_turned, 2 * i + par + 1)
                    stage(2 * i + par + 2, par)

        @block.gpsimd
        def _(pool):
            identity(pool, ident, consts, 1).then_inc(consts, 1)
            pool.memset(tiny[:], 0.25e-6).then_inc(consts, 1)
            pool.memset(norm.half[:], -0.5).then_inc(consts, 1)
            pool.wait_ge(consts, 4)

            def scale_input(b, par, p):
                c = conv[par][:, 2 * p:2 * p + 2]
                pool.wait_ge(ti_done, b * HT + 2 * p + 2)
                if not first(b):
                    pool.wait_ge(bterm_ready, 2 * b + p - 1)
                pool.tensor_tensor(scaled[p][:], ti[p][:], c, ALU.mult).then_inc(doubled, 1)
                pool.wait_ge(doubled, 2 * b + p + 1)
                pool.tensor_tensor(scaled[p][:], scaled[p][:], c, ALU.add).then_inc(scaled_ready, 1)

            def times_beta(b, p):
                pool.wait_ge(scaled_ready, 2 * b + p + 1)
                pool.wait_ge(beta_ready, 2 * b + p + 1)
                pool.tensor_tensor(bterm[p][:], scaled[p][:], beta[p][:], ALU.mult).then_inc(bterm_ready, 1)

            def batch(b, par, before=True, after=True):
                if before:
                    times_beta(b - 1, 1)
                    norm.root(pool, b - 1, 0)
                    norm.root(pool, b - 1, 1)
                scale_input(b, par, 0)
                times_beta(b, 0)
                scale_input(b, par, 1)

            both(batch)(pool)
            times_beta(BATCH - 1, 1)
            norm.root(pool, BATCH - 1, 0)
            norm.root(pool, BATCH - 1, 1)

        @block.scalar
        def _(act):
            act.wait_ge(setup, 1)
            act.activation(power[:], low[:], ACT.Exp).then_inc(setup_act, 1)
            act.wait_ge(setup, 2 * SERIES + 9)
            act.wait_ge(consts, 3)

            def tokens(b):
                act.wait_ge(x_turned, b + 1)
                act.activation(xt[:], x_bank[:], ACT.Copy).then_inc(x_ready, 1)

            def conv_input(b):
                if not first(b):
                    act.wait_ge(conved, b * TAPS * HT)
                for p in range(2):
                    act.wait_ge(in_done, 4 * b + p + 1)
                    act.activation(padded[:, 2 * p:2 * p + 2, TAPS - 1:], i_bank[p][:], ACT.Copy).then_inc(in_read, 1)

            def gates(b, par):
                if not (isinstance(b, int) and b < 2):
                    act.wait_ge(gated, 2 * b - 2)
                for p in range(2):
                    act.wait_ge(in_done, 4 * b + 2 + p + 1)
                    act.activation(gate[par][:, 2 * p:2 * p + 2], i_bank[p][:], ACT.Gelu).then_inc(in_read, 1)

            def tile(b, m):
                p, k = divmod(m, 2)
                act.wait_ge(g_done, b * HT + m + 1)
                if not (first(b) and m < 2):
                    act.wait_ge(T_done, b * HT + m - 1)
                act.activation(tf[:, k], g_bank[m][:, 0], ACT.Tanh, scale=0.5, bias=half_bias[:, 0, m:m + 1]).then_inc(tf_done, 1)
                if not first(b):
                    act.wait_ge(scaled_ready, 2 * b + p - 1)
                act.activation(ti[p][:, k], g_bank[m][:, 1], ACT.Tanh, scale=0.5, bias=half_bias[:, 1, m:m + 1]).then_inc(ti_done, 1)
                act.wait_ge(tf_done, b * HT + m + 1)
                if not first(b):
                    act.wait_ge(chain, 10 * b + 5 * p - 7)
                act.activation(T[p][:, k], tf[:, k], ACT.Tanh, scale=rate[:, m:m + 1], bias=rate[:, m:m + 1]).then_inc(T_done, 1)

            def root(b, p):
                act.wait_ge(chain, 10 * b + 5 * p + 4)
                act.activation(beta[p][:], nb[p][:], ACT.Sqrt, scale=-0.25, bias=tiny[:]).then_inc(beta_ready, 1)

            def batch(b, par, before=True, after=True):
                if after:
                    tokens(b + 1)
                    conv_input(b + 1)
                if before:
                    root(b - 1, 1)
                tile(b, 0)
                if after:
                    gates(b + 1, 1 - par)
                tile(b, 1)
                tile(b, 2)
                root(b, 0)
                tile(b, 3)

            tokens(0)
            conv_input(0)
            gates(0, 0)
            both(batch)(act)
            root(BATCH - 1, 1)

        @block.vector
        def _(dve):
            done = [0]

            def then(ins):
                done[0] += 1
                ins.then_inc(setup, 1)
                dve.wait_ge(setup, done[0])

            base = hid[:, TAPS + 3]
            dve.wait_ge(hid_loaded, 16)
            then(dve.scalar_tensor_tensor(out=low[:], in0=base, scalar=-1.0, in1=base, op0=ALU.mult, op1=ALU.min))
            dve.wait_ge(setup_act, 1)
            then(dve.tensor_scalar(ratio[:], power[:], 2.0, None, ALU.add))
            then(dve.reciprocal(square[:], ratio[:]))
            then(dve.tensor_tensor(ratio[:], power[:], square[:], ALU.mult))
            then(dve.tensor_tensor(square[:], ratio[:], ratio[:], ALU.mult))
            then(dve.memset(series[:], 1.0 / (2 * SERIES + 1)))
            for n in reversed(range(SERIES)):
                then(dve.tensor_tensor(series[:], series[:], square[:], ALU.mult))
                then(dve.tensor_scalar(series[:], series[:], 1.0 / (2 * n + 1), None, ALU.add))
            then(dve.scalar_tensor_tensor(out=series[:], in0=ratio[:], scalar=2.0, in1=series[:], op0=ALU.mult, op1=ALU.mult))
            then(dve.scalar_tensor_tensor(out=rate[:], in0=base, scalar=0.0, in1=series[:], op0=ALU.max, op1=ALU.add))
            dve.tensor_scalar(rate[:], rate[:], 2.0, None, ALU.mult)
            dve.memset(padded[:, :, 0:TAPS - 1], 0.0)
            then(dve.tensor_scalar(half_bias[:], hid[:, TAPS + 1:TAPS + 3], 0.5, None, ALU.mult))

            def convolve(b, par, p):
                dve.wait_ge(in_read, 4 * b + p + 1)
                if not (isinstance(b, int) and b < 2):
                    dve.wait_ge(scaled_ready, 2 * b - 2)
                for tap in range(TAPS):
                    for k in range(2):
                        m = 2 * p + k
                        out, x, w = conv[par][:, m], padded[:, m, tap:tap + SEQ], hid[:, tap, m:m + 1]
                        if tap == 0:
                            ins = dve.tensor_scalar(out, x, w, hid[:, TAPS, m:m + 1], ALU.mult, ALU.add)
                        else:
                            dve.wait_ge(conved, b * TAPS * HT + TAPS * 2 * p + 2 * tap + k - 1)
                            ins = dve.scalar_tensor_tensor(out=out, in0=x, scalar=w, in1=out, op0=ALU.mult, op1=ALU.add)
                        ins.then_inc(conved, 1)

            def decay(b, p):
                n = 10 * b + 5 * p
                dve.wait_ge(T_done, b * HT + 2 * p + 2)
                dve.tensor_scalar(more[p][:], T[p][:], 1.0, None, ALU.add).then_inc(chain, 1)
                dve.wait_ge(chain, n + 1)
                dve.reciprocal(recip[p][:], more[p][:]).then_inc(chain, 1)
                dve.wait_ge(chain, n + 2)
                dve.scalar_tensor_tensor(out=d[p][:], in0=T[p][:], scalar=2.0, in1=recip[p][:], op0=ALU.mult, op1=ALU.mult).then_inc(chain, 1)
                dve.wait_ge(chain, n + 3)
                dve.scalar_tensor_tensor(out=nb[p][:], in0=d[p][:], scalar=-2.0, in1=d[p][:], op0=ALU.add, op1=ALU.mult).then_inc(chain, 1)
                dve.tensor_scalar(alpha[p][:], d[p][:], -1.0, 1.0, ALU.mult, ALU.add).then_inc(chain, 1)

            def scan(b, par, p):
                dve.wait_ge(bterm_ready, 2 * b + p + 1)
                dve.wait_ge(chain, 10 * b + 5 * p + 5)
                for k in range(2):
                    ins = dve.tensor_tensor_scan(h[p][:, k], alpha[p][:, k], bterm[p][:, k], 0.0, ALU.mult, ALU.add)
                ins.then_inc(scanned, 1)
                dve.wait_ge(scanned, 2 * b + p + 1)
                dve.wait_ge(in_read, 4 * b + 4)
                dve.tensor_tensor(gh[:, 2 * p:2 * p + 2], gate[par][:, 2 * p:2 * p + 2], h[p][:], ALU.mult).then_inc(gated, 1)

            def residual(b):
                dve.wait_ge(out_done, b + 1)
                for t in range(TPB):
                    dve.tensor_tensor(norm.res[:, t], o_bank[:, t], at(X, b * TPB + t), ALU.add).then_inc(summed, 1)
                    dve.wait_ge(summed, b * TPB + t + 1)
                    norm.statistics(dve, b, t)

            def layer_norm(b):
                for t in range(TPB):
                    norm.apply(dve, b, t, at(X, b * TPB + t))

            def batch(b, par, before=True, after=True):
                if after:
                    convolve(b + 1, 1 - par, 0)
                if before:
                    scan(b - 1, 1 - par, 1)
                if after:
                    convolve(b + 1, 1 - par, 1)
                if before:
                    residual(b - 1)
                decay(b, 0)
                if before:
                    layer_norm(b - 1)
                scan(b, par, 0)
                decay(b, 1)

            convolve(0, 0, 0)
            convolve(0, 0, 1)
            both(batch)(dve)
            scan(BATCH - 1, 1, 1)
            residual(BATCH - 1)
            layer_norm(BATCH - 1)

        @block.tensor
        def _(pe):
            def way_in(b, par):
                pe.wait_ge(staged[par], 8 * (b - par) + 16)
                if not first(b):
                    pe.wait_ge(x_ready, b)
                for g in range(KT_):
                    for t in range(TPB):
                        ins = pe.transpose(x_bank[:, g, t * P:(t + 1) * P], xs[par][:, t, g * P:(g + 1) * P], ident[:])
                ins.then_inc(x_turned, 1)
                pe.wait_ge(x_ready, b + 1)
                for s in range(4):
                    if not (first(b) and s < 2):
                        pe.wait_ge(in_read, 4 * b + s - 1)
                    for k in range(2):
                        m = (HT + 2 * s + k) % (2 * HT)
                        for g in range(KT_):
                            ins = pe.matmul(i_bank[s % 2][:, k], w_in[:, g, m * P:(m + 1) * P], xt[:, g],
                                            start=(g == 0), stop=(g == KT_ - 1))
                    ins.then_inc(in_done, 1)

            def tile(b, par, m):
                if m == 0:
                    pe.wait_ge(conved, (b + 1) * TAPS * HT)
                if not first(b):
                    pe.wait_ge(ti_done, b * HT + m - HT + 1)
                for k in range(2):
                    cols = slice(k * HID + m * P, k * HID + (m + 1) * P)
                    for j in range(HT):
                        ins = pe.matmul(g_bank[m][:, k], w_g[:, j, cols], conv[par][:, j], start=(j == 0), stop=(j == HT - 1))
                ins.then_inc(g_done, 1)

            def way_out(b):
                pe.wait_ge(gated, 2 * b + 2)
                for t in range(TPB):
                    for j in range(HT):
                        ins = pe.matmul(o_bank[:, t], gh[:, j, t * P:(t + 1) * P], w_out[:, j], start=(j == 0), stop=(j == HT - 1))
                ins.then_inc(out_done, 1)

            def batch(b, par, before=True, after=True):
                if after:
                    way_in(b + 1, 1 - par)
                tile(b, par, 0)
                if before:
                    way_out(b - 1)
                for m in range(1, HT):
                    tile(b, par, m)

            pe.wait_ge(consts, 2)
            pe.wait_ge(in_loaded, 16)
            way_in(0, 0)
            pe.wait_ge(g_loaded, 16)
            pe.wait_ge(out_loaded, 16)
            both(batch)(pe)
            way_out(BATCH - 1)




def binary_ffn(nc, w1_dram, w2_dram, b1_dram, b2_dram, X, out):
    with ExitStack() as ctx:
        def sb(name, shape, dt=F32):
            return ctx.enter_context(nc.sbuf_tensor("bf_" + name, shape, dt))

        def sem(name):
            return ctx.enter_context(nc.semaphore("bf_" + name))

        w1 = sb("w1", [P, KT_, FF])
        w2 = sb("w2", [P, FT, DIM])
        size1, size2 = sb("size1", [P, KT_, FF]), sb("size2", [P, FT, DIM])
        below1, below2 = sb("below1", [P, KT_, FF], F16), sb("below2", [P, FT, DIM], F16)
        sign1, sign2 = sb("sign1", [P, KT_, FF], F16), sb("sign2", [P, FT, DIM], F16)
        alpha1 = sb("alpha1", [P, FT])
        alpha2 = sb("alpha2", [P, DIM])
        b1 = sb("b1", [P, FT])
        b2 = sb("b2", [P, DIM])
        ones = sb("ones", [P, P])
        ident = sb("ident", [P, P])
        xs = [sb(f"xs{k}", [P, TPB, DIM]) for k in range(2)]
        xb = [sb(f"xb{k}", [P, TPB, DIM]) for k in range(2)]
        xh = [sb(f"xh{k}", [P, KT_, SEQ], F16) for k in range(2)]
        xl = [sb(f"xl{k}", [P, KT_, SEQ], F16) for k in range(2)]
        h = sb("h", [P, FT, SEQ])
        hh = [sb(f"hh{k}", [P, FT, SEQ], F16) for k in range(2)]
        hl = [sb(f"hl{k}", [P, FT, SEQ], F16) for k in range(2)]
        scaled = sb("scaled", [P, TPB, DIM])
        y = [sb(f"y{k}", [P, TPB, DIM]) for k in range(2)]

        x_bank = ctx.enter_context(nc.psum_tensor("bf_x", [P, KT_, SEQ], F32))
        u_bank = [ctx.enter_context(nc.psum_tensor(f"bf_up{k}", [P, 2, SEQ], F32)) for k in range(4)]
        o_bank = [ctx.enter_context(nc.psum_tensor(f"bf_out{k}", [P, 512], F32)) for k in range(TPB)]
        a_bank = ctx.enter_context(nc.psum_tensor("bf_alpha", [P, 512], F32))

        norm = Norm(ctx, nc, "bf")
        w1_loaded = sem("w1_loaded")
        w2_loaded = sem("w2_loaded")
        biases_loaded = sem("biases_loaded")
        staged = [sem("staged0"), sem("staged1")]
        stored = [sem("stored0"), sem("stored1")]
        consts = sem("consts")
        sized = sem("sized")
        below = sem("below")
        signed = sem("signed")
        totals = sem("totals")
        alphas = sem("alphas")
        xb_ready = sem("xb_ready")
        x_turned = sem("x_turned")
        x_high = sem("x_high")
        x_low = sem("x_low")
        up = sem("up")
        h_ready = sem("h_ready")
        h_high = sem("h_high")
        h_low = sem("h_low")
        down = sem("down")
        times_alpha = sem("times_alpha")
        summed = sem("summed")

        def all_batches(batch):
            def run(engine):
                batch(0, 0)
                batch(1, 1)
                with engine.Fori(1, BATCH // 2 - 1) as i:
                    batch(2 * i, 0)
                    batch(2 * i + 1, 1)
                batch(BATCH - 2, 0, ahead=1)
                batch(BATCH - 1, 1, ahead=0)
            return run

        block = ctx.enter_context(nc.Block())

        @block.sync
        def _(sp):
            def stage(b, par):
                sp.dma_start(xs[par][:], X[:, bass.ds(b * TPB, TPB)]).then_inc(staged[par], 16)

            def restage(b, par):
                sp.wait_ge(x_turned, b + 1)
                sp.wait_ge(xb_ready, b + 1)
                stage(b + 2, par)

            def store(b, par):
                sp.wait_ge(norm.ln_done, (b + 1) * TPB)
                where = out[b] if isinstance(b, int) else out[bass.ds(b, 1)].squeeze(0)
                sp.dma_start(where.rearrange("(t p) d -> p t d", p=P), y[par][:]).then_inc(stored[par], 16)

            sp.dma_start(w1[:], w1_dram).then_inc(w1_loaded, 16)
            stage(0, 0)
            stage(1, 1)
            sp.dma_start(w2[:], w2_dram).then_inc(w2_loaded, 16)
            sp.dma_start(b1[:], b1_dram).then_inc(biases_loaded, 16)
            sp.dma_start(b2[:], b2_dram).then_inc(biases_loaded, 16)
            restage(0, 0)
            restage(1, 1)
            with sp.Fori(0, BATCH // 2 - 2) as i:
                for par in range(2):
                    restage(2 * i + par + 2, par)
                    store(2 * i + par, par)
            for b in range(BATCH - 4, BATCH):
                store(b, b % 2)
            for par in range(2):
                sp.wait_ge(stored[par], 16 * (BATCH // 2))

        @block.gpsimd
        def _(pool):
            identity(pool, ident, consts, 1).then_inc(consts, 1)
            pool.memset(ones[:], 1.0).then_inc(consts, 1)
            pool.memset(norm.half[:], -0.5).then_inc(consts, 1)
            pool.wait_ge(consts, 4)
            pool.wait_ge(biases_loaded, 32)

            def add_bias(b, par):
                pool.wait_ge(staged[par], 8 * (b - par) + 16)
                if not (isinstance(b, int) and b < 2):
                    pool.wait_ge(summed, (b - 1) * TPB)
                for t in range(TPB):
                    ins = pool.tensor_tensor(xb[par][:, t], xs[par][:, t], b2[:], ALU.add)
                ins.then_inc(xb_ready, 1)

            def batch(b, par, ahead=2):
                norm.root(pool, b, 0)
                norm.root(pool, b, 1)
                if ahead == 2:
                    add_bias(b + 2, par)

            add_bias(0, 0)
            add_bias(1, 1)
            all_batches(batch)(pool)

        @block.scalar
        def _(act):
            def tokens(b, par):
                act.wait_ge(x_turned, b + 1)
                if not (isinstance(b, int) and b < 2):
                    act.wait_ge(up, (b - 1) * 4)
                act.activation(xh[par][:], x_bank[:], ACT.Copy, scale=SCALE).then_inc(x_high, 1)

            def hidden(b, s):
                act.wait_ge(up, 4 * b + s + 1)
                if not first(b):
                    act.wait_ge(h_low, 4 * b + s - 3)
                for k in range(2):
                    m = 2 * s + k
                    ins = act.activation(h[:, m], u_bank[s][:, k], ACT.Gelu, scale=alpha1[:, m:m + 1], bias=b1[:, m:m + 1])
                ins.then_inc(h_ready, 1)

            def high(b, par, s):
                act.wait_ge(h_ready, 4 * b + s + 1)
                if not (isinstance(b, int) and b < 2):
                    act.wait_ge(down, (b - 1) * TPB)
                act.activation(hh[par][:, 2 * s:2 * s + 2], h[:, 2 * s:2 * s + 2], ACT.Copy, scale=HSCALE).then_inc(h_high, 1)

            def all_hidden(b, par):
                hidden(b, 0)
                for s in range(1, 4):
                    hidden(b, s)
                    high(b, par, s - 1)
                high(b, par, 3)

            def batch(b, par, ahead=2):
                if ahead == 2:
                    tokens(b + 2, par)
                if ahead:
                    all_hidden(b + 1, 1 - par)

            act.wait_ge(biases_loaded, 32)
            tokens(0, 0)
            tokens(1, 1)
            act.wait_ge(alphas, 2)
            all_hidden(0, 0)
            all_batches(batch)(act)

        @block.vector
        def _(dve):
            def tokens_low(b, par):
                dve.wait_ge(x_high, b + 1)
                dve.scalar_tensor_tensor(out=xl[par][:], in0=x_bank[:], scalar=SCALE, in1=xh[par][:],
                                         op0=ALU.mult, op1=ALU.subtract).then_inc(x_low, 1)

            def low(b, par, s):
                dve.wait_ge(h_high, 4 * b + s + 1)
                t = slice(2 * s, 2 * s + 2)
                dve.scalar_tensor_tensor(out=hl[par][:, t], in0=h[:, t], scalar=HSCALE, in1=hh[par][:, t],
                                         op0=ALU.mult, op1=ALU.subtract).then_inc(h_low, 1)

            def residual(b, par, t):
                dve.wait_ge(down, b * TPB + t + 1)
                if not first(b):
                    dve.wait_ge(summed, b * TPB + t - 1)
                dve.tensor_tensor(scaled[:, t], o_bank[t][:, 0:DIM], alpha2[:], ALU.mult).then_inc(times_alpha, 1)
                dve.wait_ge(times_alpha, b * TPB + t + 1)
                dve.wait_ge(xb_ready, b + 1)
                if not first(b):
                    dve.wait_ge(norm.ln_done, b * TPB)
                dve.tensor_tensor(norm.res[:, t], scaled[:, t], xb[par][:, t], ALU.add).then_inc(summed, 1)
                dve.wait_ge(summed, b * TPB + t + 1)
                norm.statistics(dve, b, t)

            def batch(b, par, ahead=2):
                if ahead == 2:
                    tokens_low(b + 2, par)
                if ahead:
                    low(b + 1, 1 - par, 0)
                    low(b + 1, 1 - par, 1)
                residual(b, par, 0)
                residual(b, par, 1)
                if ahead:
                    low(b + 1, 1 - par, 2)
                    low(b + 1, 1 - par, 3)
                if not (isinstance(b, int) and b < 2):
                    dve.wait_ge(stored[par], 8 * (b - par))
                for t in range(TPB):
                    norm.apply(dve, b, t, y[par][:, t])

            def split_weight(w, size, negative, sign, n):
                dve.scalar_tensor_tensor(out=size[:], in0=w[:], scalar=-1.0, in1=w[:], op0=ALU.mult, op1=ALU.max).then_inc(sized, 1)
                dve.tensor_scalar(negative[:], w[:], 0.0, None, ALU.is_lt).then_inc(below, 1)
                dve.wait_ge(below, n)
                dve.scalar_tensor_tensor(out=sign[:], in0=w[:], scalar=0.0, in1=negative[:],
                                         op0=ALU.is_gt, op1=ALU.subtract).then_inc(signed, 1)

            dve.wait_ge(w1_loaded, 16)
            split_weight(w1, size1, below1, sign1, 1)
            tokens_low(0, 0)
            tokens_low(1, 1)
            dve.wait_ge(totals, 1)
            dve.tensor_scalar(alpha1[:], a_bank[:, 0:FT], 1.0 / (DIM * SCALE), None, ALU.mult).then_inc(alphas, 1)
            dve.wait_ge(w2_loaded, 16)
            split_weight(w2, size2, below2, sign2, 2)
            dve.wait_ge(totals, 2)
            dve.tensor_scalar(alpha2[:], a_bank[:, 0:DIM], 1.0 / (FF * HSCALE), None, ALU.mult).then_inc(alphas, 1)
            dve.wait_ge(alphas, 2)
            for s in range(4):
                low(0, 0, s)
            all_batches(batch)(dve)

        @block.tensor
        def _(pe):
            def turn(b, par):
                pe.wait_ge(staged[par], 8 * (b - par) + 16)
                if not first(b):
                    pe.wait_ge(x_low, b)
                for g in range(KT_):
                    for t in range(TPB):
                        ins = pe.transpose(x_bank[:, g, t * P:(t + 1) * P], xs[par][:, t, g * P:(g + 1) * P], ident[:])
                ins.then_inc(x_turned, 1)

            def way_up(b, par):
                pe.wait_ge(x_low, b + 1)
                for s in range(4):
                    if not first(b):
                        pe.wait_ge(h_ready, 4 * b + s - 3)
                    for k in range(2):
                        m = 2 * s + k
                        n = 0
                        for x in (xh[par], xl[par]):
                            for g in range(KT_):
                                ins = pe.matmul(u_bank[s][:, k], sign1[:, g, m * P:(m + 1) * P], x[:, g],
                                                start=(n == 0), stop=(n == 2 * KT_ - 1))
                                n += 1
                    ins.then_inc(up, 1)

            def way_down(b, par):
                pe.wait_ge(h_low, 4 * b + 4)
                if not first(b):
                    pe.wait_ge(times_alpha, b * TPB)
                for t in range(TPB):
                    n = 0
                    for x in (hh[par], hl[par]):
                        for m in range(FT):
                            ins = pe.matmul(o_bank[t][:, 0:DIM], x[:, m, t * P:(t + 1) * P], sign2[:, m],
                                            start=(n == 0), stop=(n == 2 * FT - 1))
                            n += 1
                    ins.then_inc(down, 1)

            def batch(b, par, ahead=2):
                if ahead == 2:
                    turn(b + 2, par)
                if ahead:
                    way_up(b + 1, 1 - par)
                way_down(b, par)

            pe.wait_ge(consts, 3)
            turn(0, 0)
            turn(1, 1)
            pe.wait_ge(sized, 1)
            for m in range(FT):
                for g in range(KT_):
                    ins = pe.matmul(a_bank[:, m:m + 1], size1[:, g, m * P:(m + 1) * P], ones[:, 0:1],
                                    start=(g == 0), stop=(g == KT_ - 1))
            ins.then_inc(totals, 1)
            pe.wait_ge(signed, 1)
            way_up(0, 0)
            pe.wait_ge(sized, 2)
            pe.wait_ge(alphas, 1)
            for m in range(FT):
                ins = pe.matmul(a_bank[:, 0:DIM], ones[:], size2[:, m], start=(m == 0), stop=(m == FT - 1))
            ins.then_inc(totals, 1)
            pe.wait_ge(signed, 2)
            all_batches(batch)(pe)


def build(nc, ins, out):
    with ExitStack() as ctx:
        X = ctx.enter_context(nc.sbuf_tensor("tokens", [P, TILES, DIM], F32))
        window_attention(nc, ins["x"], ins["xt"], ins["wqkv"], ins["wo0"], ins["rope"], X)
        cross_attention(nc, "ca0", ins["xw0"], ins["xb0"], ins["xr0"], ins["context"], ins["mask0"], False, X)
        experts(nc, ins["router"], ins["ew1"], ins["ew2"], ins["eb"], X)
        recurrence(nc, ins["w_in"], ins["w_g"], ins["w_out"], ins["hid"], X)
        cross_attention(nc, "ca1", ins["xw1"], ins["xb1"], ins["xr1"], ins["context"], ins["mask1"], True, X)
        binary_ffn(nc, ins["w1t"], ins["w2t"], ins["b1"], ins["b2"], X, out)


def kernel(**inputs):
    import concourse.bacc as bacc
    from concourse.bass_utils import run_bass_kernel_spmd

    a = {k: np.asarray(v) for k, v in inputs.items()}

    def halves(w):
        return np.ascontiguousarray(w.reshape(-1, P, w.shape[-1]).transpose(1, 0, 2))

    def by_partition(v):
        return np.ascontiguousarray(v.reshape(-1, P).T)

    def on_all(v):
        return np.ascontiguousarray(np.broadcast_to(v, (P,) + v.shape))

    pos = np.arange(SEQ, dtype=np.float32)
    freq = np.float32(1.0) / np.float32(10000.0) ** (np.arange(0, HD, 2, dtype=np.float32) / np.float32(HD))
    angle = pos[:, None] * freq[None, :]
    cos, sin = np.cos(angle), np.sin(angle)
    rope = np.stack([np.concatenate([cos, cos], 1), np.concatenate([-sin, sin], 1)], 1).astype(np.float32)
    flat = a["x"].reshape(TOKENS, DIM)
    arrays = {
        "x": np.ascontiguousarray(flat.reshape(TILES, P, DIM).transpose(1, 0, 2)),
        "xt": halves(flat.T),
        "wqkv": halves(np.concatenate([a["L0_attn_Wq"], a["L0_attn_Wk"], a["L0_attn_Wv"]], 1)),
        "wo0": halves(a["L0_attn_Wo"]),
        "rope": np.ascontiguousarray(rope.reshape(TPB, P, 2, HD).transpose(1, 0, 2, 3)),
        "context": halves(a["ctx_1024"].reshape(BATCH * CTX, DIM).T),
        "mask0": np.ascontiguousarray(a["mask_BxSxS2_ik0"].reshape(TILES, P, CTX).transpose(1, 0, 2)),
        "mask1": np.ascontiguousarray(a["mask_Bx1xSxS2_ff0"].reshape(TILES, P, CTX).transpose(1, 0, 2)),
    }
    for n, names in (("0", ["L0_xattn_Wq", "L0_xattn_Wk", "L0_xattn_Wv", "L0_xattn_Wo"]),
                     ("1", ["L1_xattn_w_q", "L1_xattn_w_k", "L1_xattn_w_v", "L1_xattn_w_o"])):
        bq, bk, bv, bo = (a[x.replace("W", "b").replace("w_", "b_")] for x in names)
        arrays["xw" + n] = np.ascontiguousarray(np.stack([halves(a[x].T) for x in names], 1))
        arrays["xb" + n] = np.ascontiguousarray(np.stack([by_partition(bq), by_partition(bk)], 1))
        arrays["xr" + n] = np.ascontiguousarray(np.stack([on_all(bv), on_all(bo)], 1))
    router = a["L0_ffn_router_w"]
    others_first = [*range(1, EXPERTS), 0]
    arrays["router"] = halves(router.T)
    arrays["ew1"] = np.stack([halves(a["L0_ffn_W1"][e]) for e in others_first])
    arrays["ew2"] = np.stack([halves(a["L0_ffn_W2"][e]) for e in others_first])
    arrays["eb"] = np.stack([np.concatenate([by_partition(a["L0_ffn_b1"][e]), by_partition(a["L0_ffn_b2"][e])], 1)
                             for e in others_first], 1)
    for name in ("W_in", "W_g", "W_out"):
        arrays[name.lower()] = halves(a["L1_attn_" + name].T)
    arrays["hid"] = np.stack([*(by_partition(a["L1_attn_conv_w"][:, 0, t]) for t in range(4)), by_partition(a["L1_attn_conv_b"]),
                              *by_partition(a["L1_attn_b_g"]).reshape(P, 2, -1).transpose(1, 0, 2),
                              by_partition(a["L1_attn_forget_base"])], 1)
    arrays["w1t"] = halves(a["L1_ffn_w1"].T)
    arrays["w2t"] = halves(a["L1_ffn_w2"].T)
    arrays["b1"] = by_partition(a["L1_ffn_b1"])
    arrays["b2"] = on_all(a["L1_ffn_b2"])
    nc = bacc.Bacc("TRN2", target_bir_lowering=False, num_devices=1)
    ins = {k: nc.dram_tensor("in_" + k, v.shape, mybir.dt.from_np(v.dtype), kind="ExternalInput").ap()
           for k, v in arrays.items()}
    out = nc.dram_tensor("out", (BATCH, SEQ, DIM), F32, kind="ExternalOutput").ap()
    build(nc, ins, out)
    r = run_bass_kernel_spmd(nc, [{"in_" + k: v for k, v in arrays.items()}], core_ids=[0])
    return r.results[0]["out"]
```

```python
from contextlib import ExitStack

import numpy as np

import concourse.bass as bass
from concourse import mybir

F32 = mybir.dt.float32
F16 = mybir.dt.float16
BF16 = mybir.dt.bfloat16
I32 = mybir.dt.int32
ALU = mybir.AluOpType
ACT = mybir.ActivationFunctionType
AX = mybir.AxisListType

P = 128
BATCH, SEQ, DIM = 8, 256, 256
TOKENS = BATCH * SEQ
TILES = TOKENS // P
TPB = SEQ // P
KT_ = DIM // P
EPS = 1e-5
NEG = -1.0e30
SCALE = 1024.0
UNSCALE = 1.0 / (SCALE * SCALE)


class Ring:

    def __init__(self, steps, first, last, ahead):
        self.steps, self.first, self.last, self.ahead = steps, first, last, ahead
        self.per = sum(map(len, steps))
        assert self.per % 2 == 0

    def number(self, n, b=0):
        return n % 2, n // 2 + b * (self.per // 2)

    def slot(self, slot, b):
        static = isinstance(b, int)
        if static and b == 0:
            n, turns = len(self.first), 0
        else:
            n, turns = len(self.first) - len(self.last), b
        out = []
        for s, steps in enumerate(self.steps):
            for kind, i in steps:
                if static and (b == 0 and (kind, i) in self.last or b == BATCH - 1 and kind in self.ahead):
                    continue
                if s == slot:
                    out.append((kind, i, *self.number(n, turns)))
                n += 1
        return out

    def prologue(self):
        return [(kind, i, *self.number(n)) for n, (kind, i) in enumerate(self.first)]

    def epilogue(self):
        n = len(self.first) - len(self.last) + self.per * (BATCH - 1)
        n += sum(kind not in self.ahead for steps in self.steps for kind, _ in steps)
        return [(kind, i, *self.number(n + k)) for k, (kind, i) in enumerate(self.last)]

    def place(self, kind, i, b):
        body = b - 1 if kind in self.ahead else b + 1 if (kind, i) in self.last else b
        if first(b) and kind in self.ahead:
            found = self.prologue()
        elif isinstance(b, int) and body == BATCH:
            found = self.epilogue()
        else:
            found = [x for slot in range(len(self.steps)) for x in self.slot(slot, body)]
        return next((bank, uses) for k, j, bank, uses in found if (k, j) == (kind, i))

    def serves(self, kind, i):
        return 1 if kind in self.ahead else -1 if (kind, i) in self.last else 0

    def wait_read(self, engine, free, steps, b):
        last = {}
        for kind, i in steps:
            bank, uses = self.place(kind, i, b)
            last[bank] = uses
        for bank, uses in last.items():
            engine.wait_ge(free[bank], uses + 1)


def at(ap, index):
    return ap[:, index] if isinstance(index, int) else ap[:, bass.ds(index, 1)].squeeze(1)


def identity(pool, tile, made, done):
    pool.memset(tile[:], 0.0).then_inc(made, 1)
    pool.wait_ge(made, done)
    return pool.affine_select(out=tile[:], in_=tile[:], compare_op=ALU.not_equal, fill=1.0, base=0,
                              pattern=[[-1, P]], channel_multiplier=1)

class Norm:

    def __init__(self, ctx, nc, tag, half):
        def sb(name, shape):
            return ctx.enter_context(nc.sbuf_tensor(f"{tag}_{name}", shape, F32))

        def sem(name):
            return ctx.enter_context(nc.semaphore(f"{tag}_{name}"))

        self.res = sb("res", [P, TPB, DIM])
        self.stats = sb("stats", [P, TPB, 6])
        self.mv = sb("mv", [P, TPB, 2])
        self.var_eps = sb("var_eps", [P, TPB, 1])
        self.rstd = sb("rstd", [P, TPB, 1])
        self.half = half
        self.stat = sem("stat")
        self.mean_var = sem("mean_var")
        self.var_ready = sem("var_ready")
        self.rstd_ready = sem("rstd_ready")
        self.ln_done = sem("ln_done")

    def statistics(self, dve, b, t):
        dve.bn_stats(self.stats[:, t], self.res[:, t]).then_inc(self.stat, 1)
        dve.wait_ge(self.stat, b * TPB + t + 1)
        dve.memset(self.var_eps[:, t], 0.0)
        dve.bn_aggr(self.mv[:, t], self.stats[:, t]).then_inc(self.mean_var, 1)
        dve.wait_ge(self.mean_var, b * TPB + t + 1)
        dve.tensor_scalar(self.var_eps[:, t], self.mv[:, t, 1:2], EPS, None, ALU.add).then_inc(self.var_ready, 1)

    def root(self, pool, b, t):
        pool.wait_ge(self.var_ready, b * TPB + t + 1)
        pool.tensor_tensor(self.rstd[:, t], self.var_eps[:, t], self.half[:], ALU.pow).then_inc(self.rstd_ready, 1)

    def apply(self, dve, b, t, out):
        dve.wait_ge(self.rstd_ready, b * TPB + t + 1)
        dve.tensor_scalar(out, self.res[:, t], self.mv[:, t, 0:1], self.rstd[:, t],
                          ALU.subtract, ALU.mult).then_inc(self.ln_done, 1)


def first(b):
    return isinstance(b, int) and b == 0


HEADS, HD = 16, 64
WINDOW = SEQ // 4
SPAN = P + WINDOW
QKV = 3 * HEADS * HD
PSCALE = 4096.0
WA = Ring(
    steps=[
        [("project", 0), ("project", 1), ("project", 2)],
        [("project", 3), ("project", 4), ("project", 5)],
        [("heads", 3), ("project", 6), ("turn", 0), ("turn", 1)],
        [("project", 7), ("mix", 0), ("mix", 1), ("turn", 2), ("turn", 3), ("heads", 0)],
        [("project", 8), ("project", 9), ("project", 10)],
        [("project", 11), ("turn", 4), ("turn", 5), ("heads", 1)],
        [("turn", 6), ("turn", 7)],
        [("heads", 2)],
    ],
    first=([("project", n) for n in range(6)] + [("turn", 0), ("turn", 1), ("project", 6), ("turn", 2), ("turn", 3)]
           + [("project", n) for n in range(7, 12)] + [("turn", n) for n in range(4, 8)]),
    last=[("heads", 3), ("mix", 0), ("mix", 1)],
    ahead={"project", "turn"},
)
ROPE_SIN = {0: 0, 1: 1, 3: 2, 4: 3}
ROPE_ADD = {1: 0, 2: 1, 4: 2, 5: 3}


def windows(ap):
    return bass.AP(tensor=ap.tensor, offset=ap.offset, ap=[list(ap.ap[0]), [SEQ + WINDOW, 2], [1, SPAN]])


def window_attention(nc, x_dram, xt_dram, wqkv_dram, wo_dram, rope_dram, ident, half, X, next_loads):
    with ExitStack() as ctx:
        def sb(name, shape, dt=F32):
            return ctx.enter_context(nc.sbuf_tensor("wa_" + name, shape, dt))

        def sem(name):
            sems.append(nc.alloc_semaphore("wa_" + name))
            return sems[-1]

        sems = []

        w_stage = sb("w_stage", [P, 2, KT_, 512])
        wh = sb("wh", [P, KT_, QKV], F16)
        wl = sb("wl", [P, KT_, QKV], F16)
        wo = sb("wo", [P, HEADS * HD // P, DIM])
        cos_sin = sb("cos_sin", [P, TPB, 2, HD])
        x_stage = sb("x_stage", [P, 2, KT_, SEQ])
        xh = sb("xh", [P, 2, KT_, SEQ], F16)
        xl = sb("xl", [P, 2, KT_, SEQ], F16)
        raw = sb("raw", [P, 2, HEADS, HD])
        rot = sb("rot", [P, 2, HEADS, HD])
        sine = sb("sine", [P, HEADS, HD])
        qt = [sb(f"qt{k}", [P, HEADS, SEQ]) for k in range(2)]
        kt = [sb(f"kt{k}", [P, HEADS // 2, SEQ]) for k in range(2)]
        vh = [sb(f"vh{k}", [P, TPB, HEADS, HD + 1], F16) for k in range(2)]
        vl = [sb(f"vl{k}", [P, TPB, HEADS, HD + 1], F16) for k in range(2)]
        shifted = [sb(f"shifted{k}", [P, 2, SPAN]) for k in range(4)]
        probs = [sb(f"probs{k}", [P, 2, SEQ]) for k in range(4)]
        top = sb("top", [P, 4, 2])
        pth = [sb(f"pth{k}", [P, 2 * SEQ], F16) for k in range(4)]
        ptl = [sb(f"ptl{k}", [P, 2 * SEQ], F16) for k in range(4)]
        inv = sb("inv", [P, 2, TPB, 2])
        heads_out = sb("heads_out", [P, TPB, HEADS, HD])
        heads_t = sb("heads_t", [P, HEADS // 2, SEQ])
        ident_bf = sb("ident_bf", [P, P], BF16)
        band = sb("band", [P, TPB, SPAN], BF16)

        shared = [ctx.enter_context(nc.psum_tensor(f"wa_shared{k}", [P, 512], F32)) for k in range(2)]
        s_bank = [ctx.enter_context(nc.psum_tensor(f"wa_scores{k}", [P, 2, SEQ], F32)) for k in range(2)]
        t_bank = [ctx.enter_context(nc.psum_tensor(f"wa_turned{k}", [P, 512], F32)) for k in range(2)]
        o_bank = [ctx.enter_context(nc.psum_tensor(f"wa_out{k}", [P, TPB, 2, P], F32)) for k in range(2)]

        norm = Norm(ctx, nc, "wa", half)
        w_loaded = [sem("w_loaded0"), sem("w_loaded1")]
        w_high = sem("w_high")
        w_low = sem("w_low")
        x_loaded = [sem("x_loaded0"), sem("x_loaded1")]
        x_high = sem("x_high")
        x_low = sem("x_low")
        tokens_loaded = sem("tokens_loaded")
        wo_loaded = sem("wo_loaded")
        rope_loaded = sem("rope_loaded")
        consts = sem("consts")
        qt_zeroed = sem("qt_zeroed")
        zeroed = sem("zeroed")
        full = [sem("full0"), sem("full1")]
        free = [sem("free0"), sem("free1")]
        cos_done = sem("cos_done")
        sin_done = sem("sin_done")
        rope_done = sem("rope_done")
        v_high = sem("v_high")
        scores = sem("scores")
        maxed = sem("maxed")
        shift = sem("shift")
        exped = sem("exped")
        probs_t = sem("probs_t")
        probs_high = sem("probs_high")
        probs_low = sem("probs_low")
        weighted = sem("weighted")
        inverted = sem("inverted")
        normed = sem("normed")

        def wait_read(engine, steps, b):
            WA.wait_read(engine, free, steps, b)

        def wait_raw(engine, b, r):
            wait_read(engine, [("project", 6 * (r // 2) + 2 * (r % 2) + c) for c in range(2)], b)

        def wait_rot_used(engine, b, r):
            bank, uses = WA.place("turn", 2 * (r - 2) + 1, b) if r >= 2 else WA.place("turn", 2 * (r + 2) + 1, b - 1)
            engine.wait_ge(full[bank], uses + 1)

        block_scope = ExitStack()
        block = block_scope.enter_context(nc.Block())

        @block.sync
        def _(sp):
            def load_x(b, par):
                sp.dma_start(x_stage[:, par], xt_dram[:, :, bass.ds(b * SEQ, SEQ)]).then_inc(x_loaded[par], 16)

            load_x(0, 0)
            for c in range(6):
                if c >= 2:
                    sp.wait_ge(w_low, c - 1)
                sp.dma_start(w_stage[:, c % 2], wqkv_dram[:, :, c * 512:(c + 1) * 512]).then_inc(w_loaded[c % 2], 16)
                if c == 1:
                    load_x(1, 1)
                    sp.dma_start(cos_sin[:], rope_dram).then_inc(rope_loaded, 16)
            sp.dma_start(wo[:], wo_dram).then_inc(wo_loaded, 16)
            sp.dma_start(X[:], x_dram).then_inc(tokens_loaded, 16)
            with sp.Fori(0, BATCH // 2 - 1) as i:
                sp.wait_ge(x_low, 2 * i + 1)
                load_x(2 * i + 2, 0)
                sp.wait_ge(x_low, 2 * i + 2)
                load_x(2 * i + 3, 1)
            next_loads(sp)

        @block.gpsimd
        def _(pool):
            identity(pool, ident, consts, 1).then_inc(consts, 1)
            identity(pool, ident_bf, consts, 3).then_inc(consts, 1)
            pool.memset(half[:], -0.5).then_inc(consts, 1)
            pool.memset(band[:], 0.0).then_inc(consts, 1)
            pool.wait_ge(consts, 6)
            for t, base in ((0, 0), (1, P - WINDOW)):
                n = 6 + 2 * t
                pool.affine_select(out=band[:, t], in_=band[:, t], compare_op=ALU.is_ge, fill=NEG,
                                   base=base + WINDOW, pattern=[[-1, SPAN]], channel_multiplier=1).then_inc(consts, 1)
                pool.wait_ge(consts, n + 1)
                pool.affine_select(out=band[:, t], in_=band[:, t], compare_op=ALU.is_ge, fill=NEG,
                                   base=WINDOW - base, pattern=[[1, SPAN]], channel_multiplier=-1).then_inc(consts, 1)

            pool.wait_ge(consts, 10)
            for k in range(2):
                pool.memset(qt[k][0:HD, 1:HEADS:2], 0.0).then_inc(qt_zeroed, 1)
                pool.wait_ge(qt_zeroed, 2 * k + 1)
                pool.memset(qt[k][HD:P, 0:HEADS:2], 0.0).then_inc(qt_zeroed, 1)
                pool.wait_ge(qt_zeroed, 2 * k + 2)

            def cosine(b, r):
                wait_raw(pool, b, r)
                if r == 0 and isinstance(b, int) and b == 0:
                    pool.wait_ge(rope_loaded, 16)
                if not (first(b) and r < 2):
                    wait_rot_used(pool, b, r)
                c = cos_sin[:, r // 2, 0].unsqueeze(1).broadcast_to((P, HEADS, HD))
                pool.tensor_tensor(rot[:, r % 2], raw[:, r % 2], c, ALU.mult).then_inc(cos_done, 1)

            def batch(b, before=True, after=True):
                for slot in range(8):
                    if after and slot in ROPE_SIN:
                        cosine(b + 1, ROPE_SIN[slot])
                    if before and slot == 3:
                        norm.root(pool, b - 1, 0)
                        norm.root(pool, b - 1, 1)

            for r in range(4):
                cosine(0, r)
            batch(0, before=False)
            with pool.Fori(0, BATCH // 2 - 1) as i:
                batch(2 * i + 1)
                batch(2 * i + 2)
            batch(BATCH - 1, after=False)
            norm.root(pool, BATCH - 1, 0)
            norm.root(pool, BATCH - 1, 1)

        @block.scalar
        def _(act):
            def split_w(c):
                act.wait_ge(w_loaded[c % 2], 16 * (c // 2 + 1))
                act.activation(wh[:, :, c * 512:(c + 1) * 512], w_stage[:, c % 2], ACT.Copy, scale=SCALE).then_inc(w_high, 1)

            def split_x(b, par):
                act.wait_ge(x_loaded[par], 8 * (b - par) + 16)
                act.activation(xh[:, par], x_stage[:, par], ACT.Copy, scale=SCALE).then_inc(x_high, 1)

            def step(b, par, kind, i, bank, uses):
                src = shared[bank]
                if kind == "mix":
                    return
                act.wait_ge(full[bank], uses + 1)
                if kind == "project":
                    t, c = divmod(i, 6)
                    if c < 4:
                        unit = 2 * t + c // 2
                        if not (first(b) and unit < 2):
                            act.wait_ge(sin_done, b * 4 + unit - 1)
                            act.wait_ge(cos_done, b * 4 + unit - 1)
                        dst = raw[:, unit % 2, (c % 2) * 8:(c % 2) * 8 + 8]
                        act.activation(dst, src[:].rearrange("p (h d) -> p h d", h=8), ACT.Copy,
                                       scale=UNSCALE).then_inc(free[bank], 1)
                    else:
                        h0 = (c - 4) * 8
                        act.activation(vh[par][:, t, h0:h0 + 8, 0:HD], src[:].rearrange("p (h d) -> p h d", h=8),
                                       ACT.Copy, scale=1.0 / SCALE).then_inc(v_high, 1)
                elif kind == "turn":
                    t, c = divmod(i, 4)
                    cols = slice(t * P, (t + 1) * P)
                    s = src[:].rearrange("p (h q) -> p h q", h=4)
                    if c < 2:
                        act.activation(qt[par][0:HD, 8 * c:8 * c + 8:2, cols], s[0:HD], ACT.Copy)
                        act.activation(qt[par][HD:P, 8 * c + 1:8 * c + 8:2, cols], s[HD:P],
                                       ACT.Copy).then_inc(free[bank], 1)
                    else:
                        act.activation(kt[par][:, 4 * (c - 2):4 * (c - 2) + 4, cols], s,
                                       ACT.Copy).then_inc(free[bank], 1)
                elif kind == "heads":
                    act.activation(heads_t[:, 2 * i:2 * i + 2], src[:].rearrange("p (h q) -> p h q", h=2),
                                   ACT.Copy).then_inc(free[bank], 1)

            def batch(b, par, before=True, after=True):
                for slot in range(8):
                    if after and slot == 0:
                        split_x(b + 1, 1 - par)
                    for t in range(TPB):
                        n = 2 * slot + t
                        k = 2 * (slot % 2) + t
                        act.wait_ge(shift, b * 16 + n + 1)
                        if not (first(b) and slot < 2):
                            act.wait_ge(probs_t, b * 16 + 2 * slot - 2)
                        act.activation(probs[k][:, :, t * WINDOW:t * WINDOW + SPAN], shifted[k][:], ACT.Exp,
                                       scale=HD ** -0.5).then_inc(exped, 1)
                    for kind, i, bank, uses in WA.slot(slot, b):
                        d = WA.serves(kind, i)
                        step(b + d, (par + d) % 2, kind, i, bank, uses)
                    for h in range(2):
                        k = 2 * (slot % 2) + h
                        act.wait_ge(probs_t, b * 16 + 2 * slot + h + 1)
                        if not (first(b) and slot < 2):
                            act.wait_ge(weighted, b * 8 + slot - 1)
                        act.activation(windows(pth[k][:]), windows(t_bank[h][:]), ACT.Copy, scale=PSCALE).then_inc(probs_high, 1)

            split_x(0, 0)
            for c in range(6):
                split_w(c)
            for kind, i, bank, uses in WA.prologue():
                if (kind, i) == ("turn", 0):
                    act.wait_ge(zeroed, 1)
                    act.wait_ge(qt_zeroed, 4)
                step(0, 0, kind, i, bank, uses)
            batch(0, 0, before=False)
            with act.Fori(0, BATCH // 2 - 1) as i:
                batch(2 * i + 1, 1)
                batch(2 * i + 2, 0)
            batch(BATCH - 1, 1, after=False)
            for kind, i, bank, uses in WA.epilogue():
                step(BATCH - 1, 1, kind, i, bank, uses)

        @block.vector
        def _(dve):
            def split_w(c):
                cols = slice(c * 512, (c + 1) * 512)
                dve.wait_ge(w_high, c + 1)
                dve.scalar_tensor_tensor(out=wl[:, :, cols], in0=w_stage[:, c % 2], scalar=SCALE,
                                         in1=wh[:, :, cols], op0=ALU.mult, op1=ALU.subtract).then_inc(w_low, 1)

            def split_x(b, par):
                dve.wait_ge(x_high, b + 1)
                dve.scalar_tensor_tensor(out=xl[:, par], in0=x_stage[:, par], scalar=SCALE,
                                         in1=xh[:, par], op0=ALU.mult, op1=ALU.subtract).then_inc(x_low, 1)

            def sin_part(b, r):
                wait_raw(dve, b, r)
                if not (first(b) and r == 0):
                    dve.wait_ge(rope_done, b * 4 + r)
                for a, z in ((0, HD // 2), (HD // 2, 0)):
                    s = cos_sin[:, r // 2, 1, a:a + HD // 2].unsqueeze(1).broadcast_to((P, HEADS, HD // 2))
                    ins = dve.tensor_tensor(sine[:, :, a:a + HD // 2], raw[:, r % 2, :, z:z + HD // 2], s, ALU.mult)
                ins.then_inc(sin_done, 1)

            def add_part(b, r):
                dve.wait_ge(sin_done, b * 4 + r + 1)
                dve.wait_ge(cos_done, b * 4 + r + 1)
                dve.tensor_tensor(rot[:, r % 2], rot[:, r % 2], sine[:], ALU.add).then_inc(rope_done, 1)

            def value_low(b, par, i, bank):
                t, c = divmod(i, 6)
                h0 = (c - 4) * 8
                dve.wait_ge(v_high, b * 4 + 2 * t + c - 3)
                dve.scalar_tensor_tensor(out=vl[par][:, t, h0:h0 + 8, 0:HD],
                                         in0=shared[bank][:].rearrange("p (h d) -> p h d", h=8), scalar=1.0 / SCALE,
                                         in1=vh[par][:, t, h0:h0 + 8, 0:HD], op0=ALU.mult,
                                         op1=ALU.subtract).then_inc(free[bank], 1)

            def residual(b, t, bank, uses):
                dve.wait_ge(full[bank], uses + 1)
                dve.tensor_tensor(norm.res[:, t], shared[bank][:, 0:DIM], at(X, b * TPB + t), ALU.add).then_inc(free[bank], 1)
                dve.wait_ge(free[bank], uses + 1)
                norm.statistics(dve, b, t)

            def layer_norm(b, t):
                norm.apply(dve, b, t, at(X, b * TPB + t))

            def shift_scores(b, u, par):
                for t in range(TPB):
                    n = 2 * u + t
                    k = 2 * (u % 2) + t
                    dve.wait_ge(scores, b * 16 + n + 1)
                    if not (first(b) and u < 2):
                        dve.wait_ge(exped, b * 16 + n - 3)
                    dve.tensor_reduce(top[:, k], s_bank[t][:, :, 0:SPAN], AX.X, ALU.max).then_inc(maxed, 1)
                    dve.wait_ge(maxed, b * 16 + n + 1)
                    dve.tensor_tensor(shifted[k][:], s_bank[t][:, :, 0:SPAN],
                                      top[:, k].unsqueeze(2).broadcast_to((P, 2, SPAN)), ALU.subtract).then_inc(shift, 1)

            def normalise(b, u):
                dve.wait_ge(weighted, b * 8 + u + 1)
                bank = o_bank[u % 2]
                if not (first(b) and u < 2):
                    dve.wait_ge(normed, b * 8 + u - 1)
                dve.reciprocal(inv[:, u % 2], bank[:, :, :, HD:HD + 1].squeeze(3)).then_inc(inverted, 1)
                dve.wait_ge(inverted, b * 8 + u + 1)
                if not first(b):
                    before, uses = WA.place("heads", u // 2, b - 1)
                    dve.wait_ge(full[before], uses + 1)
                dve.tensor_tensor(heads_out[:, :, 2 * u:2 * u + 2], bank[:, :, :, 0:HD],
                                  inv[:, u % 2].unsqueeze(3).broadcast_to((P, TPB, 2, HD)), ALU.mult).then_inc(normed, 1)

            def probs_rest(b, u):
                for h in range(2):
                    k = 2 * (u % 2) + h
                    dve.wait_ge(probs_high, b * 16 + 2 * u + h + 1)
                    dve.scalar_tensor_tensor(out=windows(ptl[k][:]), in0=windows(t_bank[h][:]), scalar=PSCALE,
                                             in1=windows(pth[k][:]), op0=ALU.mult, op1=ALU.subtract).then_inc(probs_low, 1)

            def batch(b, par, before=True, after=True):
                for slot in range(8):
                    if after and slot == 0:
                        split_x(b + 1, 1 - par)
                    if slot < 7:
                        shift_scores(b, slot + 1, par)
                    elif after:
                        shift_scores(b + 1, 0, 1 - par)
                    for kind, i, bank, uses in WA.slot(slot, b):
                        if kind == "project" and i % 6 > 3:
                            value_low(b + 1, 1 - par, i, bank)
                        if kind == "mix":
                            residual(b - 1, i, bank, uses)
                    if after and slot in ROPE_ADD:
                        add_part(b + 1, ROPE_ADD[slot])
                    if after and slot in ROPE_SIN:
                        sin_part(b + 1, ROPE_SIN[slot])
                    if before and slot == 4:
                        layer_norm(b - 1, 0)
                        layer_norm(b - 1, 1)
                    probs_rest(b, slot)
                    if slot > 0:
                        normalise(b, slot - 1)
                    elif before:
                        normalise(b - 1, 7)

            split_x(0, 0)
            for c in range(6):
                split_w(c)
                if c < 2:
                    dve.memset(vh[c][:, :, :, HD:HD + 1], SCALE)
                    dve.memset(vl[c][:, :, :, HD:HD + 1], 0.0)
                else:
                    dve.memset(probs[c - 2][:], 0.0)
                    dve.memset(pth[c - 2][:], 0.0)
                    ins = dve.memset(ptl[c - 2][:], 0.0)
            ins.then_inc(zeroed, 1)
            dve.wait_ge(rope_loaded, 16)
            for kind, i, bank, uses in WA.prologue():
                if kind == "project" and i % 6 > 3:
                    value_low(0, 0, i, bank)
                if kind == "project" and i % 6 in (1, 3):
                    r = 2 * (i // 6) + (i % 6) // 2
                    sin_part(0, r)
                    add_part(0, r)
            shift_scores(0, 0, 0)
            dve.wait_ge(tokens_loaded, 16)
            batch(0, 0, before=False)
            with dve.Fori(0, BATCH // 2 - 1) as i:
                batch(2 * i + 1, 1)
                batch(2 * i + 2, 0)
            batch(BATCH - 1, 1, after=False)
            normalise(BATCH - 1, 7)
            for kind, i, bank, uses in WA.epilogue():
                if kind == "mix":
                    residual(BATCH - 1, i, bank, uses)
            layer_norm(BATCH - 1, 0)
            layer_norm(BATCH - 1, 1)

        @block.tensor
        def _(pe):
            def step(b, par, kind, i, bank, uses):
                dst = shared[bank]
                if not (isinstance(uses, int) and uses == 0):
                    pe.wait_ge(free[bank], uses)
                if kind == "project":
                    t, c = divmod(i, 6)
                    if i == 0:
                        pe.wait_ge(x_low, b + 1)
                    if first(b):
                        pe.wait_ge(w_low, c + 1)
                    tok = slice(t * P, (t + 1) * P)
                    cols = slice(c * 512, (c + 1) * 512)
                    for k in range(KT_):
                        for n, (a, w) in enumerate(((xh, wh), (xh, wl), (xl, wh))):
                            ins = pe.matmul(dst[:], a[:, par, k, tok], w[:, k, cols],
                                            start=(k == 0 and n == 0), stop=(k == KT_ - 1 and n == 2))
                elif kind == "turn":
                    t, c = divmod(i, 4)
                    unit = 2 * t + c // 2
                    pe.wait_ge(rope_done, b * 4 + unit + 1)
                    for j in range(4):
                        h = 8 * (c % 2) + 2 * j
                        ins = pe.transpose(dst[:, j * P:(j + 1) * P],
                                           rot[:, unit % 2, h:h + 2].rearrange("p h d -> p (h d)"), ident[:])
                elif kind == "heads":
                    pe.wait_ge(normed, b * 8 + 2 * i + 2)
                    for j in range(2):
                        for t in range(TPB):
                            pair = 2 * i + j
                            ins = pe.transpose(dst[:, (2 * j + t) * P:(2 * j + t + 1) * P],
                                               heads_out[:, t, 2 * pair:2 * pair + 2].rearrange("p h d -> p (h d)"), ident[:])
                else:
                    wait_read(pe, [("heads", j) for j in range(4)], b)
                    for j in range(HEADS // 2):
                        ins = pe.matmul(dst[:, 0:DIM], heads_t[:, j, i * P:(i + 1) * P], wo[:, j],
                                        start=(j == 0), stop=(j == HEADS // 2 - 1))
                ins.then_inc(full[bank], 1)

            def score(b, u, par):
                if u == 0:
                    wait_read(pe, [("turn", i) for i in range(4, 8)], b)
                for t in range(TPB):
                    if not (first(b) and u == 0):
                        pe.wait_ge(shift, b * 16 + 2 * u + t - 1)
                    for h in range(2):
                        dst = s_bank[t][:, h, 0:SPAN]
                        pe.matmul(dst, ident_bf[:], band[:, t], start=True, stop=False)
                        ins = pe.matmul(dst, qt[par][:, 2 * u + h, t * P:(t + 1) * P],
                                        kt[par][:, u, t * WINDOW:t * WINDOW + SPAN], start=False, stop=True)
                    ins.then_inc(scores, 1)

            def turn_probs(b, u):
                pe.wait_ge(exped, b * 16 + 2 * u + 2)
                for h in range(2):
                    if not (first(b) and u == 0):
                        pe.wait_ge(probs_low, b * 16 + 2 * u + h - 1)
                    for j in range(2):
                        for t in range(TPB):
                            ins = pe.transpose(t_bank[h][:, j * SEQ + t * P:j * SEQ + (t + 1) * P],
                                               probs[2 * (u % 2) + t][:, h, j * P:(j + 1) * P], ident[:])
                    ins.then_inc(probs_t, 1)

            def weigh(b, u, par):
                pe.wait_ge(probs_low, b * 16 + 2 * u + 2)
                if u == 0:
                    wait_read(pe, [("project", 10), ("project", 11)], b)
                if not (first(b) and u < 2):
                    pe.wait_ge(normed, b * 8 + u - 1)
                for t in range(TPB):
                    for h in range(2):
                        k = 2 * (u % 2) + h
                        n = 0
                        for j in range(2):
                            q = slice(j * SEQ + t * P, j * SEQ + (t + 1) * P)
                            for a, v in ((pth[k], vh[par]), (pth[k], vl[par]), (ptl[k], vh[par])):
                                ins = pe.matmul(o_bank[u % 2][:, t, h, 0:HD + 1], a[:, q], v[:, j, 2 * u + h],
                                                start=(n == 0), stop=(n == 5))
                                n += 1
                ins.then_inc(weighted, 1)

            def batch(b, par, before=True, after=True):
                for slot in range(8):
                    if slot < 7:
                        score(b, slot + 1, par)
                    elif after:
                        score(b + 1, 0, 1 - par)
                    for kind, i, bank, uses in WA.slot(slot, b):
                        d = WA.serves(kind, i)
                        step(b + d, (par + d) % 2, kind, i, bank, uses)
                    turn_probs(b, slot)
                    if slot > 0:
                        weigh(b, slot - 1, par)
                    elif before:
                        weigh(b - 1, 7, 1 - par)

            pe.wait_ge(consts, 10)
            for kind, i, bank, uses in WA.prologue():
                step(0, 0, kind, i, bank, uses)
            score(0, 0, 0)
            pe.wait_ge(wo_loaded, 16)
            batch(0, 0, before=False)
            with pe.Fori(0, BATCH // 2 - 1) as i:
                batch(2 * i + 1, 1)
                batch(2 * i + 2, 0)
            batch(BATCH - 1, 1, after=False)
            weigh(BATCH - 1, 7, 1)
            for kind, i, bank, uses in WA.epilogue():
                step(BATCH - 1, 1, kind, i, bank, uses)

        block_scope.close()
        nc.clear_and_free_semaphores(sems)
        nc.all_engine_barrier()


CTX = 77
CH, CD = 16, 16
UH = 4
UNITS = TPB * CH // UH
MASKED = -4.0e9
OPEN = 1.0e38
CA = Ring(
    steps=[
        [("key", 0)],
        [("value", 0)],
        [("heads", 1)],
        [("mix", 1)],
        [("tokens", 0)],
        [("query", 0)],
        [("heads", 0)],
        [("mix", 0)],
    ],
    first=[("key", 0), ("value", 0), ("tokens", 0), ("query", 0)],
    last=[("heads", 1), ("mix", 1)],
    ahead={"key", "value", "tokens", "query"},
)


class CrossWeights:

    def __init__(self, ctx, nc, tag, additive):
        self.tag, self.additive = tag, additive

        def sb(name, shape, dt=F32):
            return ctx.enter_context(nc.sbuf_tensor(f"{tag}_{name}", shape, dt))

        self.w = sb("w", [P, 4, KT_, DIM])
        self.bias = sb("bias", [P, 2, KT_])
        self.rows = sb("rows", [P, 2, DIM])
        self.mask = sb("mask", [P, TILES, CTX], F32 if additive else I32)
        self.loaded = ctx.enter_context(nc.semaphore(f"{tag}_loaded"))

    def load(self, sp, w_dram, b_dram, rows_dram, mask_dram):
        for tile, dram in ((self.bias, b_dram), (self.rows, rows_dram), (self.w, w_dram), (self.mask, mask_dram)):
            sp.dma_start(tile[:], dram).then_inc(self.loaded, 16)


def cross_attention(nc, weights, ctx_dram, ident, half, X, next_loads=None):
    tag, additive = weights.tag, weights.additive
    w, bias, rows, mask = weights.w, weights.bias, weights.rows, weights.mask
    with ExitStack() as ctx:
        def sb(name, shape, dt=F32):
            return ctx.enter_context(nc.sbuf_tensor(f"{tag}_{name}", shape, dt))

        def sem(name):
            sems.append(nc.alloc_semaphore(f"{tag}_{name}"))
            return sems[-1]

        sems = []

        context = [sb(f"context{k}", [P, KT_, CTX]) for k in range(2)]
        xs = [sb(f"xs{k}", [P, TPB, DIM]) for k in range(2)]
        limit = None if additive else sb("limit", [P, TILES, CTX])
        head_of = sb("head_of", [P, CH // KT_])
        xt = [sb(f"xt{k}", [P, KT_, SEQ]) for k in range(2)]
        q = [sb(f"q{k}", [P, KT_, SEQ]) for k in range(2)]
        kb = sb("kb", [P, KT_, CTX])
        km = [sb(f"km{k}", [P, KT_, CH // KT_, CTX]) for k in range(2)]
        v = sb("v", [P, CH, CD])
        vh = [sb(f"vh{k}", [P, CH, CD + 1], F16) for k in range(2)]
        vl = [sb(f"vl{k}", [P, CH, CD + 1], F16) for k in range(2)]
        z = [sb(f"z{k}", [P, UH, CTX]) for k in range(2)]
        top = sb("top", [P, 2, UH])
        probs = [sb(f"probs{k}", [P, UH, CTX]) for k in range(2)]
        pth = [sb(f"pth{k}", [P, UH * P], F16) for k in range(2)]
        ptl = [sb(f"ptl{k}", [P, UH * P], F16) for k in range(2)]
        inv = sb("inv", [P, TPB, CH])
        o = sb("o", [P, TPB, CH, CD])
        ot = sb("ot", [P, TPB, KT_, P])
        xb = sb("xb", [P, TPB, DIM])

        shared = [ctx.enter_context(nc.psum_tensor(f"{tag}_shared{k}", [P, 512], F32)) for k in range(2)]
        s_bank = [ctx.enter_context(nc.psum_tensor(f"{tag}_scores{k}", [P, 512], F32)) for k in range(2)]
        t_bank = [ctx.enter_context(nc.psum_tensor(f"{tag}_turned{k}", [P, 512], F32)) for k in range(2)]
        o_bank = [ctx.enter_context(nc.psum_tensor(f"{tag}_out{k}", [P, CH, 32], F32)) for k in range(2)]

        norm = Norm(ctx, nc, tag, half)
        context_loaded = [sem("context_loaded0"), sem("context_loaded1")]
        staged = [sem("staged0"), sem("staged1")]
        consts = sem("consts")
        limits = sem("limits")
        ones = sem("ones")
        full = [sem("full0"), sem("full1")]
        free = [sem("free0"), sem("free1")]
        key_masked = sem("key_masked")
        v_high = sem("v_high")
        v_low = sem("v_low")
        token_sum = sem("token_sum")
        scores = sem("scores")
        masked = sem("masked")
        maxed = sem("maxed")
        shift = sem("shift")
        exped = sem("exped")
        probs_t = sem("probs_t")
        probs_high = sem("probs_high")
        probs_low = sem("probs_low")
        weighted = sem("weighted")
        inverted = sem("inverted")
        normed = sem("normed")

        def wait_read(engine, steps, b):
            CA.wait_read(engine, free, steps, b)

        def wait_full(engine, kind, i, b):
            bank, uses = CA.place(kind, i, b)
            engine.wait_ge(full[bank], uses + 1)

        def both(batch):
            def run(engine):
                batch(0, 0, before=False)
                with engine.Fori(0, BATCH // 2 - 1) as i:
                    batch(2 * i + 1, 1)
                    batch(2 * i + 2, 0)
                batch(BATCH - 1, 1, after=False)
            return run

        block_scope = ExitStack()
        block = block_scope.enter_context(nc.Block())

        @block.sync
        def _(sp):
            def load_context(b, par):
                sp.dma_start(context[par][:], ctx_dram[:, :, bass.ds(b * CTX, CTX)]).then_inc(context_loaded[par], 16)

            def stage(b, par):
                sp.dma_start(xs[par][:], X[:, bass.ds(b * TPB, TPB)]).then_inc(staged[par], 16)

            for b in (0, 1):
                load_context(b, b)
                stage(b, b)
            if next_loads:
                next_loads(sp)

            def replace(b, par):
                wait_full(sp, "value", 0, b)
                load_context(b + 2, par)
                wait_full(sp, "tokens", 0, b)
                sp.wait_ge(token_sum, (b + 1) * TPB)
                stage(b + 2, par)

            replace(0, 0)
            replace(1, 1)
            with sp.Fori(1, BATCH // 2 - 1) as i:
                replace(2 * i, 0)
                replace(2 * i + 1, 1)

        @block.gpsimd
        def _(pool):
            pool.memset(head_of[:], 1.0).then_inc(consts, 1)
            pool.wait_ge(consts, 1)
            pool.affine_select(out=head_of[:], in_=head_of[:], compare_op=ALU.is_ge, fill=0.0, base=0,
                               pattern=[[-CD, CH // KT_]], channel_multiplier=1).then_inc(consts, 1)
            pool.wait_ge(consts, 2)
            pool.affine_select(out=head_of[:], in_=head_of[:], compare_op=ALU.is_ge, fill=0.0, base=CD - 1,
                               pattern=[[CD, CH // KT_]], channel_multiplier=-1).then_inc(consts, 1)
            pool.wait_ge(consts, 3)
            pool.wait_ge(weights.loaded, 64)

            def mask_keys(b, par, g):
                wait_read(pool, [("key", 0)], b)
                pool.tensor_tensor(km[par][:, g], kb[:, g].unsqueeze(1).broadcast_to((P, CH // KT_, CTX)),
                                   head_of[:].unsqueeze(2).broadcast_to((P, CH // KT_, CTX)), ALU.mult).then_inc(key_masked, 1)

            def subtract(b, c):
                pool.wait_ge(maxed, b * UNITS + c + 1)
                k = c % 2
                pool.tensor_tensor(z[k][:], z[k][:], top[:, k].unsqueeze(2).broadcast_to((P, UH, CTX)),
                                   ALU.subtract).then_inc(shift, 1)

            def add_bias(b, par, t):
                if not first(b):
                    wait_read(pool, [("mix", 0), ("mix", 1)], b - 1)
                pool.wait_ge(staged[par], 8 * (b - par) + 16)
                pool.tensor_tensor(xb[:, t], xs[par][:, t], rows[:, 1], ALU.add).then_inc(token_sum, 1)

            def batch(b, par, before=True, after=True):
                for c in range(UNITS):
                    if c < UNITS - 2:
                        subtract(b, c + 2)
                    elif after:
                        subtract(b + 1, c + 2 - UNITS)
                    if c in (1, 3) and after:
                        mask_keys(b + 1, 1 - par, c // 2)
                    if c == 4 and before:
                        norm.root(pool, b - 1, 1)
                    if c in (5, 6):
                        add_bias(b, par, c - 5)
                    if c == 7:
                        norm.root(pool, b, 0)

            mask_keys(0, 0, 0)
            mask_keys(0, 0, 1)
            subtract(0, 0)
            subtract(0, 1)
            both(batch)(pool)
            norm.root(pool, BATCH - 1, 1)

        @block.scalar
        def _(act):
            act.wait_ge(weights.loaded, 64)

            def step(b, par, kind, i, bank, uses):
                src = shared[bank]
                if kind in ("mix", "value"):
                    return
                act.wait_ge(full[bank], uses + 1)
                if kind == "tokens":
                    ins = act.activation(xt[par][:], src[:].rearrange("p (g q) -> p g q", g=KT_), ACT.Copy)
                elif kind == "query":
                    for g in range(KT_):
                        ins = act.activation(q[par][:, g], src[:, g * SEQ:(g + 1) * SEQ], ACT.Identity, bias=bias[:, 0, g:g + 1])
                elif kind == "key":
                    if not first(b):
                        act.wait_ge(key_masked, b * KT_)
                    for g in range(KT_):
                        ins = act.activation(kb[:, g], src[:, g * CTX:(g + 1) * CTX], ACT.Identity, bias=bias[:, 1, g:g + 1])
                elif kind == "heads":
                    ins = act.activation(ot[:, i], src[:, 0:DIM].rearrange("p (g q) -> p g q", g=KT_), ACT.Copy)
                ins.then_inc(free[bank], 1)

            def value_high(b, par):
                wait_read(act, [("value", 0)], b)
                act.activation(vh[par][0:CTX, :, 0:CD], v[0:CTX], ACT.Copy, scale=SCALE).then_inc(v_high, 1)

            def power(b, c):
                k = c % 2
                act.wait_ge(shift, b * UNITS + c + 1)
                if not (first(b) and c < 2):
                    act.wait_ge(probs_t, b * UNITS + c - 1)
                act.activation(probs[k][:], z[k][:], ACT.Exp, scale=1.0 if additive else CD ** -0.5).then_inc(exped, 1)

            def batch(b, par, before=True, after=True):
                for c in range(UNITS):
                    k = c % 2
                    act.wait_ge(probs_t, b * UNITS + c + 1)
                    if not (first(b) and c < 2):
                        act.wait_ge(weighted, b * UNITS + c - 1)
                    act.activation(pth[k][0:CTX], t_bank[k][0:CTX], ACT.Copy, scale=PSCALE).then_inc(probs_high, 1)
                    if c < UNITS - 1:
                        power(b, c + 1)
                    elif after:
                        power(b + 1, 0)
                    for kind, i, bank, uses in CA.slot(c, b):
                        d = CA.serves(kind, i)
                        step(b + d, (par + d) % 2, kind, i, bank, uses)
                    if c == 2 and after:
                        value_high(b + 1, 1 - par)

            act.wait_ge(ones, 1)
            for kind, i, bank, uses in CA.prologue():
                step(0, 0, kind, i, bank, uses)
            value_high(0, 0)
            power(0, 0)
            both(batch)(act)
            for kind, i, bank, uses in CA.epilogue():
                step(BATCH - 1, 1, kind, i, bank, uses)

        @block.vector
        def _(dve):
            for k in range(2):
                dve.memset(vh[k][:, :, CD:CD + 1], SCALE)
                ins = dve.memset(vl[k][:, :, CD:CD + 1], 0.0)
            ins.then_inc(ones, 1)
            dve.wait_ge(weights.loaded, 64)

            def value(b, par, bank, uses):
                dve.wait_ge(full[bank], uses + 1)
                if not first(b):
                    dve.wait_ge(v_low, b)
                dve.tensor_tensor(v[0:CTX], shared[bank][0:CTX, 0:DIM].rearrange("p (h d) -> p h d", h=CH),
                                  rows[0:CTX, 0].rearrange("p (h d) -> p h d", h=CH), ALU.add).then_inc(free[bank], 1)

            def value_low(b, par):
                dve.wait_ge(v_high, b + 1)
                dve.scalar_tensor_tensor(out=vl[par][0:CTX, :, 0:CD], in0=v[0:CTX], scalar=SCALE,
                                         in1=vh[par][0:CTX, :, 0:CD], op0=ALU.mult, op1=ALU.subtract).then_inc(v_low, 1)

            def mask_scores(b, c):
                k = c % 2
                dve.wait_ge(scores, b * UNITS + c + 1)
                if not (first(b) and c < 2):
                    dve.wait_ge(exped, b * UNITS + c - 1)
                s = s_bank[k][:, 0:UH * CTX].rearrange("p (h k) -> p h k", h=UH)
                m = at(mask if additive else limit, b * TPB + c // (UNITS // TPB)).unsqueeze(1).broadcast_to((P, UH, CTX))
                if additive:
                    ins = dve.scalar_tensor_tensor(out=z[k][:], in0=s, scalar=CD ** -0.5, in1=m, op0=ALU.mult, op1=ALU.add)
                else:
                    ins = dve.tensor_tensor(z[k][:], s, m, ALU.min)
                ins.then_inc(masked, 1)

            def take_maximum(b, c):
                k = c % 2
                dve.wait_ge(masked, b * UNITS + c + 1)
                dve.tensor_reduce(top[:, k], z[k][:], AX.X, ALU.max).then_inc(maxed, 1)

            def probs_rest(b, c):
                k = c % 2
                dve.wait_ge(probs_high, b * UNITS + c + 1)
                dve.scalar_tensor_tensor(out=ptl[k][0:CTX], in0=t_bank[k][0:CTX], scalar=PSCALE, in1=pth[k][0:CTX],
                                         op0=ALU.mult, op1=ALU.subtract).then_inc(probs_low, 1)

            def normalise(b, t):
                dve.wait_ge(weighted, b * UNITS + (t + 1) * (UNITS // TPB))
                dve.wait_ge(normed, b * TPB + t)
                dve.reciprocal(inv[:, t], o_bank[t][:, :, CD:CD + 1].squeeze(2)).then_inc(inverted, 1)
                dve.wait_ge(inverted, b * TPB + t + 1)
                if not first(b):
                    wait_read(dve, [("heads", t)], b - 1)
                dve.tensor_tensor(o[:, t], o_bank[t][:, :, 0:CD], inv[:, t].unsqueeze(2).broadcast_to((P, CH, CD)),
                                  ALU.mult).then_inc(normed, 1)

            def residual(b, t, bank, uses):
                dve.wait_ge(full[bank], uses + 1)
                dve.wait_ge(token_sum, b * TPB + t + 1)
                dve.tensor_tensor(norm.res[:, t], shared[bank][:, 0:DIM], xb[:, t], ALU.add).then_inc(free[bank], 1)
                dve.wait_ge(free[bank], uses + 1)
                norm.statistics(dve, b, t)

            def batch(b, par, before=True, after=True):
                for c in range(UNITS):
                    two_on = (b, c + 2) if c < UNITS - 2 else (b + 1, c + 2 - UNITS) if after else None
                    if two_on:
                        mask_scores(*two_on)
                    probs_rest(b, c)
                    if two_on:
                        take_maximum(*two_on)
                    if c == 5:
                        normalise(b, 0)
                    if c == 1 and before:
                        normalise(b - 1, 1)
                    for kind, i, bank, uses in CA.slot(c, b):
                        if kind == "value":
                            value(b + 1, 1 - par, bank, uses)
                        if kind == "mix":
                            residual(b + CA.serves(kind, i), i, bank, uses)
                    if c == 0 and before:
                        norm.apply(dve, b - 1, 0, at(X, (b - 1) * TPB))
                    if c == 5 and before:
                        norm.apply(dve, b - 1, 1, at(X, (b - 1) * TPB + 1))
                    if c == 2 and after:
                        value_low(b + 1, 1 - par)

            for kind, i, bank, uses in CA.prologue():
                if kind == "value":
                    value(0, 0, bank, uses)
            value_low(0, 0)
            if not additive:
                dve.tensor_scalar(limit[:], mask[:], 0, -2 * OPEN, ALU.is_equal, ALU.mult).then_inc(limits, 1)
                dve.wait_ge(limits, 1)
                dve.tensor_scalar(limit[:], limit[:], OPEN, MASKED, ALU.add, ALU.max).then_inc(limits, 1)
                dve.wait_ge(limits, 2)
            for c in range(2):
                mask_scores(0, c)
                take_maximum(0, c)
            both(batch)(dve)
            norm.apply(dve, BATCH - 1, 0, at(X, (BATCH - 1) * TPB))
            normalise(BATCH - 1, 1)
            for kind, i, bank, uses in CA.epilogue():
                if kind == "mix":
                    residual(BATCH - 1, i, bank, uses)
            norm.apply(dve, BATCH - 1, 1, at(X, (BATCH - 1) * TPB + 1))

        @block.tensor
        def _(pe):
            def step(b, par, kind, i, bank, uses):
                dst = shared[bank]
                if not (isinstance(uses, int) and uses == 0):
                    pe.wait_ge(free[bank], uses)
                if kind == "tokens":
                    pe.wait_ge(staged[par], 8 * (b - par) + 16)
                    for g in range(KT_):
                        for t in range(TPB):
                            ins = pe.transpose(dst[:, g * SEQ + t * P:g * SEQ + (t + 1) * P],
                                               xs[par][:, t, g * P:(g + 1) * P], ident[:])
                elif kind == "query":
                    wait_read(pe, [("tokens", 0)], b)
                    for g in range(KT_):
                        for k in range(KT_):
                            ins = pe.matmul(dst[:, g * SEQ:(g + 1) * SEQ], w[:, 0, k, g * P:(g + 1) * P], xt[par][:, k],
                                            start=(k == 0), stop=(k == KT_ - 1))
                elif kind == "key":
                    pe.wait_ge(context_loaded[par], 8 * (b - par) + 16)
                    for g in range(KT_):
                        for k in range(KT_):
                            ins = pe.matmul(dst[:, g * CTX:(g + 1) * CTX], w[:, 1, k, g * P:(g + 1) * P],
                                            context[par][:, k], start=(k == 0), stop=(k == KT_ - 1))
                elif kind == "value":
                    for k in range(KT_):
                        ins = pe.matmul(dst[0:CTX, 0:DIM], context[par][:, k], w[:, 2, k],
                                        start=(k == 0), stop=(k == KT_ - 1))
                elif kind == "heads":
                    pe.wait_ge(normed, b * TPB + i + 1)
                    for g in range(KT_):
                        ins = pe.transpose(dst[:, g * P:(g + 1) * P],
                                           o[:, i, g * 8:(g + 1) * 8].rearrange("p h d -> p (h d)"), ident[:])
                else:
                    wait_read(pe, [("heads", i)], b)
                    for g in range(KT_):
                        ins = pe.matmul(dst[:, 0:DIM], ot[:, i, g], w[:, 3, g], start=(g == 0), stop=(g == KT_ - 1))
                ins.then_inc(full[bank], 1)

            def score(b, c, par):
                t, part = divmod(c, UNITS // TPB)
                g, h = part // 2, UH * (part % 2)
                if c == 0:
                    wait_read(pe, [("query", 0)], b)
                    pe.wait_ge(key_masked, (b + 1) * KT_)
                if not (first(b) and c < 2):
                    pe.wait_ge(masked, b * UNITS + c - 1)
                pe.matmul(s_bank[c % 2][:, 0:UH * CTX], q[par][:, g, t * P:(t + 1) * P],
                          km[par][:, g, h:h + UH].rearrange("p h k -> p (h k)"), start=True, stop=True).then_inc(scores, 1)

            def turn_probs(b, c):
                k = c % 2
                pe.wait_ge(exped, b * UNITS + c + 1)
                if not (first(b) and c < 2):
                    pe.wait_ge(probs_low, b * UNITS + c - 1)
                for h in range(UH):
                    ins = pe.transpose(t_bank[k][0:CTX, h * P:(h + 1) * P], probs[k][:, h], ident[:])
                ins.then_inc(probs_t, 1)

            def weigh(b, c, par):
                k, t = c % 2, c // (UNITS // TPB)
                pe.wait_ge(probs_low, b * UNITS + c + 1)
                if c == 0:
                    pe.wait_ge(v_low, b + 1)
                if c % (UNITS // TPB) == 0 and not first(b):
                    pe.wait_ge(normed, b * TPB + t - 1)
                for h in range(UH):
                    head = UH * (c % (UNITS // TPB)) + h
                    cols = slice(h * P, (h + 1) * P)
                    for n, (a, x) in enumerate(((pth[k], vh[par]), (pth[k], vl[par]), (ptl[k], vh[par]))):
                        ins = pe.matmul(o_bank[t][:, head, 0:CD + 1], a[0:CTX, cols], x[0:CTX, head],
                                        start=(n == 0), stop=(n == 2))
                ins.then_inc(weighted, 1)

            def batch(b, par, before=True, after=True):
                for c in range(UNITS):
                    turn_probs(b, c)
                    if c < UNITS - 2:
                        score(b, c + 2, par)
                    elif after:
                        score(b + 1, c + 2 - UNITS, 1 - par)
                    for kind, i, bank, uses in CA.slot(c, b):
                        d = CA.serves(kind, i)
                        step(b + d, (par + d) % 2, kind, i, bank, uses)
                    if c > 0:
                        weigh(b, c - 1, par)
                    elif before:
                        weigh(b - 1, UNITS - 1, 1 - par)

            pe.wait_ge(weights.loaded, 64)
            for kind, i, bank, uses in CA.prologue():
                step(0, 0, kind, i, bank, uses)
            score(0, 0, 0)
            score(0, 1, 0)
            both(batch)(pe)
            weigh(BATCH - 1, UNITS - 1, 1)
            for kind, i, bank, uses in CA.epilogue():
                step(BATCH - 1, 1, kind, i, bank, uses)

        block_scope.close()
        nc.clear_and_free_semaphores(sems)
        nc.all_engine_barrier()


EXPERTS, FF = 8, 1024
FT = FF // P
CAP = TOKENS * 5 // (4 * EXPERTS)
UNIT = CAP // 2
ROWS = UNIT // 2
SIDE = EXPERTS - 1
MOST = -(-TOKENS // UNIT)
END = 1 + (TOKENS + EXPERTS * UNIT) // UNIT
SLOTS = (END + 2) * UNIT
ZERO_ROWS = SLOTS // 32
POOL_TILES = (5, 10)
HSCALE = 16.0


def route(nc, router_dram, slots, ident, X, slot, starts, ahead_of_experts):
    with ExitStack() as ctx:
        def sb(name, shape, dt=F32):
            return ctx.enter_context(nc.sbuf_tensor("rt_" + name, shape, dt))

        def sem(name):
            return ctx.enter_context(nc.semaphore("rt_" + name))

        router = sb("router", [P, KT_, EXPERTS])
        before = sb("before", [P, P])
        before_bf = sb("before_bf", [P, P], BF16)
        ones_bf = sb("ones_bf", [P, P], BF16)
        ones = sb("ones", [P, TILES])
        code = sb("code", [P, EXPERTS])
        steps = sb("steps", [P, MOST])
        zeros = sb("zeros", [ZERO_ROWS, 8, DIM])
        router_h = sb("router_h", [P, KT_, EXPERTS], F16)
        router_l = sb("router_l", [P, KT_, EXPERTS], F16)
        xh = [sb(f"xh{k}", [P, KT_, 2 * P], F16) for k in range(2)]
        xl = [sb(f"xl{k}", [P, KT_, 2 * P], F16) for k in range(2)]
        gap = sb("gap", [P, TILES, EXPERTS])
        power = sb("power", [P, TILES, EXPERTS])
        best = sb("best", [P, TILES])
        pick = sb("pick", [P, TILES, EXPERTS])
        chosen = sb("chosen", [P, TILES])
        onehot = sb("onehot", [P, TILES, EXPERTS])
        onehot_bf = sb("onehot_bf", [P, TILES, EXPERTS], BF16)
        key = sb("key", [P, TILES])
        keys = sb("keys", [P, TOKENS])
        same = sb("same", [P, 2, P])
        ahead = sb("ahead", [P, TILES, TOKENS], BF16)
        own = sb("own", [P, TILES, EXPERTS])
        rank = sb("rank", [P, TILES])
        kept = sb("kept", [P, TILES])
        side = sb("side", [P, TILES])
        base = sb("base", [P, TILES])
        base_bf = sb("base_bf", [P, TILES], BF16)
        upto = sb("upto", [P, TILES])
        place = sb("place", [P, TILES])
        place_side = sb("place_side", [P, TILES])
        over = sb("over", [P, MOST])
        many = sb("many", [P, 1])
        counts = sb("counts", [P, EXPERTS])
        units = sb("units", [P, EXPERTS])
        first_unit = sb("first_unit", [P, EXPERTS + 1])
        first_slot = sb("first_slot", [P, SIDE])
        theirs = sb("theirs", [P, TILES, SIDE])
        base_slot = sb("base_slot", [P, 1])
        start_slot = sb("start_slot", [P, TILES])

        x_bank = [ctx.enter_context(nc.psum_tensor(f"rt_x{k}", [P, KT_, 2 * P], F32)) for k in range(2)]
        l_bank = ctx.enter_context(nc.psum_tensor("rt_logit_bank", [P, TILES, 32], F32))
        k_bank = ctx.enter_context(nc.psum_tensor("rt_key_bank", [P, TOKENS], F32))
        r_bank = ctx.enter_context(nc.psum_tensor("rt_rank_bank", [P, 64, EXPERTS], F32))

        router_loaded = sem("router_loaded")
        consts = sem("consts")
        zero_tile = sem("zero_tile")
        zeroed = sem("zeroed")
        x_turned = sem("x_turned")
        router_high = sem("router_high")
        router_low = sem("router_low")
        x_high = sem("x_high")
        x_low = sem("x_low")
        logits = sem("logits")
        onehot_ready = sem("onehot_ready")
        tallied = sem("tallied")
        step = sem("step")
        gap_ready = sem("gap_ready")
        power_ready = sem("power_ready")
        key_ready = sem("key_ready")
        keys_turned = sem("keys_turned")
        keys_ready = sem("keys_ready")
        diagonal = sem("diagonal")
        compared = sem("compared")
        pool_compared = sem("pool_compared")
        ranks = sem("ranks")
        base_ready = sem("base_ready")
        counted = sem("counted")
        slots_ready = sem("slots_ready")
        scattered = sem("scattered")

        def logit(pe, j):
            pe.wait_ge(x_low, j + 1)
            pe.wait_ge(router_low, 1)
            for t in range(2):
                n = 0
                for g in range(KT_):
                    for x, w in ((xh, router_h), (xh, router_l), (xl, router_h)):
                        ins = pe.matmul(l_bank[:, 2 * j + t, 0:EXPERTS], x[j % 2][:, g, t * P:(t + 1) * P], w[:, g],
                                        start=(n == 0), stop=(n == 3 * KT_ - 1))
                        n += 1
            ins.then_inc(logits, 1)

        block = ctx.enter_context(nc.Block())

        @block.sync
        def _(sp):
            sp.dma_start(router[:], router_dram).then_inc(router_loaded, 16)
            ahead_of_experts["sync"](sp)
            sp.wait_ge(zero_tile, 1)
            rows = ZERO_ROWS * 8
            for n in range(4):
                sp.dma_start(slots[n * rows:(n + 1) * rows].rearrange("(t p) d -> p t d", p=ZERO_ROWS), zeros[:]).then_inc(zeroed, 16)
            ahead_of_experts["sync late"](sp)

        @block.gpsimd
        def _(pool):
            pool.memset(zeros[:], 0.0).then_inc(zero_tile, 1)
            pool.memset(before[:], 1.0).then_inc(consts, 1)
            pool.memset(before_bf[:], 1.0).then_inc(consts, 1)
            pool.wait_ge(consts, 2)
            for m in (before, before_bf):
                pool.affine_select(out=m[:], in_=m[:], compare_op=ALU.is_gt, fill=0.0, base=0,
                                   pattern=[[1, P]], channel_multiplier=-1).then_inc(consts, 1)
            pool.memset(ones_bf[:], 1.0).then_inc(consts, 1)
            pool.memset(ones[:], 1.0).then_inc(consts, 1)
            pool.iota(code[:], pattern=[[-1, EXPERTS]], base=EXPERTS, channel_multiplier=0,
                      allow_small_or_imprecise_dtypes=True).then_inc(consts, 1)
            pool.iota(steps[:], pattern=[[UNIT, MOST]], base=0, channel_multiplier=0,
                      allow_small_or_imprecise_dtypes=True).then_inc(consts, 1)
            pool.wait_ge(keys_ready, 4)
            pool.wait_ge(key_ready, 1)
            for j in POOL_TILES:
                k, a, z = key[:, j:j + 1], j * P, (j + 1) * P
                pool.tensor_scalar(ahead[:, j, 0:a], keys[:, 0:a], k, 1.0, ALU.is_gt, ALU.mult)
                ins = pool.tensor_scalar(ahead[:, j, z:], keys[:, z:], k, 1.0, ALU.is_ge, ALU.mult)
            ins.then_inc(pool_compared, 1)
            ahead_of_experts["gpsimd"](pool)
            pool.wait_ge(zeroed, 16 * 4)
            pool.wait_ge(slots_ready, 1)
            for j in range(TILES):
                pool.indirect_dma_start(out=slots[:, :], out_offset=bass.IndirectOffsetOnAxis(ap=slot[:, j:j + 1], axis=0),
                                        in_=X[:, j], in_offset=None).then_inc(scattered, 16)
            pool.wait_ge(scattered, 16 * TILES)

        @block.scalar
        def _(act):
            act.wait_ge(router_loaded, 16)
            act.activation(router_h[:], router[:], ACT.Copy, scale=SCALE).then_inc(router_high, 1)
            for j in range(TILES // 2):
                act.wait_ge(x_turned, j + 1)
                if j >= 2:
                    act.wait_ge(logits, j - 1)
                act.activation(xh[j % 2][:], x_bank[j % 2][:], ACT.Copy, scale=SCALE).then_inc(x_high, 1)
            act.wait_ge(gap_ready, 1)
            act.activation(power[:], gap[:], ACT.Exp, scale=UNSCALE).then_inc(power_ready, 1)
            for n in range(4):
                act.wait_ge(keys_turned, n + 1)
                act.activation(keys[:, n * 512:(n + 1) * 512], k_bank[:, n * 512:(n + 1) * 512], ACT.Copy).then_inc(keys_ready, 1)
            ahead_of_experts["scalar"](act)

        @block.vector
        def _(dve):
            done = [0]

            def then(ins):
                done[0] += 1
                ins.then_inc(step, 1)
                dve.wait_ge(step, done[0])

            def wide(v):
                return v.unsqueeze(2).broadcast_to((P, TILES, EXPERTS))

            tally = l_bank[:, 0:4].rearrange("p a e -> p (a e)").rearrange("p (t e) -> p t e", e=EXPERTS)
            codes = code[:].unsqueeze(1).broadcast_to((P, TILES, EXPERTS))
            dve.wait_ge(router_high, 1)
            dve.scalar_tensor_tensor(out=router_l[:], in0=router[:], scalar=SCALE, in1=router_h[:],
                                     op0=ALU.mult, op1=ALU.subtract).then_inc(router_low, 1)
            for j in range(TILES // 2):
                dve.wait_ge(x_high, j + 1)
                dve.scalar_tensor_tensor(out=xl[j % 2][:], in0=x_bank[j % 2][:], scalar=SCALE, in1=xh[j % 2][:],
                                         op0=ALU.mult, op1=ALU.subtract).then_inc(x_low, 1)
            dve.wait_ge(consts, 8)
            dve.wait_ge(logits, TILES // 2)
            l = l_bank[:, :, 0:EXPERTS]
            then(dve.tensor_reduce(best[:], l, AX.X, ALU.max))
            dve.tensor_tensor(gap[:], l, wide(best[:]), ALU.subtract).then_inc(gap_ready, 1)
            dve.wait_ge(gap_ready, 1)
            then(dve.scalar_tensor_tensor(out=pick[:], in0=gap[:], scalar=0.0, in1=codes, op0=ALU.is_equal, op1=ALU.mult))
            then(dve.tensor_reduce(chosen[:], pick[:], AX.X, ALU.max))
            then(dve.tensor_tensor(onehot[:], codes, wide(chosen[:]), ALU.is_equal))
            dve.tensor_copy(onehot_bf[:], onehot[:]).then_inc(onehot_ready, 1)
            dve.wait_ge(power_ready, 1)
            dve.tensor_reduce(key[:], power[:], AX.X, ALU.add).then_inc(key_ready, 1)
            dve.wait_ge(tallied, 1)
            then(dve.tensor_reduce(counts[:], tally.rearrange("p t e -> p e t"), AX.X, ALU.add))
            then(dve.tensor_scalar(units[:], counts[:], float(UNIT), 1.0, ALU.is_gt, ALU.add))
            then(dve.memset(first_unit[:, 0:1], 1.0))
            then(dve.tensor_tensor_scan(first_unit[:, 1:EXPERTS], ones[:, 0:SIDE], units[:, 1:], 1.0, ALU.mult, ALU.add))
            then(dve.tensor_scalar(first_slot[:], first_unit[:, 0:SIDE], float(UNIT), None, ALU.mult))
            then(dve.tensor_tensor(theirs[:], onehot[:, :, 1:], first_slot[:].unsqueeze(1).broadcast_to((P, TILES, SIDE)), ALU.mult))
            then(dve.tensor_reduce(start_slot[:], theirs[:], AX.X, ALU.add))
            then(dve.tensor_scalar(base_slot[:], first_unit[:, SIDE:EXPERTS], float(UNIT), None, ALU.mult))
            dve.wait_ge(keys_ready, 4)
            dve.wait_ge(key_ready, 1)
            for j in range(TILES):
                k, a, z = key[:, j:j + 1], j * P, (j + 1) * P
                if j and j not in POOL_TILES:
                    dve.tensor_scalar(ahead[:, j, 0:a], keys[:, 0:a], k, None, ALU.is_gt)
                if j < TILES - 1 and j not in POOL_TILES:
                    dve.tensor_scalar(ahead[:, j, z:], keys[:, z:], k, None, ALU.is_ge)
                if j >= 2:
                    dve.wait_ge(compared, j - 1)
                dve.scalar_tensor_tensor(out=same[:, j % 2], in0=keys[:, a:z], scalar=k, in1=before[:],
                                         op0=ALU.is_equal, op1=ALU.mult).then_inc(diagonal, 1)
                dve.wait_ge(diagonal, j + 1)
                dve.scalar_tensor_tensor(out=ahead[:, j, a:z], in0=keys[:, a:z], scalar=k, in1=same[:, j % 2],
                                         op0=ALU.is_gt, op1=ALU.add).then_inc(compared, 1)
            dve.wait_ge(ranks, 1)
            then(dve.tensor_tensor(own[:], r_bank[:, 0:TILES], onehot[:], ALU.mult))
            then(dve.tensor_reduce(rank[:], own[:], AX.X, ALU.add))
            then(dve.tensor_scalar(kept[:], rank[:], float(CAP), None, ALU.is_lt))
            then(dve.tensor_scalar(side[:], onehot[:, :, 0], -1.0, 1.0, ALU.mult, ALU.add))
            then(dve.tensor_tensor(side[:], side[:], kept[:], ALU.mult))
            then(dve.tensor_scalar(base[:], side[:], -1.0, 1.0, ALU.mult, ALU.add))
            dve.tensor_copy(base_bf[:], base[:]).then_inc(base_ready, 1)
            then(dve.tensor_tensor(place_side[:], start_slot[:], rank[:], ALU.add))
            then(dve.tensor_tensor(place_side[:], place_side[:], side[:], ALU.mult))
            dve.wait_ge(counted, 1)
            total = r_bank[:, 32:34].rearrange("p a e -> p (a e)")
            then(dve.tensor_tensor_scan(upto[:], ones[:], total, 0.0, ALU.mult, ALU.add))
            then(dve.tensor_tensor(place[:], r_bank[:, 48:50].rearrange("p a e -> p (a e)"), upto[:], ALU.add))
            then(dve.tensor_tensor(place[:], total, place[:], ALU.subtract))
            then(dve.tensor_scalar(place[:], place[:], -1.0, base_slot[:], ALU.mult, ALU.add))
            then(dve.tensor_tensor(place[:], place[:], base[:], ALU.mult))
            dve.tensor_tensor(slot[:], place[:], place_side[:], ALU.add).then_inc(slots_ready, 1)
            then(dve.tensor_scalar(over[:], steps[:], upto[:, TILES - 1:TILES], None, ALU.is_lt))
            then(dve.tensor_reduce(many[:], over[:], AX.X, ALU.add))
            then(dve.tensor_scalar(many[:], many[:], 1.0, None, ALU.max))
            then(dve.tensor_tensor(first_unit[:, EXPERTS:], first_unit[:, SIDE:EXPERTS], many[:], ALU.add))
            then(dve.tensor_scalar(starts[:], first_unit[:], -1.0, None, ALU.add))
            ahead_of_experts["vector"](dve)

        @block.tensor
        def _(pe):
            for j in range(TILES // 2):
                if j >= 2:
                    pe.wait_ge(x_low, j - 1)
                for t in range(2):
                    for g in range(KT_):
                        ins = pe.transpose(x_bank[j % 2][:, g, t * P:(t + 1) * P], X[:, 2 * j + t, g * P:(g + 1) * P], ident[:])
                ins.then_inc(x_turned, 1)
                if j:
                    logit(pe, j - 1)
            logit(pe, TILES // 2 - 1)
            pe.wait_ge(consts, 8)
            pe.wait_ge(onehot_ready, 1)
            pe.matmul(l_bank[:, 0:4].rearrange("p a e -> p (a e)"), ones_bf[:], onehot_bf[:].rearrange("p t e -> p (t e)"),
                      start=True, stop=True).then_inc(tallied, 1)
            pe.wait_ge(key_ready, 1)
            for j in range(TILES):
                ins = pe.transpose(k_bank[:, j * P:(j + 1) * P], key[:, j:j + 1].broadcast_to((P, P)), ident[:])
                if j % 4 == 3:
                    ins.then_inc(keys_turned, 1)
            pe.wait_ge(compared, TILES)
            pe.wait_ge(pool_compared, 1)
            for i in range(TILES):
                for j in range(TILES):
                    ins = pe.matmul(r_bank[:, i], ahead[:, j, i * P:(i + 1) * P], onehot_bf[:, j],
                                    start=(j == 0), stop=(j == TILES - 1))
            ins.then_inc(ranks, 1)
            pe.wait_ge(base_ready, 1)
            pe.matmul(r_bank[:, 32:34].rearrange("p a e -> p (a e)"), ones_bf[:], base_bf[:], start=True, stop=True)
            pe.matmul(r_bank[:, 48:50].rearrange("p a e -> p (a e)"), before_bf[:], base_bf[:], start=True, stop=True).then_inc(counted, 1)


def experts(nc, router_dram, w1_dram, w2_dram, bias_dram, slots, slot, ident, X, next_loads, gates):
    with ExitStack() as ctx:
        def sb(name, shape, dt=F32):
            return ctx.enter_context(nc.sbuf_tensor("ex_" + name, shape, dt))

        def sem(name):
            return ctx.enter_context(nc.semaphore("ex_" + name))

        starts = sb("starts", [P, EXPERTS + 1], I32)
        stage1 = [sb(f"stage1{k}", [P, KT_, FF]) for k in range(2)]
        stage2 = [sb(f"stage2{k}", [P, FT, DIM]) for k in range(2)]
        w1h = [sb(f"w1h{k}", [P, KT_, FF], F16) for k in range(2)]
        w1l = [sb(f"w1l{k}", [P, KT_, FF], F16) for k in range(2)]
        w2h = [sb(f"w2h{k}", [P, FT, DIM], F16) for k in range(2)]
        w2l = [sb(f"w2l{k}", [P, FT, DIM], F16) for k in range(2)]
        biases = sb("biases", [P, EXPERTS, FT + KT_])
        bias = [sb(f"bias{k}", [P, FT + KT_]) for k in range(2)]

        biases_loaded = sem("biases_loaded")
        w_loaded = [sem("w_loaded0"), sem("w_loaded1")]
        w1_high = sem("w1_high")
        w2_high = sem("w2_high")
        bias_ready = sem("bias_ready")
        w1_low = sem("w1_low")
        w2_scaled = sem("w2_scaled")
        w2_low = sem("w2_low")

        def load_weights(sp, n, k):
            one = (lambda dram: dram[n]) if isinstance(n, int) else (lambda dram: dram[bass.ds(n, 1)].squeeze(0))
            sp.dma_start(stage1[k][:], one(w1_dram)).then_inc(w_loaded[k], 16)
            sp.dma_start(stage2[k][:], one(w2_dram)).then_inc(w_loaded[k], 16)

        def split1(dve, n, k):
            dve.wait_ge(w_loaded[k], 16 * (n - k) + 32)
            dve.tensor_scalar(w1h[k][:], stage1[k][:], SCALE, None, ALU.mult).then_inc(w1_high, 1)
            dve.wait_ge(w1_high, n + 1)
            dve.scalar_tensor_tensor(out=w1l[k][:], in0=stage1[k][:], scalar=SCALE, in1=w1h[k][:],
                                     op0=ALU.mult, op1=ALU.subtract).then_inc(w1_low, 1)

        def high2(act, n, k):
            act.wait_ge(w_loaded[k], 16 * (n - k) + 32)
            act.activation(w2h[k][:], stage2[k][:], ACT.Copy, scale=SCALE).then_inc(w2_high, 1)
            act.activation(bias[k][:], at(biases, n), ACT.Copy).then_inc(bias_ready, 1)

        def low2(pool, n):
            stage = stage2[n % 2]
            pool.wait_ge(w2_high, n + 1)
            pool.tensor_scalar(stage[:], stage[:], SCALE, 0.0, ALU.mult, ALU.add).then_inc(w2_scaled, 1)
            pool.wait_ge(w2_scaled, n + 1)
            pool.tensor_tensor(w2l[n % 2][:], stage[:], w2h[n % 2][:], ALU.subtract).then_inc(w2_low, 1)

        def first_loads(sp):
            load_weights(sp, 0, 0)
            load_weights(sp, 1, 1)
            sp.dma_start(biases[:], bias_dram).then_inc(biases_loaded, 16)

        def second_loads(sp):
            next_loads(sp)
            sp.wait_ge(w1_low, 1)
            sp.wait_ge(w2_low, 1)
            load_weights(sp, 2, 0)

        def first_lows(pool):
            for n in (0, 1):
                low2(pool, n)

        def first_split1(dve):
            for n in (0, 1):
                split1(dve, n, n)
            gates.rates(dve)

        def first_high2(act):
            act.wait_ge(biases_loaded, 16)
            for n in (0, 1):
                high2(act, n, n)
            gates.power_of_base(act)

        route(nc, router_dram, slots, ident, X, slot, starts,
              {"sync": first_loads, "sync late": second_loads, "gpsimd": first_lows, "vector": first_split1, "scalar": first_high2})

        xe = sb("xe", [ROWS, 2, DIM])
        xh = sb("xh", [P, KT_, UNIT], F16)
        xl = sb("xl", [P, KT_, UNIT], F16)
        h = [sb(f"h{s}", [P, 2, UNIT]) for s in range(4)]
        hh = [sb(f"hh{s}", [P, 2, UNIT], F16) for s in range(4)]
        hl = [sb(f"hl{s}", [P, 2, UNIT], F16) for s in range(4)]
        yt = sb("yt", [P, KT_, UNIT])
        y = sb("y", [ROWS, 2, DIM])
        mark = sb("mark", [1, 2], I32)

        x_bank = ctx.enter_context(nc.psum_tensor("ex_x_bank", [P, KT_, 256], F32))
        u_bank = [ctx.enter_context(nc.psum_tensor(f"ex_up{s}", [P, 2, 256], F32)) for s in range(4)]
        d_bank = [ctx.enter_context(nc.psum_tensor(f"ex_down{g}", [P, 512], F32)) for g in range(KT_)]
        y_bank = ctx.enter_context(nc.psum_tensor("ex_y_bank", [P, 2, DIM], F32))

        x_loaded = sem("x_loaded")
        x_turned = sem("x_turned")
        x_high = sem("x_high")
        x_low = sem("x_low")
        up = sem("up")
        h_ready = sem("h_ready")
        h_high = sem("h_high")
        h_low = sem("h_low")
        down = sem("down")
        yt_ready = sem("yt_ready")
        y_turned = sem("y_turned")
        y_ready = sem("y_ready")
        stored = sem("stored")
        all_stored = sem("all_stored")
        all_loaded = sem("all_loaded")

        def start_of(engine, n):
            where = starts[0:1, n:n + 1] if isinstance(n, int) else starts[0:1, bass.ds(n, 1)]
            return engine.value_load(where, min_val=0, max_val=END - 1)

        def units_of(engine, n, k, unit, begin=None, prepare=None):
            a, z = start_of(engine, n), start_of(engine, n + 1)
            if begin:
                begin(n, k)
            if prepare:
                prepare(n + 1, 1 - k, a)
            with engine.Fori(a, z) as u:
                unit(u + 1, k, n)

        def all_units(engine, unit, begin=None, prepare=None):
            units_of(engine, 0, 0, unit, begin)
            with engine.Fori(0, SIDE // 2) as i:
                units_of(engine, 2 * i + 1, 1, unit, begin, prepare)
                units_of(engine, 2 * i + 2, 0, unit, begin, prepare)
            units_of(engine, SIDE, 1, unit, begin)

        block = ctx.enter_context(nc.Block())

        @block.sync
        def _(sp):
            def rows(u):
                return slots[bass.ds(u * UNIT, UNIT)].rearrange("(t p) d -> p t d", p=ROWS)

            def load(u):
                sp.dma_start(xe[:], rows(u)).then_inc(x_loaded, 16)

            def store(u):
                sp.wait_ge(y_ready, u + 1)
                sp.dma_start(rows(u), y[:]).then_inc(stored, 16)

            sp.dma_start(mark[0:1, 0:1], starts[0:1, 0:1]).then_inc(stored, 16)
            load(1)
            sp.wait_ge(x_turned, 1)
            load(2)

            def unit(u, k, n):
                sp.wait_ge(x_turned, u + 1)
                load(u + 2)
                store(u - 1)

            def more_weights(n, k):
                sp.wait_ge(w1_low, n + 1)
                sp.wait_ge(w2_low, n + 1)
                load_weights(sp, n + 2, k)

            units_of(sp, 0, 0, unit)
            with sp.Fori(0, SIDE // 2 - 1) as i:
                units_of(sp, 2 * i + 1, 1, unit, more_weights)
                units_of(sp, 2 * i + 2, 0, unit, more_weights)
            units_of(sp, SIDE - 2, 1, unit, more_weights)
            units_of(sp, SIDE - 1, 0, unit)
            units_of(sp, SIDE, 1, unit)
            last = start_of(sp, EXPERTS)
            store(last)
            sp.wait_ge(stored, last * 16 + 32)
            sp.dma_start(mark[0:1, 0:1], starts[0:1, 0:1]).then_inc(all_stored, 16)
            sp.wait_ge(x_loaded, last * 16 + 32)
            sp.dma_start(mark[0:1, 1:2], starts[0:1, 0:1]).then_inc(all_loaded, 16)
            sp.wait_ge(all_loaded, 16)
            sp.wait_ge(all_stored, 16)

        @block.gpsimd
        def _(pool):
            pool.memset(yt[:], 0.0).then_inc(yt_ready, 1)
            for n in range(2, EXPERTS):
                low2(pool, n)

        @block.scalar
        def _(act):
            def split_x(u):
                act.wait_ge(x_turned, u)
                act.activation(xh[:], x_bank[:, :, 0:UNIT], ACT.Copy, scale=SCALE).then_inc(x_high, 1)

            def unit(u, k, n):
                for s in range(4):
                    act.wait_ge(up, u * 4 + s - 3)
                    for j in range(2):
                        m = 2 * s + j
                        ins = act.activation(h[s][:, j], u_bank[s][:, j, 0:UNIT], ACT.Relu, scale=UNSCALE, bias=bias[k][:, m:m + 1])
                    ins.then_inc(h_ready, 1)
                split_x(u + 1)
                for g in range(KT_):
                    act.wait_ge(down, u * KT_ + g - 1)
                    act.activation(yt[:, g], d_bank[g][:, 0:UNIT], ACT.Identity, scale=1.0 / (SCALE * HSCALE),
                                   bias=bias[k][:, FT + g:FT + g + 1]).then_inc(yt_ready, 1)

            def prepare(n, k, a):
                act.wait_ge(yt_ready, a * KT_ + 1)
                high2(act, n, k)

            act.wait_ge(bias_ready, 2)
            split_x(1)
            all_units(act, unit, prepare=prepare)

        @block.vector
        def _(dve):
            def split_x(u):
                dve.wait_ge(x_high, u)
                dve.scalar_tensor_tensor(out=xl[:], in0=x_bank[:, :, 0:UNIT], scalar=SCALE, in1=xh[:],
                                         op0=ALU.mult, op1=ALU.subtract).then_inc(x_low, 1)

            def take_y(u):
                dve.wait_ge(y_turned, u + 1)
                dve.wait_ge(stored, u * 16 + 16)
                dve.tensor_copy(y[:], y_bank[0:ROWS]).then_inc(y_ready, 1)

            def unit(u, k, n):
                for s in range(4):
                    dve.wait_ge(h_ready, u * 4 + s - 3)
                    dve.tensor_scalar(hh[s][:], h[s][:], HSCALE, None, ALU.mult).then_inc(h_high, 1)
                    dve.wait_ge(h_high, u * 4 + s - 3)
                    dve.scalar_tensor_tensor(out=hl[s][:], in0=h[s][:], scalar=HSCALE, in1=hh[s][:],
                                             op0=ALU.mult, op1=ALU.subtract).then_inc(h_low, 1)
                    if s == 1:
                        take_y(u - 1)
                split_x(u + 1)

            def prepare(n, k, a):
                dve.wait_ge(yt_ready, a * KT_ + 1)
                split1(dve, n, k)

            split_x(1)
            all_units(dve, unit, prepare=prepare)
            take_y(start_of(dve, EXPERTS))

        @block.tensor
        def _(pe):
            def turn_x(u):
                pe.wait_ge(x_loaded, u * 16)
                for g in range(KT_):
                    for t in range(2):
                        ins = pe.transpose(x_bank[:, g, t * ROWS:(t + 1) * ROWS], xe[:, t, g * P:(g + 1) * P], ident[0:ROWS, 0:ROWS])
                ins.then_inc(x_turned, 1)

            def turn_y(u):
                pe.wait_ge(yt_ready, u * KT_ + 1)
                for g in range(KT_):
                    for t in range(2):
                        ins = pe.transpose(y_bank[0:ROWS, t, g * P:(g + 1) * P], yt[:, g, t * ROWS:(t + 1) * ROWS], ident[:])
                ins.then_inc(y_turned, 1)

            def way_up(u, k, s):
                for j in range(2):
                    m, n = 2 * s + j, 0
                    for g in range(KT_):
                        for w, x in ((w1h[k], xh), (w1h[k], xl), (w1l[k], xh)):
                            ins = pe.matmul(u_bank[s][:, j, 0:UNIT], w[:, g, m * P:(m + 1) * P], x[:, g],
                                            start=(n == 0), stop=(n == 3 * KT_ - 1))
                            n += 1
                ins.then_inc(up, 1)

            def way_down(u, k, s):
                pe.wait_ge(h_low, u * 4 + s - 3)
                for g in range(KT_):
                    for j in range(2):
                        m = 2 * s + j
                        for n, (w, x) in enumerate(((w2h[k], hh[s]), (w2h[k], hl[s]), (w2l[k], hh[s]))):
                            ins = pe.matmul(d_bank[g][:, 0:UNIT], w[:, m, g * P:(g + 1) * P], x[:, j],
                                            start=(m == 0 and n == 0), stop=(m == FT - 1 and n == 2))
                    if s == 3:
                        ins.then_inc(down, 1)

            def unit(u, k, n):
                pe.wait_ge(w1_low, n + 1)
                pe.wait_ge(w2_low, n + 1)
                pe.wait_ge(x_low, u)
                way_up(u, k, 0)
                turn_y(u - 1)
                way_up(u, k, 1)
                way_up(u, k, 2)
                way_down(u, k, 0)
                way_up(u, k, 3)
                way_down(u, k, 1)
                way_down(u, k, 2)
                turn_x(u + 1)
                way_down(u, k, 3)

            turn_x(1)
            all_units(pe, unit)
            turn_y(start_of(pe, EXPERTS))


HID = 512
HT = HID // P
TAPS = 4
SERIES = 9


class Gates:

    def __init__(self, ctx, nc):
        def sb(name, shape):
            return ctx.enter_context(nc.sbuf_tensor("re_" + name, shape, F32))

        def sem(name):
            return ctx.enter_context(nc.semaphore("re_" + name))

        self.w_in = sb("w_in", [P, KT_, 2 * HID])
        self.w_g = sb("w_g", [P, HT, 2 * HID])
        self.w_out = sb("w_out", [P, HT, DIM])
        self.hid = sb("hid", [P, TAPS + 4, HT])
        self.half_bias = sb("half_bias", [P, 2, HT])
        self.rate = sb("rate", [P, HT])
        self.low, self.power = sb("low", [P, HT]), sb("power", [P, HT])
        self.ratio, self.square, self.series = sb("ratio", [P, HT]), sb("square", [P, HT]), sb("series", [P, HT])
        self.hid_loaded = sem("hid_loaded")
        self.w_loaded = sem("w_loaded")
        self.setup = sem("setup")
        self.setup_act = sem("setup_act")

    def load(self, sp, w_in_dram, w_g_dram, w_out_dram, hid_dram):
        sp.dma_start(self.hid[:], hid_dram).then_inc(self.hid_loaded, 16)
        sp.dma_start(self.w_in[:], w_in_dram).then_inc(self.w_loaded, 16)
        sp.dma_start(self.w_g[:], w_g_dram).then_inc(self.w_loaded, 16)
        sp.dma_start(self.w_out[:], w_out_dram).then_inc(self.w_loaded, 16)

    def power_of_base(self, act):
        act.wait_ge(self.setup, 1)
        act.activation(self.power[:], self.low[:], ACT.Exp).then_inc(self.setup_act, 1)

    def rates(self, dve):
        done = [0]

        def then(ins):
            done[0] += 1
            ins.then_inc(self.setup, 1)
            dve.wait_ge(self.setup, done[0])

        low, power, ratio, square, series = self.low, self.power, self.ratio, self.square, self.series
        base = self.hid[:, TAPS + 3]
        dve.wait_ge(self.hid_loaded, 16)
        then(dve.scalar_tensor_tensor(out=low[:], in0=base, scalar=-1.0, in1=base, op0=ALU.mult, op1=ALU.min))
        dve.wait_ge(self.setup_act, 1)
        then(dve.tensor_scalar(ratio[:], power[:], 2.0, None, ALU.add))
        then(dve.reciprocal(square[:], ratio[:]))
        then(dve.tensor_tensor(ratio[:], power[:], square[:], ALU.mult))
        then(dve.tensor_tensor(square[:], ratio[:], ratio[:], ALU.mult))
        then(dve.memset(series[:], 1.0 / (2 * SERIES + 1)))
        for n in reversed(range(SERIES)):
            then(dve.tensor_tensor(series[:], series[:], square[:], ALU.mult))
            then(dve.tensor_scalar(series[:], series[:], 1.0 / (2 * n + 1), None, ALU.add))
        then(dve.scalar_tensor_tensor(out=series[:], in0=ratio[:], scalar=2.0, in1=series[:], op0=ALU.mult, op1=ALU.mult))
        then(dve.scalar_tensor_tensor(out=self.rate[:], in0=base, scalar=0.0, in1=series[:], op0=ALU.max, op1=ALU.add))
        then(dve.tensor_scalar(self.rate[:], self.rate[:], 2.0, None, ALU.mult))
        then(dve.tensor_scalar(self.half_bias[:], self.hid[:, TAPS + 1:TAPS + 3], 0.5, None, ALU.mult))


def recurrence(nc, gates, slots, slot, ident, half, X, next_loads):
    with ExitStack() as ctx:
        def sb(name, shape, dt=F32):
            return ctx.enter_context(nc.sbuf_tensor("re_" + name, shape, dt))

        def sem(name):
            return ctx.enter_context(nc.semaphore("re_" + name))

        w_in, w_g, w_out, hid, half_bias, rate = gates.w_in, gates.w_g, gates.w_out, gates.hid, gates.half_bias, gates.rate
        y = [sb(f"y{k}", [P, TPB, DIM]) for k in range(2)]
        tiny = sb("tiny", [P, 1])
        where = [sb(f"where{k}", [P, TPB], I32) for k in range(2)]
        carry = sb("carry", [P, 4])
        xs = [sb(f"xs{k}", [P, TPB, DIM]) for k in range(2)]
        xt = sb("xt", [P, KT_, SEQ])
        padded = sb("padded", [P, HT, TAPS - 1 + SEQ])
        conv = [sb(f"conv{k}", [P, HT, SEQ]) for k in range(2)]
        gate = [sb(f"gate{k}", [P, HT, SEQ]) for k in range(2)]
        tf = sb("tf", [P, 2, SEQ])
        ti = [sb(f"ti{p}", [P, 2, SEQ]) for p in range(2)]
        T = [sb(f"T{p}", [P, 2, SEQ]) for p in range(2)]
        more = [sb(f"more{p}", [P, 2, SEQ]) for p in range(2)]
        recip = [sb(f"recip{p}", [P, 2, SEQ]) for p in range(2)]
        d = [sb(f"d{p}", [P, 2, SEQ]) for p in range(2)]
        nb = [sb(f"nb{p}", [P, 2, SEQ]) for p in range(2)]
        alpha = [sb(f"alpha{p}", [P, 2, SEQ]) for p in range(2)]
        beta = [sb(f"beta{p}", [P, 2, SEQ]) for p in range(2)]
        scaled = [sb(f"scaled{p}", [P, 2, SEQ]) for p in range(2)]
        bterm = [sb(f"bterm{p}", [P, 2, SEQ]) for p in range(2)]
        h = [sb(f"h{p}", [P, 2, SEQ]) for p in range(2)]
        gh = sb("gh", [P, HT, SEQ])

        x_bank = ctx.enter_context(nc.psum_tensor("re_x", [P, KT_, SEQ], F32))
        i_bank = [ctx.enter_context(nc.psum_tensor(f"re_in{k}", [P, 2, SEQ], F32)) for k in range(2)]
        g_bank = [ctx.enter_context(nc.psum_tensor(f"re_g{m}", [P, 2, SEQ], F32)) for m in range(HT)]
        o_bank = ctx.enter_context(nc.psum_tensor("re_out", [P, TPB, DIM], F32))

        norm = Norm(ctx, nc, "re", half)
        norm_in = Norm(ctx, nc, "rn", half)
        gathered = [sem("gathered0"), sem("gathered1")]
        pointed = sem("pointed")
        entered = sem("entered")
        staged = [sem("staged0"), sem("staged1")]
        consts = sem("consts")
        cleared = sem("cleared")
        x_turned = sem("x_turned")
        x_ready = sem("x_ready")
        in_done = sem("in_done")
        in_read = sem("in_read")
        conved = sem("conved")
        g_done = sem("g_done")
        tf_done = sem("tf_done")
        ti_done = sem("ti_done")
        T_done = sem("T_done")
        chain = sem("chain")
        beta_ready = sem("beta_ready")
        doubled = sem("doubled")
        scaled_ready = sem("scaled_ready")
        bterm_ready = sem("bterm_ready")
        scanned = sem("scanned")
        gated = sem("gated")
        out_done = sem("out_done")
        summed = sem("summed")

        def both(batch):
            def run(engine):
                batch(0, 0, before=False)
                with engine.Fori(0, BATCH // 2 - 2) as i:
                    batch(2 * i + 1, 1)
                    batch(2 * i + 2, 0)
                batch(BATCH - 3, 1, fetches=False)
                batch(BATCH - 2, 0, enters=False, fetches=False)
                batch(BATCH - 1, 1, after=False, enters=False, fetches=False)
            return run

        block = ctx.enter_context(nc.Block())

        @block.sync
        def _(sp):
            def stage(b, par):
                sp.wait_ge(norm_in.ln_done, (b + 1) * TPB)
                sp.dma_start(xs[par][:], X[:, bass.ds(b * TPB, TPB)]).then_inc(staged[par], 16)

            stage(0, 0)
            stage(1, 1)
            next_loads(sp)
            with sp.Fori(1, BATCH // 2) as i:
                stage(2 * i, 0)
                stage(2 * i + 1, 1)

        @block.gpsimd
        def _(pool):
            pool.memset(tiny[:], 0.25e-6).then_inc(consts, 1)

            def fetch(b, par):
                def passes(n):
                    pool.tensor_tensor(carry[:, 2 * par + n:2 * par + n + 1], half[:], half[:], ALU.add)

                if not (isinstance(b, int) and b < 2):
                    pool.wait_ge(entered, (b - 1) * TPB)
                    passes(0)
                pool.tensor_copy(where[par][:], slot[:, bass.ds(b * TPB, TPB)]).then_inc(pointed, 1)
                pool.wait_ge(pointed, b + 1)
                passes(1)
                for t in range(TPB):
                    pool.indirect_dma_start(out=y[par][:, t], out_offset=None, in_=slots[:, :],
                                            in_offset=bass.IndirectOffsetOnAxis(ap=where[par][:, t:t + 1], axis=0)).then_inc(gathered[par], 16)

            def root_in(b):
                norm_in.root(pool, b, 0)
                norm_in.root(pool, b, 1)

            def scale_input(b, par, p):
                c = conv[par][:, 2 * p:2 * p + 2]
                pool.wait_ge(ti_done, b * HT + 2 * p + 2)
                if not first(b):
                    pool.wait_ge(bterm_ready, 2 * b + p - 1)
                pool.tensor_tensor(scaled[p][:], ti[p][:], c, ALU.mult).then_inc(doubled, 1)
                pool.wait_ge(doubled, 2 * b + p + 1)
                pool.tensor_tensor(scaled[p][:], scaled[p][:], c, ALU.add).then_inc(scaled_ready, 1)

            def times_beta(b, p):
                pool.wait_ge(scaled_ready, 2 * b + p + 1)
                pool.wait_ge(beta_ready, 2 * b + p + 1)
                pool.tensor_tensor(bterm[p][:], scaled[p][:], beta[p][:], ALU.mult).then_inc(bterm_ready, 1)

            def batch(b, par, before=True, after=True, enters=True, fetches=True):
                if fetches:
                    fetch(b + 3, 1 - par)
                if before:
                    times_beta(b - 1, 0)
                    times_beta(b - 1, 1)
                if enters:
                    root_in(b + 2)
                if before:
                    norm.root(pool, b - 1, 0)
                    norm.root(pool, b - 1, 1)
                scale_input(b, par, 0)
                scale_input(b, par, 1)

            for b in (0, 1):
                fetch(b, b)
            root_in(0)
            root_in(1)
            fetch(2, 0)
            both(batch)(pool)
            times_beta(BATCH - 1, 0)
            times_beta(BATCH - 1, 1)
            norm.root(pool, BATCH - 1, 0)
            norm.root(pool, BATCH - 1, 1)

        @block.scalar
        def _(act):
            act.wait_ge(consts, 1)

            def tokens(b):
                act.wait_ge(x_turned, b + 1)
                act.activation(xt[:], x_bank[:], ACT.Copy).then_inc(x_ready, 1)

            def conv_input(b):
                if not first(b):
                    act.wait_ge(conved, b * TAPS * HT)
                for p in range(2):
                    act.wait_ge(in_done, 4 * b + p + 1)
                    act.activation(padded[:, 2 * p:2 * p + 2, TAPS - 1:], i_bank[p][:], ACT.Copy).then_inc(in_read, 1)

            def gates(b, par):
                if not (isinstance(b, int) and b < 2):
                    act.wait_ge(gated, 2 * b - 2)
                for p in range(2):
                    act.wait_ge(in_done, 4 * b + 2 + p + 1)
                    act.activation(gate[par][:, 2 * p:2 * p + 2], i_bank[p][:], ACT.Gelu).then_inc(in_read, 1)

            def tile(b, m):
                p, k = divmod(m, 2)
                act.wait_ge(g_done, b * HT + m + 1)
                if not (first(b) and m < 2):
                    act.wait_ge(T_done, b * HT + m - 1)
                act.activation(tf[:, k], g_bank[m][:, 0], ACT.Tanh, scale=0.5, bias=half_bias[:, 0, m:m + 1]).then_inc(tf_done, 1)
                if not first(b):
                    act.wait_ge(scaled_ready, 2 * b + p - 1)
                act.activation(ti[p][:, k], g_bank[m][:, 1], ACT.Tanh, scale=0.5, bias=half_bias[:, 1, m:m + 1]).then_inc(ti_done, 1)
                act.wait_ge(tf_done, b * HT + m + 1)
                if not first(b):
                    act.wait_ge(chain, 10 * b + 5 * p - 7)
                act.activation(T[p][:, k], tf[:, k], ACT.Tanh, scale=rate[:, m:m + 1], bias=rate[:, m:m + 1]).then_inc(T_done, 1)

            def root(b, p):
                act.wait_ge(chain, 10 * b + 5 * p + 4)
                act.activation(beta[p][:], nb[p][:], ACT.Sqrt, scale=-0.25, bias=tiny[:]).then_inc(beta_ready, 1)

            def batch(b, par, before=True, after=True, enters=True, fetches=True):
                if after:
                    tokens(b + 1)
                    conv_input(b + 1)
                if before:
                    root(b - 1, 0)
                    root(b - 1, 1)
                tile(b, 0)
                if after:
                    gates(b + 1, 1 - par)
                tile(b, 1)
                tile(b, 2)
                tile(b, 3)

            tokens(0)
            conv_input(0)
            gates(0, 0)
            both(batch)(act)
            root(BATCH - 1, 0)
            root(BATCH - 1, 1)

        @block.vector
        def _(dve):
            dve.memset(padded[:, :, 0:TAPS - 1], 0.0).then_inc(cleared, 1)

            def enter(b, par):
                for t in range(TPB):
                    dve.wait_ge(gathered[par], 16 * (b - par) + 32)
                    if not first(b):
                        dve.wait_ge(norm_in.ln_done, b * TPB)
                    dve.tensor_tensor(norm_in.res[:, t], y[par][:, t], at(X, b * TPB + t), ALU.add).then_inc(entered, 1)
                    dve.wait_ge(entered, b * TPB + t + 1)
                    norm_in.statistics(dve, b, t)

            def enter_norm(b):
                for t in range(TPB):
                    norm_in.apply(dve, b, t, at(X, b * TPB + t))

            def convolve(b, par, p):
                dve.wait_ge(in_read, 4 * b + p + 1)
                if not (isinstance(b, int) and b < 2):
                    dve.wait_ge(scaled_ready, 2 * b - 2)
                for tap in range(TAPS):
                    for k in range(2):
                        m = 2 * p + k
                        out, x, w = conv[par][:, m], padded[:, m, tap:tap + SEQ], hid[:, tap, m:m + 1]
                        if tap == 0:
                            ins = dve.tensor_scalar(out, x, w, hid[:, TAPS, m:m + 1], ALU.mult, ALU.add)
                        else:
                            dve.wait_ge(conved, b * TAPS * HT + TAPS * 2 * p + 2 * tap + k - 1)
                            ins = dve.scalar_tensor_tensor(out=out, in0=x, scalar=w, in1=out, op0=ALU.mult, op1=ALU.add)
                        ins.then_inc(conved, 1)

            def decay(b, p):
                n = 10 * b + 5 * p
                dve.wait_ge(T_done, b * HT + 2 * p + 2)
                dve.tensor_scalar(more[p][:], T[p][:], 1.0, None, ALU.add).then_inc(chain, 1)
                dve.wait_ge(chain, n + 1)
                dve.reciprocal(recip[p][:], more[p][:]).then_inc(chain, 1)
                dve.wait_ge(chain, n + 2)
                dve.scalar_tensor_tensor(out=d[p][:], in0=T[p][:], scalar=2.0, in1=recip[p][:], op0=ALU.mult, op1=ALU.mult).then_inc(chain, 1)
                dve.wait_ge(chain, n + 3)
                dve.scalar_tensor_tensor(out=nb[p][:], in0=d[p][:], scalar=-2.0, in1=d[p][:], op0=ALU.add, op1=ALU.mult).then_inc(chain, 1)
                dve.tensor_scalar(alpha[p][:], d[p][:], -1.0, 1.0, ALU.mult, ALU.add).then_inc(chain, 1)

            def scan(b, par, p):
                dve.wait_ge(bterm_ready, 2 * b + p + 1)
                dve.wait_ge(chain, 10 * b + 5 * p + 5)
                for k in range(2):
                    ins = dve.tensor_tensor_scan(h[p][:, k], alpha[p][:, k], bterm[p][:, k], 0.0, ALU.mult, ALU.add)
                ins.then_inc(scanned, 1)
                dve.wait_ge(scanned, 2 * b + p + 1)
                dve.wait_ge(in_read, 4 * b + 4)
                dve.tensor_tensor(gh[:, 2 * p:2 * p + 2], gate[par][:, 2 * p:2 * p + 2], h[p][:], ALU.mult).then_inc(gated, 1)

            def residual(b):
                dve.wait_ge(out_done, b + 1)
                for t in range(TPB):
                    dve.tensor_tensor(norm.res[:, t], o_bank[:, t], at(X, b * TPB + t), ALU.add).then_inc(summed, 1)
                    dve.wait_ge(summed, b * TPB + t + 1)
                    norm.statistics(dve, b, t)

            def layer_norm(b):
                for t in range(TPB):
                    norm.apply(dve, b, t, at(X, b * TPB + t))

            def batch(b, par, before=True, after=True, enters=True, fetches=True):
                if after:
                    convolve(b + 1, 1 - par, 0)
                if enters:
                    enter(b + 2, par)
                if before:
                    scan(b - 1, 1 - par, 0)
                    scan(b - 1, 1 - par, 1)
                if after:
                    convolve(b + 1, 1 - par, 1)
                if enters:
                    enter_norm(b + 2)
                if before:
                    residual(b - 1)
                decay(b, 0)
                if before:
                    layer_norm(b - 1)
                decay(b, 1)

            for b in (0, 1):
                enter(b, b)
                enter_norm(b)
            dve.wait_ge(cleared, 1)
            convolve(0, 0, 0)
            convolve(0, 0, 1)
            both(batch)(dve)
            scan(BATCH - 1, 1, 0)
            scan(BATCH - 1, 1, 1)
            residual(BATCH - 1)
            layer_norm(BATCH - 1)

        @block.tensor
        def _(pe):
            pe.wait_ge(gates.w_loaded, 48)

            def way_in(b, par):
                pe.wait_ge(staged[par], 8 * (b - par) + 16)
                if not first(b):
                    pe.wait_ge(x_ready, b)
                for g in range(KT_):
                    for t in range(TPB):
                        ins = pe.transpose(x_bank[:, g, t * P:(t + 1) * P], xs[par][:, t, g * P:(g + 1) * P], ident[:])
                ins.then_inc(x_turned, 1)
                pe.wait_ge(x_ready, b + 1)
                for s in range(4):
                    if not (first(b) and s < 2):
                        pe.wait_ge(in_read, 4 * b + s - 1)
                    for k in range(2):
                        m = (HT + 2 * s + k) % (2 * HT)
                        for g in range(KT_):
                            ins = pe.matmul(i_bank[s % 2][:, k], w_in[:, g, m * P:(m + 1) * P], xt[:, g],
                                            start=(g == 0), stop=(g == KT_ - 1))
                    ins.then_inc(in_done, 1)

            def tile(b, par, m):
                if m == 0:
                    pe.wait_ge(conved, (b + 1) * TAPS * HT)
                if not first(b):
                    pe.wait_ge(ti_done, b * HT + m - HT + 1)
                for k in range(2):
                    cols = slice(k * HID + m * P, k * HID + (m + 1) * P)
                    for j in range(HT):
                        ins = pe.matmul(g_bank[m][:, k], w_g[:, j, cols], conv[par][:, j], start=(j == 0), stop=(j == HT - 1))
                ins.then_inc(g_done, 1)

            def way_out(b):
                pe.wait_ge(gated, 2 * b + 2)
                for t in range(TPB):
                    for j in range(HT):
                        ins = pe.matmul(o_bank[:, t], gh[:, j, t * P:(t + 1) * P], w_out[:, j], start=(j == 0), stop=(j == HT - 1))
                ins.then_inc(out_done, 1)

            def batch(b, par, before=True, after=True, enters=True, fetches=True):
                if after:
                    way_in(b + 1, 1 - par)
                tile(b, par, 0)
                tile(b, par, 1)
                if before:
                    way_out(b - 1)
                tile(b, par, 2)
                tile(b, par, 3)

            way_in(0, 0)
            both(batch)(pe)
            way_out(BATCH - 1)




class BinaryWeights:

    def __init__(self, ctx, nc):
        def sb(name, shape):
            return ctx.enter_context(nc.sbuf_tensor("bf_" + name, shape, F32))

        self.w1 = sb("w1", [P, KT_, FF])
        self.w2 = sb("w2", [P, FT, DIM])
        self.b1 = sb("b1", [P, FT])
        self.b2 = sb("b2", [P, DIM])
        self.loaded = ctx.enter_context(nc.semaphore("bf_loaded"))

    def load(self, sp, w1_dram, w2_dram, b1_dram, b2_dram):
        for tile, dram in ((self.w1, w1_dram), (self.w2, w2_dram), (self.b1, b1_dram), (self.b2, b2_dram)):
            sp.dma_start(tile[:], dram).then_inc(self.loaded, 16)


def binary_ffn(nc, weights, ident, half, X, out):
    with ExitStack() as ctx:
        def sb(name, shape, dt=F32):
            return ctx.enter_context(nc.sbuf_tensor("bf_" + name, shape, dt))

        def sem(name):
            return ctx.enter_context(nc.semaphore("bf_" + name))

        w1, w2, b1, b2 = weights.w1, weights.w2, weights.b1, weights.b2
        size1, size2 = sb("size1", [P, KT_, FF]), sb("size2", [P, FT, DIM])
        below1, below2 = sb("below1", [P, KT_, FF], F16), sb("below2", [P, FT, DIM], F16)
        sign1, sign2 = sb("sign1", [P, KT_, FF], F16), sb("sign2", [P, FT, DIM], F16)
        alpha1 = sb("alpha1", [P, FT])
        alpha2 = sb("alpha2", [P, DIM])
        ones = sb("ones", [P, P])
        xs = [sb(f"xs{k}", [P, TPB, DIM]) for k in range(2)]
        xb = [sb(f"xb{k}", [P, TPB, DIM]) for k in range(2)]
        xh = [sb(f"xh{k}", [P, KT_, SEQ], F16) for k in range(2)]
        xl = [sb(f"xl{k}", [P, KT_, SEQ], F16) for k in range(2)]
        h = sb("h", [P, FT, SEQ])
        hh = [sb(f"hh{k}", [P, FT, SEQ], F16) for k in range(2)]
        hl = [sb(f"hl{k}", [P, FT, SEQ], F16) for k in range(2)]
        scaled = sb("scaled", [P, TPB, DIM])
        y = [sb(f"y{k}", [P, TPB, DIM]) for k in range(2)]

        x_bank = ctx.enter_context(nc.psum_tensor("bf_x", [P, KT_, SEQ], F32))
        u_bank = [ctx.enter_context(nc.psum_tensor(f"bf_up{k}", [P, 2, SEQ], F32)) for k in range(4)]
        o_bank = [ctx.enter_context(nc.psum_tensor(f"bf_out{k}", [P, 512], F32)) for k in range(TPB)]
        a_bank = ctx.enter_context(nc.psum_tensor("bf_alpha", [P, 512], F32))

        norm = Norm(ctx, nc, "bf", half)
        staged = [sem("staged0"), sem("staged1")]
        stored = [sem("stored0"), sem("stored1")]
        consts = sem("consts")
        sized = sem("sized")
        below = sem("below")
        signed = sem("signed")
        totals = sem("totals")
        alphas = sem("alphas")
        xb_ready = sem("xb_ready")
        x_turned = sem("x_turned")
        x_high = sem("x_high")
        x_low = sem("x_low")
        up = sem("up")
        h_ready = sem("h_ready")
        h_high = sem("h_high")
        h_low = sem("h_low")
        down = sem("down")
        times_alpha = sem("times_alpha")
        summed = sem("summed")

        def all_batches(batch):
            def run(engine):
                batch(0, 0)
                batch(1, 1)
                with engine.Fori(1, BATCH // 2 - 1) as i:
                    batch(2 * i, 0)
                    batch(2 * i + 1, 1)
                batch(BATCH - 2, 0, ahead=1)
                batch(BATCH - 1, 1, ahead=0)
            return run

        block = ctx.enter_context(nc.Block())

        @block.sync
        def _(sp):
            def stage(b, par):
                sp.dma_start(xs[par][:], X[:, bass.ds(b * TPB, TPB)]).then_inc(staged[par], 16)

            def restage(b, par):
                sp.wait_ge(x_turned, b + 1)
                sp.wait_ge(xb_ready, b + 1)
                stage(b + 2, par)

            def store(b, par):
                sp.wait_ge(norm.ln_done, (b + 1) * TPB)
                where = out[b] if isinstance(b, int) else out[bass.ds(b, 1)].squeeze(0)
                sp.dma_start(where.rearrange("(t p) d -> p t d", p=P), y[par][:]).then_inc(stored[par], 16)

            stage(0, 0)
            stage(1, 1)
            restage(0, 0)
            restage(1, 1)
            with sp.Fori(0, BATCH // 2 - 2) as i:
                for par in range(2):
                    restage(2 * i + par + 2, par)
                    store(2 * i + par, par)
            for b in range(BATCH - 4, BATCH):
                store(b, b % 2)
            for par in range(2):
                sp.wait_ge(stored[par], 16 * (BATCH // 2))

        @block.gpsimd
        def _(pool):
            pool.memset(ones[:], 1.0).then_inc(consts, 1)
            pool.wait_ge(weights.loaded, 64)

            def add_bias(b, par):
                pool.wait_ge(staged[par], 8 * (b - par) + 16)
                if not (isinstance(b, int) and b < 2):
                    pool.wait_ge(summed, (b - 1) * TPB)
                for t in range(TPB):
                    ins = pool.tensor_tensor(xb[par][:, t], xs[par][:, t], b2[:], ALU.add)
                ins.then_inc(xb_ready, 1)

            def batch(b, par, ahead=2):
                norm.root(pool, b, 0)
                norm.root(pool, b, 1)
                if ahead == 2:
                    add_bias(b + 2, par)

            add_bias(0, 0)
            add_bias(1, 1)
            all_batches(batch)(pool)

        @block.scalar
        def _(act):
            def tokens(b, par):
                act.wait_ge(x_turned, b + 1)
                if not (isinstance(b, int) and b < 2):
                    act.wait_ge(up, (b - 1) * 4)
                act.activation(xh[par][:], x_bank[:], ACT.Copy, scale=SCALE).then_inc(x_high, 1)

            def hidden(b, s):
                act.wait_ge(up, 4 * b + s + 1)
                if not first(b):
                    act.wait_ge(h_low, 4 * b + s - 3)
                for k in range(2):
                    m = 2 * s + k
                    ins = act.activation(h[:, m], u_bank[s][:, k], ACT.Gelu, scale=alpha1[:, m:m + 1], bias=b1[:, m:m + 1])
                ins.then_inc(h_ready, 1)

            def high(b, par, s):
                act.wait_ge(h_ready, 4 * b + s + 1)
                if not (isinstance(b, int) and b < 2):
                    act.wait_ge(down, (b - 1) * TPB)
                act.activation(hh[par][:, 2 * s:2 * s + 2], h[:, 2 * s:2 * s + 2], ACT.Copy, scale=HSCALE).then_inc(h_high, 1)

            def all_hidden(b, par):
                hidden(b, 0)
                for s in range(1, 4):
                    hidden(b, s)
                    high(b, par, s - 1)
                high(b, par, 3)

            def batch(b, par, ahead=2):
                if ahead == 2:
                    tokens(b + 2, par)
                if ahead:
                    all_hidden(b + 1, 1 - par)

            act.wait_ge(weights.loaded, 64)
            tokens(0, 0)
            tokens(1, 1)
            act.wait_ge(alphas, 2)
            all_hidden(0, 0)
            all_batches(batch)(act)

        @block.vector
        def _(dve):
            def tokens_low(b, par):
                dve.wait_ge(x_high, b + 1)
                dve.scalar_tensor_tensor(out=xl[par][:], in0=x_bank[:], scalar=SCALE, in1=xh[par][:],
                                         op0=ALU.mult, op1=ALU.subtract).then_inc(x_low, 1)

            def low(b, par, s):
                dve.wait_ge(h_high, 4 * b + s + 1)
                t = slice(2 * s, 2 * s + 2)
                dve.scalar_tensor_tensor(out=hl[par][:, t], in0=h[:, t], scalar=HSCALE, in1=hh[par][:, t],
                                         op0=ALU.mult, op1=ALU.subtract).then_inc(h_low, 1)

            def residual(b, par, t):
                dve.wait_ge(down, b * TPB + t + 1)
                if not first(b):
                    dve.wait_ge(summed, b * TPB + t - 1)
                dve.tensor_tensor(scaled[:, t], o_bank[t][:, 0:DIM], alpha2[:], ALU.mult).then_inc(times_alpha, 1)
                dve.wait_ge(times_alpha, b * TPB + t + 1)
                dve.wait_ge(xb_ready, b + 1)
                if not first(b):
                    dve.wait_ge(norm.ln_done, b * TPB)
                dve.tensor_tensor(norm.res[:, t], scaled[:, t], xb[par][:, t], ALU.add).then_inc(summed, 1)
                dve.wait_ge(summed, b * TPB + t + 1)
                norm.statistics(dve, b, t)

            def batch(b, par, ahead=2):
                if ahead == 2:
                    tokens_low(b + 2, par)
                if ahead:
                    low(b + 1, 1 - par, 0)
                    low(b + 1, 1 - par, 1)
                residual(b, par, 0)
                residual(b, par, 1)
                if ahead:
                    low(b + 1, 1 - par, 2)
                    low(b + 1, 1 - par, 3)
                if not (isinstance(b, int) and b < 2):
                    dve.wait_ge(stored[par], 8 * (b - par))
                for t in range(TPB):
                    norm.apply(dve, b, t, y[par][:, t])

            def split_weight(w, size, negative, sign, n):
                dve.scalar_tensor_tensor(out=size[:], in0=w[:], scalar=-1.0, in1=w[:], op0=ALU.mult, op1=ALU.max).then_inc(sized, 1)
                dve.tensor_scalar(negative[:], w[:], 0.0, None, ALU.is_lt).then_inc(below, 1)
                dve.wait_ge(below, n)
                dve.scalar_tensor_tensor(out=sign[:], in0=w[:], scalar=0.0, in1=negative[:],
                                         op0=ALU.is_gt, op1=ALU.subtract).then_inc(signed, 1)

            dve.wait_ge(weights.loaded, 64)
            split_weight(w1, size1, below1, sign1, 1)
            tokens_low(0, 0)
            tokens_low(1, 1)
            dve.wait_ge(totals, 1)
            dve.tensor_scalar(alpha1[:], a_bank[:, 0:FT], 1.0 / (DIM * SCALE), None, ALU.mult).then_inc(alphas, 1)
            split_weight(w2, size2, below2, sign2, 2)
            dve.wait_ge(totals, 2)
            dve.tensor_scalar(alpha2[:], a_bank[:, 0:DIM], 1.0 / (FF * HSCALE), None, ALU.mult).then_inc(alphas, 1)
            dve.wait_ge(alphas, 2)
            for s in range(4):
                low(0, 0, s)
            all_batches(batch)(dve)

        @block.tensor
        def _(pe):
            def turn(b, par):
                pe.wait_ge(staged[par], 8 * (b - par) + 16)
                if not first(b):
                    pe.wait_ge(x_low, b)
                for g in range(KT_):
                    for t in range(TPB):
                        ins = pe.transpose(x_bank[:, g, t * P:(t + 1) * P], xs[par][:, t, g * P:(g + 1) * P], ident[:])
                ins.then_inc(x_turned, 1)

            def way_up(b, par):
                pe.wait_ge(x_low, b + 1)
                for s in range(4):
                    if not first(b):
                        pe.wait_ge(h_ready, 4 * b + s - 3)
                    for k in range(2):
                        m = 2 * s + k
                        n = 0
                        for x in (xh[par], xl[par]):
                            for g in range(KT_):
                                ins = pe.matmul(u_bank[s][:, k], sign1[:, g, m * P:(m + 1) * P], x[:, g],
                                                start=(n == 0), stop=(n == 2 * KT_ - 1))
                                n += 1
                    ins.then_inc(up, 1)

            def way_down(b, par):
                pe.wait_ge(h_low, 4 * b + 4)
                if not first(b):
                    pe.wait_ge(times_alpha, b * TPB)
                for t in range(TPB):
                    n = 0
                    for x in (hh[par], hl[par]):
                        for m in range(FT):
                            ins = pe.matmul(o_bank[t][:, 0:DIM], x[:, m, t * P:(t + 1) * P], sign2[:, m],
                                            start=(n == 0), stop=(n == 2 * FT - 1))
                            n += 1
                    ins.then_inc(down, 1)

            def batch(b, par, ahead=2):
                if ahead == 2:
                    turn(b + 2, par)
                if ahead:
                    way_up(b + 1, 1 - par)
                way_down(b, par)

            turn(0, 0)
            turn(1, 1)
            pe.wait_ge(consts, 1)
            pe.wait_ge(sized, 1)
            for m in range(FT):
                for g in range(KT_):
                    ins = pe.matmul(a_bank[:, m:m + 1], size1[:, g, m * P:(m + 1) * P], ones[:, 0:1],
                                    start=(g == 0), stop=(g == KT_ - 1))
            ins.then_inc(totals, 1)
            pe.wait_ge(signed, 1)
            way_up(0, 0)
            pe.wait_ge(sized, 2)
            pe.wait_ge(alphas, 1)
            for m in range(FT):
                ins = pe.matmul(a_bank[:, 0:DIM], ones[:], size2[:, m], start=(m == 0), stop=(m == FT - 1))
            ins.then_inc(totals, 1)
            pe.wait_ge(signed, 2)
            all_batches(batch)(pe)


def build(nc, ins, out):
    with ExitStack() as ctx:
        X = ctx.enter_context(nc.sbuf_tensor("tokens", [P, TILES, DIM], F32))
        ident = ctx.enter_context(nc.sbuf_tensor("ident", [P, P], F32))
        half = ctx.enter_context(nc.sbuf_tensor("half", [P, 1], F32))
        def loads(what, *names):
            return lambda sp: what.load(sp, *(ins[name] for name in names))

        with ExitStack() as only:
            cross0 = CrossWeights(only, nc, "ca0", additive=False)
            window_attention(nc, ins["x"], ins["xt"], ins["wqkv"], ins["wo0"], ins["rope"], ident, half, X,
                             loads(cross0, "xw0", "xb0", "xr0", "mask0"))
            cross_attention(nc, cross0, ins["context"], ident, half, X)
        slots = nc.dram_tensor("slots", (SLOTS, DIM), F32, kind="Internal").ap()
        slot = ctx.enter_context(nc.sbuf_tensor("slot", [P, TILES], I32))
        gates = Gates(ctx, nc)
        experts(nc, ins["router"], ins["ew1"], ins["ew2"], ins["eb"], slots, slot, ident, X,
                loads(gates, "w_in", "w_g", "w_out", "hid"), gates)
        cross1 = CrossWeights(ctx, nc, "ca1", additive=True)
        recurrence(nc, gates, slots, slot, ident, half, X, loads(cross1, "xw1", "xb1", "xr1", "mask1"))
        binary = BinaryWeights(ctx, nc)
        cross_attention(nc, cross1, ins["context"], ident, half, X, loads(binary, "w1t", "w2t", "b1", "b2"))
        binary_ffn(nc, binary, ident, half, X, out)


def kernel(**inputs):
    import concourse.bacc as bacc
    from concourse.bass_utils import run_bass_kernel_spmd

    a = {k: np.asarray(v) for k, v in inputs.items()}

    def halves(w):
        return np.ascontiguousarray(w.reshape(-1, P, w.shape[-1]).transpose(1, 0, 2))

    def by_partition(v):
        return np.ascontiguousarray(v.reshape(-1, P).T)

    def on_all(v):
        return np.ascontiguousarray(np.broadcast_to(v, (P,) + v.shape))

    pos = np.arange(SEQ, dtype=np.float32)
    freq = np.float32(1.0) / np.float32(10000.0) ** (np.arange(0, HD, 2, dtype=np.float32) / np.float32(HD))
    angle = pos[:, None] * freq[None, :]
    cos, sin = np.cos(angle), np.sin(angle)
    rope = np.stack([np.concatenate([cos, cos], 1), np.concatenate([-sin, sin], 1)], 1).astype(np.float32)
    flat = a["x"].reshape(TOKENS, DIM)
    arrays = {
        "x": np.ascontiguousarray(flat.reshape(TILES, P, DIM).transpose(1, 0, 2)),
        "xt": halves(flat.T),
        "wqkv": halves(np.concatenate([a["L0_attn_Wq"], a["L0_attn_Wk"], a["L0_attn_Wv"]], 1)),
        "wo0": halves(a["L0_attn_Wo"]),
        "rope": np.ascontiguousarray(rope.reshape(TPB, P, 2, HD).transpose(1, 0, 2, 3)),
        "context": halves(a["ctx_1024"].reshape(BATCH * CTX, DIM).T),
        "mask0": np.ascontiguousarray(a["mask_BxSxS2_ik0"].reshape(TILES, P, CTX).transpose(1, 0, 2)),
        "mask1": np.ascontiguousarray(a["mask_Bx1xSxS2_ff0"].reshape(TILES, P, CTX).transpose(1, 0, 2)),
    }
    for n, names in (("0", ["L0_xattn_Wq", "L0_xattn_Wk", "L0_xattn_Wv", "L0_xattn_Wo"]),
                     ("1", ["L1_xattn_w_q", "L1_xattn_w_k", "L1_xattn_w_v", "L1_xattn_w_o"])):
        bq, bk, bv, bo = (a[x.replace("W", "b").replace("w_", "b_")] for x in names)
        arrays["xw" + n] = np.ascontiguousarray(np.stack([halves(a[x].T) for x in names], 1))
        arrays["xb" + n] = np.ascontiguousarray(np.stack([by_partition(bq), by_partition(bk)], 1))
        arrays["xr" + n] = np.ascontiguousarray(np.stack([on_all(bv), on_all(bo)], 1))
    router = a["L0_ffn_router_w"]
    others_first = [*range(1, EXPERTS), 0]
    arrays["router"] = halves(router.T)
    arrays["ew1"] = np.stack([halves(a["L0_ffn_W1"][e]) for e in others_first])
    arrays["ew2"] = np.stack([halves(a["L0_ffn_W2"][e]) for e in others_first])
    arrays["eb"] = np.stack([np.concatenate([by_partition(a["L0_ffn_b1"][e]), by_partition(a["L0_ffn_b2"][e])], 1)
                             for e in others_first], 1)
    for name in ("W_in", "W_g", "W_out"):
        arrays[name.lower()] = halves(a["L1_attn_" + name].T)
    arrays["hid"] = np.stack([*(by_partition(a["L1_attn_conv_w"][:, 0, t]) for t in range(4)), by_partition(a["L1_attn_conv_b"]),
                              *by_partition(a["L1_attn_b_g"]).reshape(P, 2, -1).transpose(1, 0, 2),
                              by_partition(a["L1_attn_forget_base"])], 1)
    arrays["w1t"] = halves(a["L1_ffn_w1"].T)
    arrays["w2t"] = halves(a["L1_ffn_w2"].T)
    arrays["b1"] = by_partition(a["L1_ffn_b1"])
    arrays["b2"] = on_all(a["L1_ffn_b2"])
    nc = bacc.Bacc("TRN2", target_bir_lowering=False, num_devices=1)
    ins = {k: nc.dram_tensor("in_" + k, v.shape, mybir.dt.from_np(v.dtype), kind="ExternalInput").ap()
           for k, v in arrays.items()}
    out = nc.dram_tensor("out", (BATCH, SEQ, DIM), F32, kind="ExternalOutput").ap()
    build(nc, ins, out)
    r = run_bass_kernel_spmd(nc, [{"in_" + k: v for k, v in arrays.items()}], core_ids=[0])
    return r.results[0]["out"]
```
